# Optimizing a Trainium2 kernel written in Bass

```python
import numpy as np
import jax
import jax.numpy as jnp

def _softmax(x, axis=-1):
    return jax.nn.softmax(x, axis=axis)

def _gelu(x):
    return jax.nn.gelu(x, approximate=True)

def _silu(x):
    return jax.nn.silu(x)

def _sigmoid(x):
    return jax.nn.sigmoid(x)

def _layernorm(x, axis=-1, eps=1e-05):
    m = jnp.mean(x, axis=axis, keepdims=True)
    v = jnp.var(x, axis=axis, keepdims=True)
    return (x - m) / jnp.sqrt(v + eps)

def _scatter_add(tgt, idx, src, axis=0):
    return tgt.at[idx].add(src)

def _segment_sum(src, seg, n):
    return jax.ops.segment_sum(src, seg, n)
kernel_name = 'mk_adaln_ffn_d2_seqx_r8_1b144c'

def setup_inputs(seed: int=0):
    np.random.seed(seed)
    _w = jnp.asarray

    def _rec_inputs():
        import jax
        import jax.numpy as jnp
        _rk = jax.random.key(seed)
        x = -0.0002928 + 1 * jax.random.normal(jax.random.fold_in(_rk, 1), (16, 128, 128), jnp.float32)
        _lenS = 128 - jax.random.randint(jax.random.fold_in(_rk, 7), (16,), 0, max(1, 128 // 4) + 1, jnp.int32)
        _lenS2 = 128 - jax.random.randint(jax.random.fold_in(_rk, 8), (16,), 0, max(1, 128 // 4) + 1, jnp.int32)
        cond_64 = -0.0184271 + 1.00439 * jax.random.normal(jax.random.fold_in(_rk, 12), (16, 64), jnp.float32)
        fside_16xSxS_0 = -5.72187e-05 + 0.999849 * jax.random.normal(jax.random.fold_in(_rk, 13), (16, 128, 128), jnp.float32)
        _validS = jnp.arange(128)[None, :] < _lenS[:, None]
        _validS2 = jnp.arange(128)[None, :] < _lenS2[:, None]
        _causal = jnp.tril(jnp.ones((128, 128), dtype=bool))
        mask_BxS_bf1 = jnp.ones((16, 128), dtype=bool)
        mask_BxS_bk0 = jnp.logical_not(jnp.broadcast_to(_validS[:, :], (16, 128)))
        return (x, cond_64, fside_16xSxS_0, mask_BxS_bf1, mask_BxS_bk0)
    x, cond_64, fside_16xSxS_0, mask_BxS_bf1, mask_BxS_bk0 = _rec_inputs()

    def _L0_cond_setup():
        import jax, jax.numpy as jnp
        import numpy as np
        DIM = 128
        HEADS = 16
        DIM_HEAD = 64
        SCALE = 8.0

        def ln(x, g, eps=1e-05):
            mean = x.mean(axis=-1, keepdims=True)
            var = ((x - mean) ** 2).mean(axis=-1, keepdims=True)
            return (x - mean) * jax.lax.rsqrt(var + eps) * g

        def l2norm(t):
            n = jnp.maximum(jnp.linalg.norm(t, axis=-1, keepdims=True), 1e-12)
            return t / n

        def rel_pos_bias(n, w0, b0, g0, w1, b1, g1, w2, b2, dtype):
            pos = jnp.arange(-n + 1, n, dtype=dtype)[:, None]
            h = jax.nn.silu(ln(pos @ w0 + b0, g0))
            h = jax.nn.silu(ln(h @ w1 + b1, g1))
            h = h @ w2 + b2
            i = jnp.arange(n)
            idx = i[:, None] - i[None, :] + n - 1
            bias = h[idx]
            return jnp.transpose(bias, (2, 0, 1))
        key = jax.random.key(seed)
        ks = jax.random.split(key, 16)
        b, n = (2, 256)
        inner = HEADS * DIM_HEAD
        s = 0.02
        return {'x': jax.random.normal(ks[0], (b, n, DIM), jnp.float32), 'mask': jnp.ones((b, n), dtype=bool), 'g_norm': jnp.ones((DIM,), jnp.float32), 'Wq': jax.random.normal(ks[1], (DIM, inner), jnp.float32) * s, 'Wkv': jax.random.normal(ks[2], (DIM, 2 * DIM_HEAD), jnp.float32) * s, 'q_scale': jnp.ones((DIM_HEAD,), jnp.float32), 'k_scale': jnp.ones((DIM_HEAD,), jnp.float32), 'null_kv': jax.random.normal(ks[3], (2, DIM_HEAD), jnp.float32), 'null_attn_bias': jax.random.normal(ks[4], (HEADS,), jnp.float32), 'w0': jax.random.normal(ks[5], (1, DIM), jnp.float32) * s, 'b0': jnp.zeros((DIM,), jnp.float32), 'g0': jnp.ones((DIM,), jnp.float32), 'w1': jax.random.normal(ks[6], (DIM, DIM), jnp.float32) * s, 'b1': jnp.zeros((DIM,), jnp.float32), 'g1': jnp.ones((DIM,), jnp.float32), 'w2': jax.random.normal(ks[7], (DIM, HEADS), jnp.float32) * s, 'b2': jnp.zeros((HEADS,), jnp.float32), 'Wout': jax.random.normal(ks[8], (inner, DIM), jnp.float32) * s, 'g_out': jnp.ones((DIM,), jnp.float32)}
    _L0_cond_all = _L0_cond_setup()
    _L0_cond_in = {k: v for k, v in _L0_cond_all.items() if k in ('g_norm', 'Wq', 'Wkv', 'q_scale', 'k_scale', 'null_attn_bias', 'w0', 'b0', 'g0', 'w1', 'b1', 'g1', 'w2', 'b2', 'Wout', 'g_out')}
    del _L0_cond_all

    def _L0_ffn_setup():
        import jax, jax.numpy as jnp
        import numpy as np
        LN_EPS = 1e-05

        def layer_norm(x, g, b):
            mu = jnp.mean(x, axis=-1, keepdims=True)
            var = jnp.mean(jnp.square(x - mu), axis=-1, keepdims=True)
            return (x - mu) * jax.lax.rsqrt(var + LN_EPS) * g + b

        def ternary_quant(w):
            scale = 1.0 / jnp.clip(jnp.mean(jnp.abs(w)), 1e-05)
            wq = jnp.clip(jnp.round(w * scale), -1.0, 1.0) / scale
            return w + jax.lax.stop_gradient(wq - w)
        key = jax.random.key(seed)
        ks = jax.random.split(key, 3)
        dim, hidden = (128, 512)
        B, S = (8, 128)
        x = jax.random.normal(ks[0], (B, S, dim), dtype=jnp.float32)
        w1 = jax.random.normal(ks[1], (hidden, dim), dtype=jnp.float32) * 0.02
        w2 = jax.random.normal(ks[2], (dim, hidden), dtype=jnp.float32) * 0.02
        return {'x': x, 'ln1_g': jnp.ones((dim,), jnp.float32), 'ln1_b': jnp.zeros((dim,), jnp.float32), 'w1': w1, 'b1': jnp.zeros((hidden,), jnp.float32), 'ln2_g': jnp.ones((hidden,), jnp.float32), 'ln2_b': jnp.zeros((hidden,), jnp.float32), 'w2': w2, 'b2': jnp.zeros((dim,), jnp.float32)}
    _L0_ffn_all = _L0_ffn_setup()
    _L0_ffn_in = {k: v for k, v in _L0_ffn_all.items() if k in ('ln1_g', 'ln1_b', 'w1', 'b1', 'ln2_g', 'ln2_b', 'w2', 'b2')}
    del _L0_ffn_all

    def _L1_cond_setup():
        import jax, jax.numpy as jnp
        import numpy as np
        B, N, DIM, H, DH = (2, 256, 128, 16, 64)
        INNER = H * DH
        EPS = 1e-05

        def layernorm(x, g):
            mean = jnp.mean(x, axis=-1, keepdims=True)
            var = jnp.var(x, axis=-1, keepdims=True)
            return (x - mean) * jax.lax.rsqrt(var + EPS) * g
        key = jax.random.key(seed)
        ks = jax.random.split(key, 10)
        x = jax.random.normal(ks[0], (B, N, DIM), dtype=jnp.float32)
        attn_bias = jax.random.normal(ks[1], (H, N, N), dtype=jnp.float32)
        mask = jax.random.randint(ks[2], (B, N), 0, 2).astype(bool)
        g_in = jnp.ones((DIM,), dtype=jnp.float32)
        null_attn_bias = jax.random.normal(ks[3], (H,), dtype=jnp.float32)
        null_kv = jax.random.normal(ks[4], (2, DH), dtype=jnp.float32)
        Wq = jax.random.normal(ks[5], (DIM, INNER), dtype=jnp.float32) * 0.02
        Wkv = jax.random.normal(ks[6], (DIM, 2 * DH), dtype=jnp.float32) * 0.02
        Wo = jax.random.normal(ks[7], (INNER, DIM), dtype=jnp.float32) * 0.02
        g_out = jnp.ones((DIM,), dtype=jnp.float32)
        return {'x': x, 'attn_bias': attn_bias, 'mask': mask, 'g_in': g_in, 'null_attn_bias': null_attn_bias, 'null_kv': null_kv, 'Wq': Wq, 'Wkv': Wkv, 'Wo': Wo, 'g_out': g_out}
    _L1_cond_all = _L1_cond_setup()
    _L1_cond_in = {k: v for k, v in _L1_cond_all.items() if k in ('g_in', 'null_attn_bias', 'Wq', 'Wkv', 'Wo', 'g_out')}
    del _L1_cond_all

    def _L1_ffn_setup():
        import math
        import jax, jax.numpy as jnp
        import numpy as np
        B, L, D, FF, E, K = (4, 256, 128, 512, 8, 2)
        CAPACITY_FACTOR = 1.25
        T = B * L
        CAP = math.ceil(CAPACITY_FACTOR * T * K / E)
        key = jax.random.key(seed)
        ks = jax.random.split(key, 7)
        return {'h': jax.random.normal(ks[0], (B, L, D), dtype=jnp.float32), 'gate_w': 0.02 * jax.random.normal(ks[1], (E, D), dtype=jnp.float32), 'gate_b': jnp.zeros((E,), dtype=jnp.float32), 'W1': 0.02 * jax.random.normal(ks[2], (E, D, FF), dtype=jnp.float32), 'b1': jnp.zeros((E, FF), dtype=jnp.float32), 'W2': 0.02 * jax.random.normal(ks[3], (E, FF, D), dtype=jnp.float32), 'b2': jnp.zeros((E, D), dtype=jnp.float32)}
    _L1_ffn_all = _L1_ffn_setup()
    _L1_ffn_in = {k: v for k, v in _L1_ffn_all.items() if k in ('gate_w', 'gate_b', 'W1', 'b1', 'W2', 'b2')}
    del _L1_ffn_all
    return {'x': x, 'cond_64': cond_64, 'fside_16xSxS_0': fside_16xSxS_0, 'mask_BxS_bf1': mask_BxS_bf1, 'mask_BxS_bk0': mask_BxS_bk0, 'L0_cond_g_norm': _L0_cond_in['g_norm'], 'L0_cond_Wq': _L0_cond_in['Wq'], 'L0_cond_Wkv': _L0_cond_in['Wkv'], 'L0_cond_q_scale': _L0_cond_in['q_scale'], 'L0_cond_k_scale': _L0_cond_in['k_scale'], 'L0_cond_null_attn_bias': _L0_cond_in['null_attn_bias'], 'L0_cond_w0': _L0_cond_in['w0'], 'L0_cond_b0': _L0_cond_in['b0'], 'L0_cond_g0': _L0_cond_in['g0'], 'L0_cond_w1': _L0_cond_in['w1'], 'L0_cond_b1': _L0_cond_in['b1'], 'L0_cond_g1': _L0_cond_in['g1'], 'L0_cond_w2': _L0_cond_in['w2'], 'L0_cond_b2': _L0_cond_in['b2'], 'L0_cond_Wout': _L0_cond_in['Wout'], 'L0_cond_g_out': _L0_cond_in['g_out'], 'L0_ffn_ln1_g': _L0_ffn_in['ln1_g'], 'L0_ffn_ln1_b': _L0_ffn_in['ln1_b'], 'L0_ffn_w1': _L0_ffn_in['w1'], 'L0_ffn_b1': _L0_ffn_in['b1'], 'L0_ffn_ln2_g': _L0_ffn_in['ln2_g'], 'L0_ffn_ln2_b': _L0_ffn_in['ln2_b'], 'L0_ffn_w2': _L0_ffn_in['w2'], 'L0_ffn_b2': _L0_ffn_in['b2'], 'L1_cond_g_in': _L1_cond_in['g_in'], 'L1_cond_null_attn_bias': _L1_cond_in['null_attn_bias'], 'L1_cond_Wq': _L1_cond_in['Wq'], 'L1_cond_Wkv': _L1_cond_in['Wkv'], 'L1_cond_Wo': _L1_cond_in['Wo'], 'L1_cond_g_out': _L1_cond_in['g_out'], 'L1_ffn_gate_w': _L1_ffn_in['gate_w'], 'L1_ffn_gate_b': _L1_ffn_in['gate_b'], 'L1_ffn_W1': _L1_ffn_in['W1'], 'L1_ffn_b1': _L1_ffn_in['b1'], 'L1_ffn_W2': _L1_ffn_in['W2'], 'L1_ffn_b2': _L1_ffn_in['b2']}

def reference(x, cond_64, fside_16xSxS_0, mask_BxS_bf1, mask_BxS_bk0, L0_cond_g_norm, L0_cond_Wq, L0_cond_Wkv, L0_cond_q_scale, L0_cond_k_scale, L0_cond_null_attn_bias, L0_cond_w0, L0_cond_b0, L0_cond_g0, L0_cond_w1, L0_cond_b1, L0_cond_g1, L0_cond_w2, L0_cond_b2, L0_cond_Wout, L0_cond_g_out, L0_ffn_ln1_g, L0_ffn_ln1_b, L0_ffn_w1, L0_ffn_b1, L0_ffn_ln2_g, L0_ffn_ln2_b, L0_ffn_w2, L0_ffn_b2, L1_cond_g_in, L1_cond_null_attn_bias, L1_cond_Wq, L1_cond_Wkv, L1_cond_Wo, L1_cond_g_out, L1_ffn_gate_w, L1_ffn_gate_b, L1_ffn_W1, L1_ffn_b1, L1_ffn_W2, L1_ffn_b2):
    import jax
    import jax.numpy as jnp

    def _L0_cond_ref(x, mask, g_norm, Wq, Wkv, q_scale, k_scale, null_kv, null_attn_bias, w0, b0, g0, w1, b1, g1, w2, b2, Wout, g_out):
        import jax, jax.numpy as jnp
        import numpy as np
        DIM = 128
        HEADS = 16
        DIM_HEAD = 64
        SCALE = 8.0

        def ln(x, g, eps=1e-05):
            mean = x.mean(axis=-1, keepdims=True)
            var = ((x - mean) ** 2).mean(axis=-1, keepdims=True)
            return (x - mean) * jax.lax.rsqrt(var + eps) * g

        def l2norm(t):
            n = jnp.maximum(jnp.linalg.norm(t, axis=-1, keepdims=True), 1e-12)
            return t / n

        def rel_pos_bias(n, w0, b0, g0, w1, b1, g1, w2, b2, dtype):
            pos = jnp.arange(-n + 1, n, dtype=dtype)[:, None]
            h = jax.nn.silu(ln(pos @ w0 + b0, g0))
            h = jax.nn.silu(ln(h @ w1 + b1, g1))
            h = h @ w2 + b2
            i = jnp.arange(n)
            idx = i[:, None] - i[None, :] + n - 1
            bias = h[idx]
            return jnp.transpose(bias, (2, 0, 1))
        b, n, _ = x.shape
        xn = ln(x, g_norm)
        q = (xn @ Wq).reshape(b, n, HEADS, DIM_HEAD).transpose(0, 2, 1, 3)
        kv = xn @ Wkv
        k, v = (kv[..., :DIM_HEAD], kv[..., DIM_HEAD:])
        nk = jnp.broadcast_to(null_kv[0], (b, 1, DIM_HEAD))
        nv = jnp.broadcast_to(null_kv[1], (b, 1, DIM_HEAD))
        k = jnp.concatenate([nk, k], axis=1)
        v = jnp.concatenate([nv, v], axis=1)
        q = l2norm(q) * q_scale
        k = l2norm(k) * k_scale
        sim = jnp.einsum('bhid,bjd->bhij', q, k) * SCALE
        bias = rel_pos_bias(n, w0, b0, g0, w1, b1, g1, w2, b2, q.dtype)
        null_bias = jnp.broadcast_to(null_attn_bias[:, None, None], (HEADS, n, 1))
        attn_bias = jnp.concatenate([null_bias, bias], axis=-1)
        sim = sim + attn_bias
        neg = -jnp.finfo(sim.dtype).max
        causal = jnp.triu(jnp.ones((n, n + 1), dtype=bool), k=2)
        sim = jnp.where(causal, neg, sim)
        m = jnp.pad(mask, ((0, 0), (1, 0)), constant_values=True)[:, None, None, :]
        sim = jnp.where(m, sim, neg)
        attn = jax.nn.softmax(sim, axis=-1)
        out = jnp.einsum('bhij,bjd->bhid', attn, v)
        out = out.transpose(0, 2, 1, 3).reshape(b, n, HEADS * DIM_HEAD)
        return ln(out @ Wout, g_out)

    def _L0_ffn_ref(x, ln1_g, ln1_b, w1, b1, ln2_g, ln2_b, w2, b2):
        import jax, jax.numpy as jnp
        import numpy as np
        LN_EPS = 1e-05

        def layer_norm(x, g, b):
            mu = jnp.mean(x, axis=-1, keepdims=True)
            var = jnp.mean(jnp.square(x - mu), axis=-1, keepdims=True)
            return (x - mu) * jax.lax.rsqrt(var + LN_EPS) * g + b

        def ternary_quant(w):
            scale = 1.0 / jnp.clip(jnp.mean(jnp.abs(w)), 1e-05)
            wq = jnp.clip(jnp.round(w * scale), -1.0, 1.0) / scale
            return w + jax.lax.stop_gradient(wq - w)
        h = layer_norm(x, ln1_g, ln1_b)
        h = jnp.einsum('bsd,hd->bsh', h, ternary_quant(w1)) + b1
        h = jax.nn.gelu(h, approximate=False)
        h = layer_norm(h, ln2_g, ln2_b)
        out = jnp.einsum('bsh,dh->bsd', h, ternary_quant(w2)) + b2
        return out

    def _L1_cond_ref(x, attn_bias, mask, g_in, null_attn_bias, null_kv, Wq, Wkv, Wo, g_out):
        import jax, jax.numpy as jnp
        import numpy as np
        B, N, DIM, H, DH = (2, 256, 128, 16, 64)
        INNER = H * DH
        EPS = 1e-05

        def layernorm(x, g):
            mean = jnp.mean(x, axis=-1, keepdims=True)
            var = jnp.var(x, axis=-1, keepdims=True)
            return (x - mean) * jax.lax.rsqrt(var + EPS) * g
        b, n, _ = x.shape
        scale = DH ** (-0.5)
        xn = layernorm(x, g_in)
        q = (xn @ Wq).reshape(b, n, H, DH).transpose(0, 2, 1, 3) * scale
        kv = xn @ Wkv
        k, v = (kv[..., :DH], kv[..., DH:])
        nk = jnp.broadcast_to(null_kv[0], (b, 1, DH))
        nv = jnp.broadcast_to(null_kv[1], (b, 1, DH))
        k = jnp.concatenate([nk, k], axis=1)
        v = jnp.concatenate([nv, v], axis=1)
        sim = jnp.einsum('bhid,bjd->bhij', q, k)
        null_col = jnp.broadcast_to(null_attn_bias[:, None, None], (H, n, 1))
        bias = jnp.concatenate([null_col, attn_bias], axis=-1)
        sim = sim + bias
        neg = -jnp.finfo(sim.dtype).max
        j = n + 1
        causal_mask = jnp.triu(jnp.ones((n, j), dtype=bool), k=j - n + 1)
        sim = jnp.where(causal_mask, neg, sim)
        mask_p = jnp.pad(mask, ((0, 0), (1, 0)), constant_values=True)
        sim = jnp.where(mask_p[:, None, None, :], sim, neg)
        attn = jax.nn.softmax(sim, axis=-1)
        out = jnp.einsum('bhij,bjd->bhid', attn, v)
        out = out.transpose(0, 2, 1, 3).reshape(b, n, INNER)
        out = out @ Wo
        return layernorm(out, g_out)

    def _L1_ffn_ref(h, gate_w, gate_b, W1, b1, W2, b2):
        import math
        import jax, jax.numpy as jnp
        import numpy as np
        B, L, D, FF, E, K = (4, 256, 128, 512, 8, 2)
        CAPACITY_FACTOR = 1.25
        T = B * L
        CAP = math.ceil(CAPACITY_FACTOR * T * K / E)
        Bb, Ll, Dm = h.shape
        Tt = Bb * Ll
        x = h.reshape(Tt, Dm)
        logits = x @ gate_w.T + gate_b
        probs = jax.nn.softmax(logits, axis=-1)
        topk_prob, topk_idx = jax.lax.top_k(probs, K)
        y = jnp.zeros((Tt, Dm), dtype=h.dtype)
        n_slots = E * CAP
        for c in range(K):
            idx = topk_idx[:, c]
            prb = topk_prob[:, c]
            oh = jax.nn.one_hot(idx, E, dtype=jnp.int32)
            pos = jnp.take_along_axis(jnp.cumsum(oh, axis=0) - 1, idx[:, None], axis=1)[:, 0]
            keep = pos < CAP
            buf_idx = jnp.where(keep, idx * CAP + pos, n_slots)
            xbuf = jnp.zeros((n_slots, Dm), x.dtype).at[buf_idx].set(x, mode='drop')
            xb = xbuf.reshape(E, CAP, Dm)
            hmid = jax.nn.relu(jnp.einsum('ecd,edf->ecf', xb, W1) + b1[:, None, :])
            yb = jnp.einsum('ecf,efd->ecd', hmid, W2) + b2[:, None, :]
            ytok = yb.reshape(n_slots, Dm)[jnp.clip(buf_idx, 0, n_slots - 1)]
            y = y + ytok * (prb * keep.astype(prb.dtype))[:, None]
        return y.reshape(Bb, Ll, Dm)
    x = x + _L0_ffn_ref(_L0_cond_ref(x, mask_BxS_bf1, L0_cond_g_norm, L0_cond_Wq, L0_cond_Wkv, L0_cond_q_scale, L0_cond_k_scale, cond_64, L0_cond_null_attn_bias, L0_cond_w0, L0_cond_b0, L0_cond_g0, L0_cond_w1, L0_cond_b1, L0_cond_g1, L0_cond_w2, L0_cond_b2, L0_cond_Wout, L0_cond_g_out), L0_ffn_ln1_g, L0_ffn_ln1_b, L0_ffn_w1, L0_ffn_b1, L0_ffn_ln2_g, L0_ffn_ln2_b, L0_ffn_w2, L0_ffn_b2)
    x = x + _L1_ffn_ref(_L1_cond_ref(x, fside_16xSxS_0, mask_BxS_bk0, L1_cond_g_in, L1_cond_null_attn_bias, cond_64, L1_cond_Wq, L1_cond_Wkv, L1_cond_Wo, L1_cond_g_out), L1_ffn_gate_w, L1_ffn_gate_b, L1_ffn_W1, L1_ffn_b1, L1_ffn_W2, L1_ffn_b2)
    return x

_drawn_inputs = setup_inputs


def setup_inputs(seed=0):
    import zlib

    import numpy as np

    out = dict(_drawn_inputs(seed))
    spreads = {'L0_cond_g_norm': (1.0, 0.2),
     'L0_cond_q_scale': (1.0, 0.2),
     'L0_cond_k_scale': (1.0, 0.2),
     'L0_cond_b0': (0.0, 0.8),
     'L0_cond_g0': (1.0, 0.6),
     'L0_cond_b1': (0.0, 0.8),
     'L0_cond_g1': (1.0, 0.6),
     'L0_cond_b2': (0.0, 0.8),
     'L0_cond_g_out': (1.0, 0.2),
     'L0_ffn_ln1_g': (1.0, 0.2),
     'L0_ffn_ln1_b': (0.0, 0.316),
     'L0_ffn_b1': (0.0, 0.1),
     'L0_ffn_ln2_g': (1.0, 0.2),
     'L0_ffn_ln2_b': (0.0, 0.291),
     'L0_ffn_b2': (0.0, 0.1),
     'L1_cond_g_in': (1.0, 0.6),
     'L1_cond_g_out': (1.0, 0.6),
     'L1_ffn_gate_b': (0.0, 0.8),
     'L1_ffn_b1': (0.0, 0.8),
     'L1_ffn_b2': (0.0, 0.776)}
    factors = {'fside_16xSxS_0': 8.0,
     'L0_cond_w0': 6.062,
     'L0_cond_w1': 3.593,
     'L0_cond_w2': 3.846,
     'L1_cond_null_attn_bias': 8.0,
     'L1_cond_Wq': 8.0,
     'L1_cond_Wkv': 8.0,
     'L1_cond_Wo': 5.6,
     'L1_ffn_gate_w': 4.239,
     'L1_ffn_W1': 8.0,
     'L1_ffn_W2': 7.033}
    for name, (base, spread) in spreads.items():
        noise = np.random.default_rng([zlib.crc32(name.encode()), seed]).standard_normal(out[name].shape)
        drawn = base * np.exp(spread * noise) if base else spread * noise
        out[name] = jnp.asarray(drawn.astype(out[name].dtype))
    for name, factor in factors.items():
        out[name] = (out[name] * factor).astype(out[name].dtype)
    return out
```

```python
from contextlib import ExitStack

import concourse.bass as bass
from concourse import mybir

F32 = mybir.dt.float32
BF16 = mybir.dt.bfloat16
U32 = mybir.dt.uint32
I32 = mybir.dt.int32
U8 = mybir.dt.uint8
ALU = mybir.AluOpType
ACT = mybir.ActivationFunctionType
X_AXIS = mybir.AxisListType.X

P = 128
NB = 16
HEADS = 16
DH = 64
HIDDEN = 512
FB = HIDDEN // P
EXPERTS = 8
CAP = 320
TOPK = 2
SLOTS = EXPERTS * TOPK * CAP
TILES = TOPK * CAP // P
ROW = 132
QB = 32
UNITS = P // QB
KEYS = P + 2
WIDTH = [QB * (u + 1) + 1 for u in range(UNITS)]
BIAS_AT = [4 * sum(WIDTH[:u]) for u in range(UNITS + 1)]
CONSTS = 19
ROWS_DMAS = 15
BCAST_DMAS = 29
SCRATCH_ALL = 1 + 16 * (SLOTS // (TILES * P) + TOPK * NB // 4)
FAR = -1e30
MASKED = -1e20
LN_EPS = 1e-5


def build(nc, a, out):
    ctx = ExitStack()
    with ctx:
        def sb(name, shape, dt=F32):
            return ctx.enter_context(nc.sbuf_tensor(name, shape, dt))

        def pb(name, shape, dt=F32):
            return ctx.enter_context(nc.psum_tensor(name, shape, dt))

        def sem(name):
            return ctx.enter_context(nc.semaphore(name))

        def dram(name, shape, dt=F32):
            return nc.dram_tensor(name, shape, dt).ap()

        def at(ap, offset, dims):
            return bass.AP(ap.tensor, offset, dims)

        rel_d = dram("rel_scratch", (HEADS, QB, 2 * P))
        slot_d = dram("slot_rows", (SLOTS + P, ROW))
        back_d = dram("choice_rows", (TOPK * NB * P + P, P))

        X = sb("X", [P, NB, P])
        Y = sb("Y", [P, NB, P])
        ident = sb("ident", [P, P])
        ones = sb("ones", [P, P])
        ones_bf = sb("ones_bf", [P, P], BF16)
        before_bf = sb("before_bf", [P, P], BF16)
        rows = sb("rows", [P, P])
        cols = sb("cols", [P, P])
        Wq = [sb("Wq0", [P, HEADS * DH]), sb("Wq1", [P, HEADS * DH])]
        Wkv = [sb("Wkv0", [P, P]), sb("Wkv1", [P, P])]
        Wo = [sb("Wo0", [P, 8, P]), sb("Wo1", [P, 8, P])]
        bias = [sb("bias0", [P, BIAS_AT[-1]]), sb("bias1", [P, BIAS_AT[-1]])]
        nullb = [sb("nullb0", [P, 4]), sb("nullb1", [P, 4])]
        mask_u8 = [sb("mask0_u8", [P, NB * P], U8), sb("mask1_u8", [P, NB * P], U8)]
        mask = [sb("mask0", [P, NB, KEYS], BF16), sb("mask1", [P, NB, KEYS], BF16)]
        g_out = [sb("g_out0", [P, P]), sb("g_out1", [P, P])]
        kqs = sb("kqs", [P, DH])
        qs_row = sb("qs_row", [P, DH])
        nk_row = sb("nk_row", [P, DH])
        vnull = sb("vnull", [P, DH])
        nk0 = sb("nk0", [P, 1])
        w1_raw = sb("w1_raw", [P, FB, P])
        w2_raw = sb("w2_raw", [P, FB, P])
        w1T = sb("w1T", [P, HIDDEN])
        w2T = sb("w2T", [P, FB, P])
        tern = sb("tern", [P, 2, HIDDEN])
        wabs = sb("wabs", [P, 2])
        wmean = sb("wmean", [P, 2])
        wscale = sb("wscale", [P, 2])
        fb1 = sb("fb1", [P, HIDDEN])
        fb2 = sb("fb2", [P, P])
        rel_rows = sb("rel_rows", [P, 5, P])
        rel_w1 = sb("rel_w1", [P, P])
        rel_w2 = sb("rel_w2", [P, HEADS])
        rel_b2 = sb("rel_b2", [HEADS, 1])
        rel_h = sb("rel_h", [P, P])
        rel_n = sb("rel_n", [P, P])
        rel_s = sb("rel_s", [P, P])
        rel_T = sb("rel_T", [P, P])
        rel_tab = sb("rel_tab", [HEADS, 2 * P])
        pos_i = sb("pos_i", [P, 1], I32)
        pos_f = sb("pos_f", [P, 1])
        half = sb("half", [P, 20])
        small = sb("small", [P, 16])
        gate_rows = sb("gate_rows", [EXPERTS, P])
        gateT = sb("gateT", [P, EXPERTS])
        gate_b = sb("gate_b", [P, EXPERTS])
        mb2 = sb("mb2", [P, EXPERTS, P])

        stats = sb("stats", [P, NB, 6])
        mv = sb("mv", [P, NB, 2])
        ve = sb("ve", [P, NB])
        rstd = sb("rstd", [P, NB])

        xn = sb("xn", [P, 2, P])
        xnT = [sb("xnT0", [P, P]), sb("xnT1", [P, P])]
        qsq = sb("qsq", [P, HEADS + 1, DH])
        qss = sb("qss", [P, HEADS + 1])
        qssc = sb("qssc", [P, HEADS + 1])
        qrn = sb("qrn", [P, HEADS + 1])
        qn = sb("qn", [P, HEADS * DH])
        qT = [sb("qT0", [P, 2, UNITS, 4, QB]), sb("qT1", [P, 2, UNITS, 4, QB])]
        kd = [sb("kd0", [P, 2, DH]), sb("kd1", [P, 2, DH])]
        vp = [sb("vp0", [P, DH]), sb("vp1", [P, DH])]
        kk = [sb("kk0", [P, 2, KEYS]), sb("kk1", [P, 2, KEYS])]
        sc = [sb(f"sc{u}", [P, 2, 2, WIDTH[u]]) for u in range(UNITS)]
        negmax = sb("negmax", [P, UNITS, 4])
        psum_row = sb("psum_row", [P, UNITS, 4])
        rsum = sb("rsum", [P, UNITS, 4])
        pn = [sb(f"pn{i}", [P, 4, P]) for i in range(2)]
        PT = [sb(f"PT{i}", [P, 2, 2, P]) for i in range(2)]
        OT = [sb(f"OT{i}", [P, 8, UNITS, QB]) for i in range(2)]

        z = sb("z", [P, 2, HIDDEN])
        hT = [sb("hT0", [P, P]), sb("hT1", [P, P])]
        gn = sb("gn", [P, 2, HIDDEN])
        gnT = [sb("gnT0", [P, FB, P]), sb("gnT1", [P, FB, P])]
        zst = sb("zst", [P, 2, 6])
        zmv = sb("zmv", [P, 2, 2])
        zve = sb("zve", [P, 2])
        zrstd = sb("zrstd", [P, 2])
        ffo = sb("ffo", [P, P])

        lg = sb("lg", [P, NB, EXPERTS])
        lgm = sb("lgm", [P, NB])
        le = sb("le", [P, NB, EXPERTS])
        lsum = sb("lsum", [P, NB])
        prob = sb("prob", [P, NB, EXPERTS])
        top = sb("top", [P, NB, 8])
        topi = sb("topi", [P, NB, 8], U32)
        topf = sb("topf", [P, NB, TOPK])
        io_i = sb("io_i", [P, EXPERTS], I32)
        io_f = sb("io_f", [P, EXPERTS])
        oh = sb("oh", [P, NB, TOPK, EXPERTS])
        oh_bf = sb("oh_bf", [P, NB, TOPK, EXPERTS], BF16)
        cnt = sb("cnt", [P, NB, TOPK, EXPERTS])
        base = sb("base", [P, NB, TOPK, EXPERTS])
        posn = sb("posn", [P, NB, TOPK, EXPERTS])
        own = sb("own", [P, NB, TOPK])
        keep = sb("keep", [P, NB, TOPK])
        dest = sb("dest", [P, NB, TOPK])
        dest_u = sb("dest_u", [P, NB, TOPK], U32)
        cbase_i = sb("cbase_i", [P, NB, TOPK], I32)
        cbase = sb("cbase", [P, NB, TOPK])
        trash_i = sb("trash_i", [P, 1], I32)
        trash = sb("trash", [P, 1])
        tok_i = sb("tok_i", [P, NB, TOPK], I32)
        pay = sb("pay", [P, NB, TOPK, ROW])
        empty = sb("empty", [P, ROW])
        zero_row = sb("zero_row", [P, 4, P])
        ept = sb("ept_id", [P, 1], I32)

        eW1 = [sb("eW10", [P, HIDDEN]), sb("eW11", [P, HIDDEN])]
        eW2 = [sb("eW20", [P, FB, P]), sb("eW21", [P, FB, P])]
        xb = [sb("xb0", [P, TILES, ROW]), sb("xb1", [P, TILES, ROW])]
        xbT = sb("xbT", [P, TILES * P])
        hm = sb("hm", [P, FB, TILES * P])
        yb = [sb("yb0", [P, TILES, P]), sb("yb1", [P, TILES, P])]
        flat_pay = pay[:].rearrange("p t c r -> p (t c r)")
        back = pay[:].rearrange("p t c r -> p (t c r)")[:, 0:TOPK * NB * P].rearrange(
            "p (c t d) -> p c t d", c=TOPK, t=NB)
        masked_bias = [flat_pay[:, i * BIAS_AT[-1]:(i + 1) * BIAS_AT[-1]] for i in range(2)]

        psS = pb("psS", [P, 2, 512])
        psT = pb("psT", [P, 2, 512])
        psQ = pb("psQ", [P, 2, 512])
        psO = pb("psO", [P, 512])
        psA = pb("psA", [P, 512])

        C_GN0, C_GIN1, C_LN1G, C_LN1B, C_LN2G, C_LN2B, C_MB1 = 0, 1, 2, 3, 4, 8, 12
        C_VN, C_NK, C_QS, C_KS = 44, 45, 46, 47
        N_ROWS = 48

        rows_in = sem("rows_in")
        x_in = sem("x_in")
        bcast_in = sem("bcast_in")
        ffnw_in = sem("ffnw_in")
        attw_in = sem("attw_in")
        table_in = sem("table_in")
        rel_out = sem("rel_out")
        rel_in = sem("rel_in")
        scratch_out = sem("scratch_out")
        const_done = sem("const_done")
        pool_step = sem("pool_step")
        dve_step = sem("dve_step")

        names = ["xn_ready", "xnT_psum", "xnT_ready", "kv_psum", "q_psum", "kv_ready", "kT_psum",
                 "kk_ready", "q_ready", "sq_ready", "ss_step", "rn_ready", "qn_ready", "qT_psum",
                 "scores_psum", "scores_ready", "negmax_ready", "exp_done", "rsum_ready",
                 "probs_ready", "probsT_psum", "probsT_ready", "out_psum", "out_ready", "y_psum",
                 "y_done", "kk_null", "bias_ready"]
        s = {n: sem(n) for n in names}
        for n in ["cols_psum", "wabs_ready", "rel_s_ready", "rel_n_ready", "rel_psum", "rel_T_ready",
                  "tern_ready", "ternT_psum", "setup_read", "ffnw_ready", "normed", "cols_ready", "r_x",
                  "mul_ready"]:
            s[n] = sem(n)
        for n in ["f_h", "f_h_psum", "f_hT", "f_z_psum", "f_z_ready", "f_gelu", "f_stat", "f_var", "f_rstd",
                  "f_gn", "f_gnT_psum", "f_gnT", "f_o_psum", "f_o_step"]:
            s[n] = sem(n)
        for n in ["ln_step", "ln_var", "ln_rstd", "r_T_psum", "r_T", "r_lg_psum", "r_step", "r_exp",
                  "r_oh", "r_pos_read", "r_pos_psum", "r_pay", "r_pool", "slots_out", "e_w0", "e_w1", "e_x0", "e_x1",
                  "e_T_psum", "e_T", "e_h_psum", "e_h_act", "e_h_dve", "e_y_psum", "e_y_add", "e_y",
                  "e_out", "back_in", "z_step", "final_out", "back_ready", "e_sent"]:
            s[n] = sem(n)

        def unit_bias(layer, u):
            return bias[layer][:, BIAS_AT[u]:BIAS_AT[u + 1]].rearrange(
                "p (h e k) -> p h e k", h=2, e=2)

        def unit_masked(i, u):
            return masked_bias[i][:, BIAS_AT[u]:BIAS_AT[u + 1]].rearrange("p (h e k) -> p h e k", h=2, e=2)

        def unit_psum(u):
            return psS[:, :, 0:2 * WIDTH[u]].rearrange("p h (e k) -> p h e k", e=2)

        block = ctx.enter_context(nc.Block())

        def over(eng, count, body):
            body(0, 0)
            body(1, 1)
            with eng.Fori(1, count // 2 - 1) as k:
                body(2 * k, 0)
                body(2 * k + 1, 1)
            body(count - 2, 0)
            body(count - 1, 1)

        def held(eng, semaphore, value):
            if not (isinstance(value, int) and value <= 0):
                eng.wait_ge(semaphore, value)

        def apart(eng, *waits):
            values = [v if isinstance(v, int) else eng.to_reg(v) for _, v in waits]
            eng.wait_ge(const_done, CONSTS)
            for (semaphore, _), v in zip(waits, values):
                if not isinstance(v, int) or v > 0:
                    eng.wait_ge(semaphore, v)

        def arrived(e, i, count):
            return count * (e // 2 + 1) if isinstance(e, int) else (e - i) * (count // 2) + count

        def no(t, value):
            return isinstance(t, int) and t == value

        @block.sync
        def _(sp):
            n_rows = 0

            def row(name, r0, n=1, k=P, at_col=0):
                nonlocal n_rows
                src = a[name]
                src = at(src, src.offset, [[k, n], [1, k]])
                sp.dma_start(rows[r0:r0 + n, at_col:at_col + k], src).then_inc(rows_in, 16)
                n_rows += 1

            row("L0_cond_g_norm", C_GN0)
            row("L1_cond_g_in", C_GIN1)
            row("L0_ffn_ln1_g", C_LN1G)
            row("L0_ffn_ln1_b", C_LN1B)
            row("L0_ffn_ln2_g", C_LN2G, 4)
            row("L0_ffn_ln2_b", C_LN2B, 4)
            row("L1_ffn_b1", C_MB1, 32)
            for d in range(2):
                c = a["cond_64"]
                sp.dma_start(rows[C_VN:C_VN + 1, d * DH:(d + 1) * DH], c[1:2, :]).then_inc(rows_in, 16)
                sp.dma_start(rows[C_NK:C_NK + 1, d * DH:(d + 1) * DH], c[0:1, :]).then_inc(rows_in, 16)
                row("L0_cond_q_scale", C_QS, 1, DH, d * DH)
                row("L0_cond_k_scale", C_KS, 1, DH, d * DH)
            assert n_rows + 4 == ROWS_DMAS

            sp.dma_start(X[:], a["x"].rearrange("b n d -> n b d")).then_inc(x_in, 16)

            def spread(dst, name, k, offset=0):
                src = a[name]
                sp.dma_start(dst, at(src, src.offset + offset, [[0, P], [1, k]])).then_inc(bcast_in, 16)

            for i, name in enumerate(("L0_cond_w0", "L0_cond_b0", "L0_cond_g0", "L0_cond_b1",
                                      "L0_cond_g1")):
                spread(rel_rows[:, i, :], name, P)
            spread(kqs[:], "L0_cond_k_scale", DH)
            spread(qs_row[:], "L0_cond_q_scale", DH)
            spread(nk_row[:], "cond_64", DH)
            spread(vnull[:], "cond_64", DH, DH)
            spread(fb1[:], "L0_ffn_b1", HIDDEN)
            spread(fb2[:], "L0_ffn_b2", P)
            spread(g_out[0][:], "L0_cond_g_out", P)
            spread(g_out[1][:], "L1_cond_g_out", P)
            spread(gate_b[:], "L1_ffn_gate_b", EXPERTS)
            spread(mb2[:].rearrange("p e d -> p (e d)"), "L1_ffn_b2", EXPERTS * P)
            sp.dma_start(rel_w1[:], a["L0_cond_w1"]).then_inc(bcast_in, 16)
            sp.dma_start(rel_w2[:], a["L0_cond_w2"]).then_inc(bcast_in, 16)
            sp.dma_start(rel_b2[:], at(a["L0_cond_b2"], 0, [[1, HEADS], [1, 1]])).then_inc(bcast_in, 16)
            sp.dma_start(gate_rows[:], a["L1_ffn_gate_w"]).then_inc(bcast_in, 16)
            for layer, name in enumerate(("mask_BxS_bf1", "mask_BxS_bk0")):
                sp.dma_start(mask_u8[layer][:].bitcast(U32),
                             at(a[name], 0, [[0, P], [1, NB * P // 4]])).then_inc(bcast_in, 16)
            for layer in range(2):
                src = a[f"L{layer}_cond_null_attn_bias"]
                for m in range(4):
                    sp.dma_start(nullb[layer][QB * m:QB * (m + 1), :].rearrange("p (h e) -> p h e", e=2),
                                 at(src, 2 * m, [[0, QB], [8, 2], [1, 2]])).then_inc(bcast_in, 16)
            assert BCAST_DMAS == 5 + 10 + 4 + 2 + 8

            sp.dma_start(w1_raw[:], a["L0_ffn_w1"].rearrange("(j p) d -> p j d", p=P)).then_inc(ffnw_in, 16)
            sp.dma_start(w2_raw[:], a["L0_ffn_w2"].rearrange("p (j h) -> p j h", j=FB)).then_inc(ffnw_in, 16)
            for layer in range(2):
                wo = a["L0_cond_Wout" if layer == 0 else "L1_cond_Wo"]
                sp.dma_start(Wq[layer][:], a[f"L{layer}_cond_Wq"]).then_inc(attw_in, 16)
                sp.dma_start(Wkv[layer][:], a[f"L{layer}_cond_Wkv"]).then_inc(attw_in, 16)
                sp.dma_start(Wo[layer][:], wo.rearrange("(j p) d -> p j d", p=P)).then_inc(attw_in, 16)
            fs = a["fside_16xSxS_0"]
            for u in range(UNITS):
                for m in range(4):
                    for hh in range(2):
                        sp.dma_start(unit_bias(1, u)[QB * m:QB * (m + 1), hh, :, 1:WIDTH[u]],
                                     at(fs, ((8 * hh + 2 * m) * P + QB * u) * P,
                                        [[P, QB], [P * P, 2], [1, WIDTH[u] - 1]])).then_inc(table_in, 16)

            sp.wait_ge(rel_out, 1)
            sp.dma_start(rel_d, rel_tab[:].unsqueeze(1).broadcast_to([HEADS, QB, 2 * P])).then_inc(rel_out, 16)
            sp.wait_ge(rel_out, 17)
            for u in range(UNITS):
                for m in range(4):
                    for hh in range(2):
                        sp.dma_start(unit_bias(0, u)[QB * m:QB * (m + 1), hh, :, 1:WIDTH[u]],
                                     at(rel_d, (8 * hh + 2 * m) * QB * 2 * P + P - 1 - QB * u,
                                        [[2 * P - 1, QB], [QB * 2 * P, 2], [1, WIDTH[u] - 1]])).then_inc(
                                            rel_in, 16)

            sp.wait_ge(scratch_out, 1)
            for r in range(0, SLOTS, TILES * P):
                sp.dma_start(at(slot_d, r * ROW, [[ROW, P], [P * ROW, TILES], [1, ROW]]),
                             empty[:].unsqueeze(1).broadcast_to([P, TILES, ROW])).then_inc(scratch_out, 16)
            for r in range(0, TOPK * NB, 4):
                sp.dma_start(at(back_d, r * P * P, [[P, P], [P * P, 4], [1, P]]),
                             zero_row[:]).then_inc(scratch_out, 16)

            def load_expert(e, i):
                sp.dma_start(eW1[i][:], a["L1_ffn_W1"][e]).then_inc(s[f"e_w{i}"], 16)
                sp.dma_start(eW2[i][:], a["L1_ffn_W2"][e].rearrange("(j p) d -> p j d", p=P)).then_inc(
                    s[f"e_w{i}"], 16)

            def load_slots(e, i):
                src = slot_d[bass.ts(e, TILES * P), :].rearrange("(t p) r -> p t r", p=P)
                sp.dma_start(xb[i][:], src).then_inc(s[f"e_x{i}"], 16)

            load_expert(0, 0)
            load_expert(1, 1)
            sp.wait_ge(s["slots_out"], 16 * NB * TOPK)
            load_slots(0, 0)
            load_slots(1, 1)
            with sp.Fori(0, EXPERTS // 2 - 1) as k:
                for i in range(2):
                    e = 2 * k + i
                    sp.wait_ge(s["e_y_psum"], e + 1)
                    load_expert(e + 2, i)
                    sp.wait_ge(s["e_sent"], 16 * TILES * (e + 1))
                    load_slots(e + 2, i)
            sp.wait_ge(s["e_sent"], 16 * TILES * EXPERTS)
            for q in range(4):
                for c in range(TOPK):
                    src = at(back_d, (c * NB + 4 * q) * P * P, [[P, P], [P * P, 4], [1, P]])
                    sp.dma_start(back[:, c, 4 * q:4 * q + 4, :], src).then_inc(s["back_in"], 16)
                sp.wait_ge(s["back_in"], 32 * (q + 1))
                sp.sem_inc(s["back_ready"], 1)
            out_v = out.rearrange("b n d -> n b d")
            for q in range(4):
                sp.wait_ge(s["z_step"], 2 * (q + 1))
                sp.dma_start(out_v[:, 4 * q:4 * q + 4, :], X[:, 4 * q:4 * q + 4, :]).then_inc(
                    s["final_out"], 16)
            sp.wait_ge(s["final_out"], 64)

        @block.gpsimd
        def _(pool):
            pool.memset(ident[:], 0.0).then_inc(const_done, 1)
            pool.memset(ones[:], 1.0).then_inc(const_done, 1)
            pool.memset(ones_bf[:], 1.0).then_inc(const_done, 1)
            pool.memset(half[:], -0.5).then_inc(const_done, 1)
            pool.memset(rel_tab[:], FAR).then_inc(const_done, 1)
            pool.memset(kk[0][:], 0.0).then_inc(const_done, 1)
            pool.memset(kk[1][:], 0.0).then_inc(const_done, 1)
            pool.memset(mask[0][:], 0.0).then_inc(const_done, 1)
            pool.memset(mask[1][:], 0.0).then_inc(const_done, 1)
            pool.memset(empty[:], 0.0).then_inc(const_done, 1)
            pool.memset(zero_row[:], 0.0).then_inc(const_done, 1)
            pool.wait_ge(const_done, 11)
            pool.affine_select(ident[:], ident[:], pattern=[[-1, P]], compare_op=ALU.not_equal, fill=1.0,
                               base=0, channel_multiplier=1).then_inc(const_done, 1)
            pool.affine_select(before_bf[:], ones_bf[:], pattern=[[1, P]], compare_op=ALU.is_gt, fill=0.0,
                               base=0, channel_multiplier=-1).then_inc(const_done, 1)
            pool.iota(pos_i[:], pattern=[[0, 1]], base=P - 1, channel_multiplier=-1).then_inc(const_done, 1)
            pool.iota(io_i[:], pattern=[[1, EXPERTS]], base=0, channel_multiplier=0).then_inc(const_done, 1)
            pool.iota(cbase_i[:], pattern=[[0, NB], [CAP, TOPK]], base=0, channel_multiplier=0).then_inc(const_done, 1)
            pool.iota(trash_i[:], pattern=[[0, 1]], base=SLOTS, channel_multiplier=1).then_inc(const_done, 1)
            pool.iota(tok_i[:], pattern=[[P, NB], [NB * P, TOPK]], base=0, channel_multiplier=1).then_inc(const_done, 1)
            pool.iota(ept[:], pattern=[[0, 1]], base=TOPK * NB * P, channel_multiplier=1).then_inc(const_done, 1)
            pool.wait_ge(const_done, CONSTS)
            pool.tensor_copy(empty[:, P:P + 1].bitcast(I32), ept[:]).then_inc(scratch_out, 1)

            def rsqrt(dst, src, k, done, count=1):
                pool.tensor_tensor(dst, src, half[:, 0:k], ALU.pow).then_inc(done, count)

            for n, (dst, src) in enumerate(((small[:, 1:2], small[:, 0:1]), (small[:, 3:4], small[:, 2:3]),
                                            (small[:, 5:6], small[:, 4:5]))):
                pool.wait_ge(s["ln_var"], n + 1)
                rsqrt(dst, src, 1, s["ln_rstd"])
            pool.wait_ge(table_in, 16 * 32)
            pool.wait_ge(s["ln_rstd"], 3)
            for u in range(UNITS):
                for m in range(4):
                    if 4 * u + m:
                        pool.wait_ge(pool_step, 4 * u + m)
                    v = unit_bias(1, u)[QB * m:QB * (m + 1)].rearrange("p h e k -> p (h e) k")[:, :, 1:WIDTH[u]]
                    pool.affine_select(v, v, pattern=[[0, 4], [-1, WIDTH[u] - 1]], compare_op=ALU.is_ge,
                                       fill=FAR, base=QB * u, channel_multiplier=1).then_inc(pool_step, 1)

            lns = 3

            pool.wait_ge(pool_step, 16)

            def bulk_rstd(n):
                pool.wait_ge(s["ln_var"], n + 1)
                rsqrt(rstd[:], ve[:], NB, s["ln_rstd"])

            def divide(n, u):
                pool.wait_ge(s["rsum_ready"], n + 1)
                held(pool, s["probsT_psum"], n - 1)
                k = WIDTH[u] - 1
                pool.tensor_tensor(pn[u % 2][:, :, 0:k],
                                   sc[u][:].rearrange("p h e k -> p (h e) k")[:, :, 1:k + 1],
                                   rsum[:, u, :].unsqueeze(2).broadcast_to([P, 4, k]),
                                   ALU.mult).then_inc(s["probs_ready"], 1)

            def q_norm(b):
                pool.wait_ge(s["ss_step"], 2 * b + 2)
                rsqrt(qrn[:], qssc[:], HEADS + 1, s["rn_ready"])

            def mask_bias(layer, b, u, i):
                n = 4 * (b + NB * layer) + u
                apart(pool, (s["scores_ready"], n - 7))
                k = WIDTH[u]
                pool.tensor_tensor(unit_masked(i, u).rearrange("p h e k -> p (h e) k"),
                                   unit_bias(layer, u).rearrange("p h e k -> p (h e) k"),
                                   mask[layer][:, bass.ds(b, 1), 0:k].broadcast_to([P, 4, k]),
                                   ALU.add).then_inc(s["bias_ready"], 1)

            def attention(layer):
                def batch(b, i):
                    n = 4 * (b + NB * layer)
                    for u in range(UNITS):
                        if not (no(b, 0) and u == 0):
                            divide(n + u - 1, (u - 1) % UNITS)
                        if not no(b, NB - 1):
                            mask_bias(layer, b + 1, u, 1 - i)
                        if layer == 0 and u == 1 and not no(b, NB - 1):
                            q_norm(b + 1)

                if layer == 0:
                    pool.wait_ge(rel_in, 16 * 32)
                    pool.wait_ge(s["setup_read"], 1)
                for u in range(UNITS):
                    mask_bias(layer, 0, u, 0)
                if layer == 0:
                    q_norm(0)
                over(pool, NB, batch)
                divide(4 * (NB + NB * layer) - 1, 3)

            bulk_rstd(lns)
            attention(0)
            bulk_rstd(lns + 1)
            bulk_rstd(lns + 2)

            def f_norm(t, i):
                pool.wait_ge(s["f_var"], t + 1)
                rsqrt(zrstd[:, i:i + 1], zve[:, i:i + 1], 1, s["f_rstd"])

            over(pool, NB, f_norm)
            bulk_rstd(lns + 3)
            attention(1)
            bulk_rstd(lns + 4)

            pool.wait_ge(s["normed"], 2)
            for c in range(TOPK):
                pool.tensor_copy(pay[:, :, c, 0:P], Y[:]).then_inc(s["r_pool"], 1)
            pool.tensor_copy(pay[:, :, :, P:P + 1].bitcast(I32), tok_i[:].unsqueeze(3)).then_inc(s["r_pool"], 1)
            pool.memset(pay[:, :, :, P + 2:ROW], 0.0).then_inc(s["r_pool"], 1)
            pool.wait_ge(s["r_pool"], 4)
            pool.wait_ge(s["r_pay"], 2)
            pool.wait_ge(scratch_out, SCRATCH_ALL)
            for t in range(NB):
                for c in range(TOPK):
                    if TOPK * t + c:
                        pool.wait_ge(s["slots_out"], 16 * (TOPK * t + c))
                    pool.indirect_dma_start(slot_d, bass.IndirectOffsetOnAxis(dest_u[:, t, c:c + 1], 0),
                                            pay[:, t, c, :], None).then_inc(s["slots_out"], 16)

            def send(e, i):
                for t in range(TILES):
                    apart(pool, (s["e_y"], TILES * e + t + 1), (s["e_sent"], 16 * (TILES * e + t)))
                    pool.indirect_dma_start(back_d, bass.IndirectOffsetOnAxis(
                        xb[i][:, t, P:P + 1].bitcast(U32), 0), yb[i][:, t, :], None).then_inc(s["e_sent"], 16)

            over(pool, EXPERTS, send)

        @block.tensor
        def _(pe):
            pe.wait_ge(const_done, CONSTS)
            pe.wait_ge(rows_in, 16 * ROWS_DMAS)
            pe.transpose(psA[:, 0:N_ROWS], rows[0:N_ROWS, :], ident[0:N_ROWS, 0:N_ROWS]).then_inc(s["cols_psum"], 1)
            pe.wait_ge(bcast_in, 16 * BCAST_DMAS)
            pe.transpose(psA[:, 64:64 + EXPERTS], gate_rows[:], ident[0:EXPERTS, 0:EXPERTS]).then_inc(s["cols_psum"], 1)
            pe.wait_ge(s["wabs_ready"], 2)
            pe.matmul(psO[:, 0:2], ones[:], wabs[:], start=True, stop=True).then_inc(s["cols_psum"], 1)
            pe.wait_ge(s["rel_s_ready"], 1)
            pe.transpose(psQ[:, 0, 0:P], rel_s[:], ident[:]).then_inc(s["rel_psum"], 1)
            pe.wait_ge(s["rel_T_ready"], 1)
            pe.matmul(psQ[:, 0, P:2 * P], rel_T[:], rel_w1[:], start=True, stop=True).then_inc(s["rel_psum"], 1)
            pe.wait_ge(s["rel_s_ready"], 2)
            pe.transpose(psQ[:, 0, 2 * P:3 * P], rel_s[:], ident[:]).then_inc(s["rel_psum"], 1)
            pe.wait_ge(s["rel_T_ready"], 2)
            pe.matmul(psQ[0:HEADS, 0, 3 * P:4 * P], rel_w2[:], rel_T[:], start=True, stop=True).then_inc(
                s["rel_psum"], 1)
            pe.wait_ge(s["tern_ready"], 2)
            for i in range(2):
                for j in range(FB):
                    m = pe.transpose(psT[:, i, j * P:(j + 1) * P], tern[:, i, j * P:(j + 1) * P], ident[:])
            m.then_inc(s["ternT_psum"], 1)
            pe.wait_ge(s["setup_read"], 1)
            pe.wait_ge(s["ffnw_ready"], 2)

            def turn_input(layer, b, i):
                B = b + NB * layer
                pe.wait_ge(s["xn_ready"], B + 1)
                held(pe, s["y_done"], B - 2)
                held(pe, s["kk_ready"], B)
                held(pe, s["kv_ready"], 2 * B)
                pe.transpose(psA[:, 0:P], xn[:, i, :], ident[:]).then_inc(s["xnT_psum"], 1)

            def project_in(layer, b, i):
                B = b + NB * layer
                pe.wait_ge(s["xnT_ready"], B + 1)
                held(pe, s["q_ready"], B)
                pe.matmul(psA[:, P:2 * P], xnT[i][:], Wkv[layer][:], start=True, stop=True).then_inc(s["kv_psum"], 1)
                if layer == 0:
                    for h in range(2):
                        m = pe.matmul(psQ[:, h, :], xnT[i][:], Wq[0][:, 512 * h:512 * (h + 1)],
                                      start=True, stop=True)
                else:
                    for j in range(8):
                        m = pe.matmul(psQ[:, j // 4, (j % 4) * P:(j % 4 + 1) * P], Wq[1][:, j * P:(j + 1) * P],
                                      xnT[i][:], start=True, stop=True)
                m.then_inc(s["q_psum"], 1)

            def turn_keys(layer, b, i):
                B = b + NB * layer
                pe.wait_ge(s["kv_ready"], 2 * B + 1)
                pe.transpose(psA[:, 2 * P:3 * P], kd[i][:].rearrange("p a d -> p (a d)"), ident[:]).then_inc(
                    s["kT_psum"], 1)

            def turn_queries(b):
                pe.wait_ge(s["qn_ready"], b + 1)
                for j in range(8):
                    m = pe.transpose(psQ[:, j // 4, (j % 4) * P:(j % 4 + 1) * P], qn[:, j * P:(j + 1) * P], ident[:])
                m.then_inc(s["qT_psum"], 1)

            def scores(layer, b, u, i):
                B = b + NB * layer
                n = 4 * B + u
                w = WIDTH[u]
                if no(b, 0) and u == 0:
                    pe.wait_ge(s["kk_null"], 4 * (layer + 1))
                apart(pe, *([(s["kk_ready"], B + 1), (s["q_ready"], B + 1)] if u == 0 else []),
                      (s["scores_ready"], n))
                for h in range(2):
                    m = pe.matmul(psS[:, h, 0:2 * w], qT[i][:, h, u].rearrange("p m q -> p (m q)"),
                                  kk[i][:, :, 0:w], start=True, stop=True)
                m.then_inc(s["scores_psum"], 1)

            def turn_probs(n, u):
                apart(pe, (s["probs_ready"], n + 1), (s["probsT_ready"], n - 1))
                k = WIDTH[u] - 1
                for g in range(4):
                    m = pe.transpose(psT[0:k, u % 2, g * P:(g + 1) * P], pn[u % 2][:, g, 0:k], ident[:])
                m.then_inc(s["probsT_psum"], 1)

            def values(n, u, i):
                apart(pe, (s["probsT_ready"], n + 1), (s["out_ready"], n))
                k = WIDTH[u] - 1
                for e in range(2):
                    m = pe.matmul(psO[DH * e:DH * (e + 1), 0:256], vp[i][0:k, :], PT[u % 2][0:k, :, e, :],
                                  start=True, stop=True)
                m.then_inc(s["out_psum"], 1)

            def project(layer, b, i, ahead):
                B = b + NB * layer
                pe.wait_ge(s["out_ready"], 4 * B + 4)
                pe.wait_ge(s["kv_ready"], 2 * (B + ahead + 1))
                held(pe, s["y_done"], B)
                for j in range(8):
                    m = pe.matmul(psA[:, 3 * P:4 * P], OT[i][:, j].rearrange("p u q -> p (u q)"), Wo[layer][:, j, :],
                                  start=(j == 0), stop=(j == 7))
                m.then_inc(s["y_psum"], 1)

            def attention(layer):
                def batch(b, i):
                    n = 4 * (b + NB * layer)
                    first, last = no(b, 0), no(b, NB - 1)

                    def earlier(u, lag):
                        return not (first and u < lag)

                    for u in range(UNITS):
                        if u == 0 and not first and not no(b, 1):
                            project(layer, b - 2, i, 2)
                        scores(layer, b, u, i)
                        if earlier(u, 2):
                            turn_probs(n + u - 2, (u - 2) % UNITS)
                        if u == 0 and not last:
                            turn_input(layer, b + 1, 1 - i)
                        if layer == 0 and u == 3 and not last:
                            turn_queries(b + 1)
                            turn_keys(layer, b + 1, 1 - i)
                        if earlier(u, 3):
                            values(n + u - 3, (u - 3) % UNITS, i if u == 3 else 1 - i)
                        if u == 0 and not last:
                            project_in(layer, b + 1, 1 - i)
                        if layer == 1 and u == 2 and not last:
                            turn_keys(layer, b + 1, 1 - i)

                if layer == 0:
                    pe.wait_ge(attw_in, 16 * 6)
                turn_input(layer, 0, 0)
                project_in(layer, 0, 0)
                if layer == 0:
                    turn_queries(0)
                turn_keys(layer, 0, 0)
                over(pe, NB, batch)
                N = 4 * (NB + NB * layer)
                project(layer, NB - 2, 0, 1)
                turn_probs(N - 2, 2)
                values(N - 3, 1, 1)
                turn_probs(N - 1, 3)
                values(N - 2, 2, 1)
                values(N - 1, 3, 1)
                project(layer, NB - 1, 1, 0)

            attention(0)

            def f_up(t, i):
                pe.wait_ge(s["f_h"], t + 1)
                held(pe, s["f_hT"], t)
                pe.transpose(psA[:, 0:P], xn[:, i, :], ident[:]).then_inc(s["f_h_psum"], 1)
                pe.wait_ge(s["f_hT"], t + 1)
                held(pe, s["f_z_ready"], t - 1)
                pe.matmul(psQ[:, i, :], hT[i][:], w1T[:], start=True, stop=True).then_inc(s["f_z_psum"], 1)

            def f_down(t, i):
                pe.wait_ge(s["f_gn"], t + 1)
                held(pe, s["f_gnT"], t - 1)
                for j in range(FB):
                    m = pe.transpose(psT[:, i, j * P:(j + 1) * P], gn[:, i, j * P:(j + 1) * P], ident[:])
                m.then_inc(s["f_gnT_psum"], 1)
                pe.wait_ge(s["f_gnT"], t + 1)
                held(pe, s["f_o_step"], 2 * t - 1)
                for j in range(FB):
                    m = pe.matmul(psO[:, 0:P], gnT[i][:, j, :], w2T[:, j, :], start=(j == 0),
                                  stop=(j == FB - 1))
                m.then_inc(s["f_o_psum"], 1)

            def ffn(t, i):
                if not no(t, NB - 1):
                    f_up(t + 1, 1 - i)
                f_down(t, i)

            f_up(0, 0)
            over(pe, NB, ffn)

            attention(1)

            def gate(t, i):
                pe.wait_ge(s["r_x"], t + 1)
                held(pe, s["r_T"], t)
                pe.transpose(psA[:, 0:P], xn[:, i, :], ident[:]).then_inc(s["r_T_psum"], 1)
                pe.wait_ge(s["r_T"], t + 1)
                pe.matmul(psQ[:, 0, bass.ts(t, EXPERTS)], hT[i][:], gateT[:], start=True, stop=True).then_inc(
                    s["r_lg_psum"], 1)

            over(pe, NB, gate)
            pe.wait_ge(s["r_oh"], 1)
            flat = oh_bf[:].rearrange("p t c e -> p (t c e)")
            pe.matmul(psQ[:, 1, 0:256], before_bf[:], flat, start=True, stop=True)
            pe.matmul(psQ[:, 1, 256:512], ones_bf[:], flat, start=True, stop=True).then_inc(s["r_pos_psum"], 1)
            pe.wait_ge(s["r_pos_read"], 1)

            def expert(e, i):
                pe.wait_ge(s[f"e_x{i}"], arrived(e, i, 16))
                held(pe, s["e_T"], 2 * e)
                for t in range(TILES):
                    m = pe.transpose(psT[:, t // 4, (t % 4) * P:(t % 4 + 1) * P], xb[i][:, t, 0:P], ident[:])
                m.then_inc(s["e_T_psum"], 1)
                pe.wait_ge(s[f"e_w{i}"], arrived(e, i, 32))
                pe.wait_ge(s["e_T"], 2 * e + 2)
                for j in range(FB):
                    for h in range(2):
                        held(pe, s["e_h_act" if h == 0 else "e_h_dve"], 4 * e + j)
                        pe.matmul(psQ[:, h, 0:CAP], eW1[i][:, j * P:(j + 1) * P], xbT[:, h * CAP:(h + 1) * CAP],
                                  start=True, stop=True).then_inc(s["e_h_psum"], 1)
                pe.wait_ge(s["e_h_act"], 4 * e + 4)
                pe.wait_ge(s["e_h_dve"], 4 * e + 4)
                held(pe, s["e_y_add"], 2 * e)
                for t in range(TILES):
                    for j in range(FB):
                        m = pe.matmul(psS[:, t // 4, (t % 4) * P:(t % 4 + 1) * P], hm[:, j, t * P:(t + 1) * P],
                                      eW2[i][:, j, :], start=(j == 0), stop=(j == FB - 1))
                m.then_inc(s["e_y_psum"], 1)

            over(pe, EXPERTS, expert)

        @block.scalar
        def _(act):
            act.wait_ge(ffnw_in, 32)
            for i, w in enumerate((w1_raw, w2_raw)):
                act.activation(tern[:, i, :], w[:].rearrange("p j d -> p (j d)"), ACT.Abs,
                               accum_out=wabs[:, i:i + 1]).then_inc(s["wabs_ready"], 1)
            for n in range(2):
                act.wait_ge(s["rel_n_ready"], n + 1)
                act.activation(rel_s[:], rel_n[:], ACT.Silu).then_inc(s["rel_s_ready"], 1)
            act.wait_ge(s["ternT_psum"], 1)
            act.copy(w1T[:], psT[:, 0, :]).then_inc(s["ffnw_ready"], 1)
            act.copy(w2T[:].rearrange("p j d -> p (j d)"), psT[:, 1, :]).then_inc(s["ffnw_ready"], 1)

            def input_T(layer, b, i):
                B = b + NB * layer
                act.wait_ge(s["xnT_psum"], B + 1)
                held(act, s["q_psum"], B - 1)
                c = C_GN0 if layer == 0 else C_GIN1
                act.activation(xnT[i][:], psA[:, 0:P], ACT.Copy, scale=cols[:, c:c + 1]).then_inc(
                    s["xnT_ready"], 1)

            def squares(b):
                act.wait_ge(s["q_psum"], b + 1)
                held(act, s["ss_step"], 2 * b)
                act.activation(qsq[:, 0:HEADS, :], psQ[:].rearrange("p a (h d) -> p (a h) d", d=DH), ACT.Square)
                act.activation(qsq[:, HEADS, :], psA[:, P:P + DH], ACT.Square).then_inc(s["sq_ready"], 1)

            def queries(layer, b, i):
                B = b + NB * layer
                if layer == 0:
                    act.wait_ge(s["qT_psum"], b + 1)
                else:
                    act.wait_ge(s["q_psum"], B + 1)
                held(act, s["scores_psum"], 4 * B - 4)
                for h in range(2):
                    m = act.activation(qT[i][:, h].rearrange("p u m q -> p m u q"),
                                       psQ[:, h, :].rearrange("p (m u q) -> p m u q", u=UNITS, q=QB), ACT.Copy,
                                       scale=1.0 if layer == 0 else DH ** -0.5)
                m.then_inc(s["q_ready"], 1)

            def keys_T(layer, b, i):
                B = b + NB * layer
                act.wait_ge(s["kT_psum"], B + 1)
                held(act, s["scores_psum"], 4 * B - 4)
                act.copy(kk[i][0:DH, 0, 1:P + 1], psA[0:DH, 2 * P:3 * P])
                act.copy(kk[i][DH:P, 1, 1:P + 1], psA[DH:P, 2 * P:3 * P]).then_inc(s["kk_ready"], 1)

            def weights(n, u):
                act.wait_ge(s["negmax_ready"], n + 1)
                for g in range(4):
                    v = sc[u][:, g // 2, g % 2, :]
                    m = act.activation(v, v, ACT.Exp, bias=negmax[:, u, g:g + 1], accum_out=psum_row[:, u, g:g + 1])
                m.then_inc(s["exp_done"], 1)

            def weights_T(n, u):
                act.wait_ge(s["probsT_psum"], n + 1)
                held(act, s["out_psum"], n - 1)
                k = WIDTH[u] - 1
                act.copy(PT[u % 2][0:k].rearrange("p h e q -> p (h e q)"), psT[0:k, u % 2, :]).then_inc(
                    s["probsT_ready"], 1)

            def attention(layer):
                def batch(b, i):
                    n = 4 * (b + NB * layer)
                    first, last = no(b, 0), no(b, NB - 1)
                    for u in range(UNITS):
                        if u == 0 and not last:
                            input_T(layer, b + 1, 1 - i)
                        if not (first and u < 2):
                            weights_T(n + u - 2, (u - 2) % UNITS)
                        if u == 1 and not last:
                            if layer == 0:
                                squares(b + 1)
                            else:
                                queries(layer, b + 1, 1 - i)
                        weights(n + u, u)
                        if layer == 1 and u == 2 and not last:
                            keys_T(layer, b + 1, 1 - i)
                        if layer == 0 and u == 3 and not last:
                            queries(layer, b + 1, 1 - i)
                            keys_T(layer, b + 1, 1 - i)

                if layer == 0:
                    act.wait_ge(s["cols_ready"], 1)
                input_T(layer, 0, 0)
                if layer == 0:
                    squares(0)
                queries(layer, 0, 0)
                keys_T(layer, 0, 0)
                over(act, NB, batch)
                N = 4 * (NB + NB * layer)
                weights_T(N - 2, 2)
                weights_T(N - 1, 3)

            attention(0)

            def f_in(t, i):
                act.wait_ge(s["f_h_psum"], t + 1)
                held(act, s["f_z_psum"], t - 1)
                act.activation(hT[i][:], psA[:, 0:P], ACT.Identity, scale=cols[:, C_LN1G:C_LN1G + 1],
                               bias=cols[:, C_LN1B:C_LN1B + 1]).then_inc(s["f_hT"], 1)

            def f_mid(t, i):
                act.wait_ge(s["f_gnT_psum"], t + 1)
                held(act, s["f_o_psum"], t - 1)
                for j in range(FB):
                    m = act.activation(gnT[i][:, j, :], psT[:, i, j * P:(j + 1) * P], ACT.Identity,
                                       scale=cols[:, C_LN2G + j:C_LN2G + j + 1],
                                       bias=cols[:, C_LN2B + j:C_LN2B + j + 1])
                m.then_inc(s["f_gnT"], 1)

            def f_gelu(t, i):
                act.wait_ge(s["f_z_ready"], t + 1)
                act.activation(z[:, i, :], z[:, i, :], ACT.Gelu).then_inc(s["f_gelu"], 1)

            def ffn(t, i):
                if not no(t, NB - 1):
                    f_in(t + 1, 1 - i)
                f_mid(t, i)
                if not no(t, NB - 1):
                    f_gelu(t + 1, 1 - i)

            f_in(0, 0)
            f_gelu(0, 0)
            over(act, NB, ffn)

            attention(1)

            def gate(t, i):
                act.wait_ge(s["r_T_psum"], t + 1)
                held(act, s["r_lg_psum"], t - 1)
                act.copy(hT[i][:], psA[:, 0:P]).then_inc(s["r_T"], 1)

            over(act, NB, gate)
            act.wait_ge(s["r_step"], 3)
            act.activation(le[:], le[:], ACT.Exp).then_inc(s["r_exp"], 1)

            def rows_T(e):
                act.wait_ge(s["e_T_psum"], e + 1)
                held(act, s["e_h_psum"], 8 * e)
                act.copy(xbT[:, 0:512], psT[:, 0, :]).then_inc(s["e_T"], 1)
                act.copy(xbT[:, 512:TILES * P], psT[:, 1, 0:P]).then_inc(s["e_T"], 1)

            def expert(e, i):
                held(act, s["e_y_psum"], e)
                for j in range(FB):
                    act.wait_ge(s["e_h_psum"], 8 * e + 2 * j + 1)
                    act.activation(hm[:, j, 0:CAP], psQ[:, 0, 0:CAP], ACT.Relu,
                                   bias=cols[:, bass.ds(4 * e + (C_MB1 + j), 1)]).then_inc(s["e_h_act"], 1)
                if not no(e, EXPERTS - 1):
                    rows_T(e + 1)
                act.wait_ge(s["e_y_add"], 2 * e + 2)
                for t in range(TILES):
                    act.activation(yb[i][:, t, :], yb[i][:, t, :], ACT.Copy,
                                   scale=xb[i][:, t, P + 1:P + 2]).then_inc(s["e_y"], 1)

            rows_T(0)
            over(act, EXPERTS, expert)

        @block.vector
        def _(dve):
            steps = 0

            def step(ins):
                nonlocal steps
                ins.then_inc(dve_step, 1)
                steps += 1
                dve.wait_ge(dve_step, steps)

            def norm_scale(dst, src, k, n, eps=LN_EPS):
                dve.tensor_scalar(dst, src, eps, None, ALU.add).then_inc(s["ln_var"], 1)
                dve.wait_ge(s["ln_rstd"], n)

            dve.wait_ge(const_done, CONSTS)
            step(dve.tensor_copy(pos_f[:], pos_i[:]))
            step(dve.tensor_copy(trash[:], trash_i[:]))
            step(dve.tensor_copy(cbase[:], cbase_i[:]))
            step(dve.tensor_copy(io_f[:], io_i[:]))
            dve.wait_ge(bcast_in, 16 * BCAST_DMAS)

            def rel_norm(n, g):
                step(dve.bn_stats(stats[:, 0, :], rel_h[:]))
                step(dve.bn_aggr(mv[:, 0, :], stats[:, 0, :]))
                norm_scale(small[:, 2 * n:2 * n + 1], mv[:, 0, 1:2], 1, n + 1)
                step(dve.tensor_scalar(rel_n[:], rel_h[:], mv[:, 0, 0:1], small[:, 2 * n + 1:2 * n + 2],
                                       ALU.subtract, ALU.mult))
                dve.tensor_tensor(rel_n[:], rel_n[:], g, ALU.mult).then_inc(s["rel_n_ready"], 1)

            step(dve.scalar_tensor_tensor(rel_h[:], rel_rows[:, 0, :], pos_f[:], rel_rows[:, 1, :],
                                          ALU.mult, ALU.add))
            rel_norm(0, rel_rows[:, 2, :])
            dve.wait_ge(s["rel_psum"], 1)
            dve.tensor_copy(rel_T[:], psQ[:, 0, 0:P]).then_inc(s["rel_T_ready"], 1)
            dve.wait_ge(s["rel_psum"], 2)
            step(dve.tensor_tensor(rel_h[:], psQ[:, 0, P:2 * P], rel_rows[:, 3, :], ALU.add))
            rel_norm(1, rel_rows[:, 4, :])
            dve.wait_ge(s["rel_psum"], 3)
            dve.tensor_copy(rel_T[:], psQ[:, 0, 2 * P:3 * P]).then_inc(s["rel_T_ready"], 1)
            dve.wait_ge(s["rel_psum"], 4)
            step(dve.tensor_scalar(rel_tab[:, 0:P], psQ[0:HEADS, 0, 3 * P:4 * P], rel_b2[:], None, ALU.add))
            dve.tensor_copy(half[:, 18:19], half[:, 19:20]).then_inc(rel_out, 1)
            dve.wait_ge(s["cols_psum"], 2)
            step(dve.tensor_copy(gateT[:], psA[:, 64:64 + EXPERTS]))
            dve.tensor_copy(cols[:, 0:N_ROWS], psA[:, 0:N_ROWS]).then_inc(s["cols_ready"], 1)
            dve.wait_ge(s["cols_ready"], 1)
            step(dve.tensor_tensor(rel_h[:, 0:DH], nk_row[:], nk_row[:], ALU.mult))
            step(dve.tensor_reduce(small[:, 6:7], rel_h[:, 0:DH], X_AXIS, ALU.add))
            step(dve.tensor_scalar(small[:, 7:8], small[:, 6:7], 1e-24, None, ALU.max))
            norm_scale(small[:, 4:5], small[:, 7:8], 1, 3, 0.0)
            step(dve.tensor_tensor(nk0[:], cols[:, C_NK:C_NK + 1], small[:, 5:6], ALU.mult))
            step(dve.tensor_tensor(nk0[:], nk0[:], cols[:, C_QS:C_QS + 1], ALU.mult))
            step(dve.scalar_tensor_tensor(nk0[:], nk0[:], 8.0, cols[:, C_KS:C_KS + 1], ALU.mult, ALU.mult))

            def null_keys(column):
                for i in range(2):
                    for e in range(2):
                        half_of = slice(DH * e, DH * (e + 1))
                        dve.tensor_copy(kk[i][half_of, e, 0:1], column[half_of]).then_inc(s["kk_null"], 1)

            null_keys(nk0[:])
            step(dve.tensor_tensor(kqs[:], kqs[:], qs_row[:], ALU.mult))
            step(dve.tensor_scalar(kqs[:], kqs[:], 8.0, None, ALU.mult))
            for layer in range(2):
                step(dve.tensor_scalar(mask[layer][:, :, 1:P + 1],
                                       mask_u8[layer][:].rearrange("p (b k) -> p b k", k=P), -MASKED, MASKED,
                                       ALU.mult, ALU.add))
            dve.wait_ge(s["cols_psum"], 3)
            step(dve.tensor_scalar(wmean[:], psO[:, 0:2], 1.0 / (HIDDEN * P), 1e-5, ALU.mult, ALU.max))
            step(dve.reciprocal(wscale[:], wmean[:]))
            for i, w in enumerate((w1_raw, w2_raw)):
                flat_w = w[:].rearrange("p j d -> p (j d)")
                step(dve.tensor_scalar(tern[:, i, :], flat_w, wscale[:, i:i + 1], 0.5, ALU.mult, ALU.is_gt))
                step(dve.tensor_scalar(z[:, i, :], flat_w, wscale[:, i:i + 1], -0.5, ALU.mult, ALU.is_lt))
                dve.tensor_tensor(tern[:, i, :], tern[:, i, :], z[:, i, :], ALU.subtract).then_inc(
                    s["tern_ready"], 1)
            for layer in range(2):
                for u in range(UNITS):
                    ins = dve.tensor_copy(unit_bias(layer, u)[:, :, :, 0],
                                          nullb[layer][:].rearrange("p (h e) -> p h e", e=2))
            ins.then_inc(s["setup_read"], 1)

            def norm_stats(src, n):
                nonlocal steps
                with dve.Fori(0, NB) as t:
                    dve.bn_stats(stats[:, t, :], src[:, t, :]).then_inc(dve_step, 1)
                steps += NB
                dve.wait_ge(dve_step, steps)
                for t in range(NB):
                    ins = dve.bn_aggr(mv[:, t, :], stats[:, t, :])
                step(ins)
                norm_scale(ve[:], mv[:, :, 1], NB, n)

            def normed(t):
                return mv[:, t, 0:1], rstd[:, bass.ds(t, 1)]

            def norm_output(layer, n):
                nonlocal steps
                norm_stats(Y, n)
                with dve.Fori(0, NB) as t:
                    mean, r = normed(t)
                    dve.tensor_scalar(Y[:, t, :], Y[:, t, :], mean, r, ALU.subtract, ALU.mult).then_inc(
                        dve_step, 1)
                steps += NB
                dve.wait_ge(dve_step, steps)
                dve.tensor_tensor(Y[:], Y[:], g_out[layer][:].unsqueeze(1).broadcast_to([P, NB, P]),
                                  ALU.mult).then_inc(s["normed"], 1)
                dve.wait_ge(s["normed"], layer + 1)

            def input_norm(layer, b, i):
                B = b + NB * layer
                held(dve, s["xnT_psum"], B - 1)
                mean, r = normed(b)
                dve.tensor_scalar(xn[:, i, :], X[:, b, :], mean, r, ALU.subtract, ALU.mult).then_inc(
                    s["xn_ready"], 1)

            def values_in(layer, b, i):
                B = b + NB * layer
                dve.wait_ge(s["kk_ready"], B + 1)
                held(dve, s["out_psum"], 4 * B - 4)
                dve.tensor_tensor(vp[i][:], psA[:, P + DH:2 * P], vnull[:], ALU.subtract).then_inc(
                    s["kv_ready"], 1)

            def keys_in(layer, b, i):
                B = b + NB * layer
                dve.wait_ge(s["kv_psum"], B + 1)
                held(dve, s["kT_psum"], B - 1)
                k_raw = psA[:, P:P + DH].unsqueeze(1).broadcast_to([P, 2, DH])
                if layer == 0:
                    ins = dve.scalar_tensor_tensor(kd[i][:], k_raw, qrn[:, HEADS:HEADS + 1],
                                                   kqs[:].unsqueeze(1).broadcast_to([P, 2, DH]),
                                                   ALU.mult, ALU.mult)
                else:
                    ins = dve.tensor_copy(kd[i][:], k_raw)
                ins.then_inc(s["kv_ready"], 1)

            def sum_squares(b):
                dve.wait_ge(s["sq_ready"], b + 1)
                dve.tensor_reduce(qss[:], qsq[:], X_AXIS, ALU.add).then_inc(s["ss_step"], 1)
                dve.wait_ge(s["ss_step"], 2 * b + 1)
                dve.tensor_scalar(qssc[:], qss[:], 1e-24, None, ALU.max).then_inc(s["ss_step"], 1)

            def queries_norm(b):
                dve.wait_ge(s["rn_ready"], b + 1)
                held(dve, s["qT_psum"], b)
                dve.tensor_tensor(qn[:].rearrange("p (h d) -> p h d", d=DH),
                                  psQ[:].rearrange("p a (h d) -> p (a h) d", d=DH),
                                  qrn[:, 0:HEADS].unsqueeze(2).broadcast_to([P, HEADS, DH]),
                                  ALU.mult).then_inc(s["qn_ready"], 1)

            def biased(n, u, i):
                held(dve, s["probs_ready"], n - 3)
                dve.wait_ge(s["bias_ready"], n + 1)
                dve.wait_ge(s["scores_psum"], n + 1)
                dve.tensor_tensor(sc[u][:], unit_psum(u), unit_masked(i, u), ALU.add).then_inc(s["scores_ready"], 1)
                dve.wait_ge(s["scores_ready"], n + 1)
                dve.tensor_reduce(negmax[:, u, :], sc[u][:].rearrange("p h e k -> p (h e) k"), X_AXIS,
                                  ALU.max, negate=True).then_inc(s["negmax_ready"], 1)

            def sums(n, u):
                dve.wait_ge(s["exp_done"], n + 1)
                dve.reciprocal(rsum[:, u, :], psum_row[:, u, :]).then_inc(s["rsum_ready"], 1)

            def outputs(layer, n, b, u, i):
                B = b + NB * layer
                dve.wait_ge(s["out_psum"], n + 1)
                if u == 0:
                    held(dve, s["y_psum"], B - 1)
                dve.tensor_scalar(OT[i][:, :, u, :], psO[:, 0:256].rearrange("p (j q) -> p j q", q=QB),
                                  cols[:, C_VN:C_VN + 1], None, ALU.add).then_inc(s["out_ready"], 1)

            def project_out(layer, b):
                B = b + NB * layer
                dve.wait_ge(s["y_psum"], B + 1)
                dve.tensor_copy(Y[:, b, :], psA[:, 3 * P:4 * P]).then_inc(s["y_done"], 1)

            def attention(layer):
                def batch(b, i):
                    B = b + NB * layer
                    n = 4 * B
                    first, last = no(b, 0), no(b, NB - 1)
                    for u in range(UNITS):
                        if u == 0 and not first and not no(b, 1):
                            project_out(layer, b - 2)
                        biased(n + u, u, i)
                        if not (first and u < 1):
                            sums(n + u - 1, (u - 1) % UNITS)
                        if layer == 1 and u == 1 and not last:
                            keys_in(layer, b + 1, 1 - i)
                        if layer == 0 and u == 2 and not last:
                            queries_norm(b + 1)
                            keys_in(layer, b + 1, 1 - i)
                        if not (first and u < 3):
                            outputs(layer, n + u - 3, b if u == 3 else b - 1, (u - 3) % UNITS, i if u == 3 else 1 - i)
                        if layer == 0 and u == 1 and not last:
                            sum_squares(b + 1)
                        if u == 3 and not last:
                            values_in(layer, b + 1, 1 - i)
                        if u == 3 and not last and not no(b, NB - 2):
                            input_norm(layer, b + 2, i)

                input_norm(layer, 0, 0)
                input_norm(layer, 1, 1)
                if layer == 0:
                    sum_squares(0)
                    queries_norm(0)
                keys_in(layer, 0, 0)
                values_in(layer, 0, 0)
                over(dve, NB, batch)
                n = 4 * (NB + NB * layer)
                project_out(layer, NB - 2)
                sums(n - 1, 3)
                outputs(layer, n - 3, NB - 1, 1, 1)
                outputs(layer, n - 2, NB - 1, 2, 1)
                outputs(layer, n - 1, NB - 1, 3, 1)
                project_out(layer, NB - 1)
                dve.wait_ge(s["y_done"], NB * (layer + 1))

            dve.wait_ge(x_in, 16)
            norm_stats(X, 4)
            attention(0)

            norm_output(0, 5)
            norm_stats(Y, 6)

            def f_norm_in(t, i):
                held(dve, s["f_h_psum"], t - 1)
                mean, r = normed(t)
                dve.tensor_scalar(xn[:, i, :], Y[:, t, :], mean, r, ALU.subtract, ALU.mult).then_inc(s["f_h"], 1)

            def f_hidden(t, i):
                dve.wait_ge(s["f_z_psum"], t + 1)
                dve.scalar_tensor_tensor(z[:, i, :], psQ[:, i, :], wmean[:, 0:1], fb1[:], ALU.mult,
                                         ALU.add).then_inc(s["f_z_ready"], 1)

            def f_stats(t, i):
                dve.wait_ge(s["f_gelu"], t + 1)
                dve.bn_stats(zst[:, i, :], z[:, i, :]).then_inc(s["f_stat"], 1)
                apart(dve, (s["f_stat"], 2 * t + 1))
                dve.bn_aggr(zmv[:, i, :], zst[:, i, :]).then_inc(s["f_stat"], 1)
                dve.wait_ge(s["f_stat"], 2 * t + 2)
                dve.tensor_scalar(zve[:, i:i + 1], zmv[:, i, 1:2], LN_EPS, None, ALU.add).then_inc(s["f_var"], 1)

            def f_norm_mid(t, i):
                dve.wait_ge(s["f_rstd"], t + 1)
                held(dve, s["f_gnT_psum"], t - 1)
                dve.tensor_scalar(gn[:, i, :], z[:, i, :], zmv[:, i, 0:1], zrstd[:, i:i + 1], ALU.subtract,
                                  ALU.mult).then_inc(s["f_gn"], 1)

            def f_out(t):
                dve.wait_ge(s["f_o_psum"], t + 1)
                dve.scalar_tensor_tensor(ffo[:], psO[:, 0:P], wmean[:, 1:2], fb2[:], ALU.mult,
                                         ALU.add).then_inc(s["f_o_step"], 1)
                dve.wait_ge(s["f_o_step"], 2 * t + 1)
                dve.tensor_tensor(X[:, t, :], X[:, t, :], ffo[:], ALU.add).then_inc(s["f_o_step"], 1)

            def ffn(t, i):
                f_norm_mid(t, i)
                if not no(t, NB - 1) and not no(t, NB - 2):
                    f_norm_in(t + 2, i)
                if not no(t, NB - 1):
                    f_hidden(t + 1, 1 - i)
                f_out(t)
                if not no(t, NB - 1):
                    f_stats(t + 1, 1 - i)

            f_norm_in(0, 0)
            f_norm_in(1, 1)
            f_hidden(0, 0)
            f_stats(0, 0)
            over(dve, NB, ffn)
            dve.wait_ge(s["f_o_step"], 2 * NB)

            null_keys(cols[:, C_NK:C_NK + 1])
            norm_stats(X, 7)
            attention(1)

            norm_output(1, 8)

            def gate(t, i):
                held(dve, s["r_T_psum"], t - 1)
                dve.tensor_copy(xn[:, i, :], Y[:, t, :]).then_inc(s["r_x"], 1)

            over(dve, NB, gate)

            def wide(v, shape, axis):
                return v.unsqueeze(axis).broadcast_to(shape)

            TE = [P, NB, EXPERTS]
            TCE = [P, NB, TOPK, EXPERTS]
            dve.wait_ge(s["r_lg_psum"], NB)
            dve.tensor_tensor(lg[:], psQ[:, 0, 0:P].rearrange("p (t e) -> p t e", e=EXPERTS),
                              wide(gate_b[:], TE, 1), ALU.add).then_inc(s["r_step"], 1)
            dve.wait_ge(s["r_step"], 1)
            dve.tensor_reduce(lgm[:], lg[:], X_AXIS, ALU.max, negate=True).then_inc(s["r_step"], 1)
            dve.wait_ge(s["r_step"], 2)
            dve.tensor_tensor(le[:], lg[:], wide(lgm[:], TE, 2), ALU.add).then_inc(s["r_step"], 1)
            dve.wait_ge(s["r_exp"], 1)
            step(dve.tensor_reduce(lsum[:], le[:], X_AXIS, ALU.add))
            step(dve.reciprocal(lsum[:], lsum[:]))
            step(dve.tensor_tensor(prob[:], le[:], wide(lsum[:], TE, 2), ALU.mult))
            for t in range(NB):
                ins = dve.max(top[:, t, :], prob[:, t, :])
            step(ins)
            for t in range(NB):
                ins = dve.max_index(topi[:, t, :], top[:, t, :], prob[:, t, :])
            step(ins)
            step(dve.tensor_copy(topf[:], topi[:, :, 0:TOPK]))
            step(dve.tensor_tensor(oh[:].rearrange("p t c e -> p (t c) e"),
                                   wide(io_f[:], [P, NB * TOPK, EXPERTS], 1),
                                   wide(topf[:].rearrange("p t c -> p (t c)"), [P, NB * TOPK, EXPERTS], 2),
                                   ALU.is_equal))
            dve.tensor_copy(oh_bf[:], oh[:]).then_inc(s["r_oh"], 1)
            dve.wait_ge(s["r_pos_psum"], 1)
            counted = psQ[:, 1, :].rearrange("p (w t ce) -> p w t ce", w=2, ce=TOPK * EXPERTS)
            baset = base[:].rearrange("p t c e -> p t (c e)")
            step(dve.memset(baset[:, 0, :], 0.0))
            for t in range(1, NB):
                step(dve.tensor_tensor(baset[:, t, :], baset[:, t - 1, :], counted[:, 1, t - 1, :], ALU.add))
            step(dve.tensor_tensor(posn[:].rearrange("p t c e -> p t (c e)"), counted[:, 0], baset, ALU.add))
            dve.tensor_tensor(posn[:], posn[:], oh[:], ALU.mult).then_inc(s["r_pos_read"], 1)
            dve.wait_ge(s["r_pos_read"], 1)
            step(dve.tensor_reduce(own[:], posn[:], X_AXIS, ALU.add))
            step(dve.tensor_scalar(keep[:], own[:], float(CAP), None, ALU.is_lt))
            step(dve.scalar_tensor_tensor(dest[:], topf[:], float(TOPK * CAP), cbase[:], ALU.mult, ALU.add))
            step(dve.tensor_tensor(dest[:], dest[:], own[:], ALU.add))
            step(dve.scalar_tensor_tensor(dest[:], dest[:], trash[:], keep[:], ALU.subtract, ALU.mult))
            step(dve.tensor_scalar(dest[:], dest[:], trash[:], None, ALU.add))
            dve.tensor_copy(dest_u[:], dest[:]).then_inc(s["r_pay"], 1)
            dve.tensor_tensor(pay[:, :, :, P + 1], top[:, :, 0:TOPK], keep[:], ALU.mult).then_inc(s["r_pay"], 1)

            def expert(e, i):
                held(dve, s["e_y_psum"], e)
                for j in range(FB):
                    dve.wait_ge(s["e_h_psum"], 8 * e + 2 * j + 2)
                    dve.tensor_scalar(hm[:, j, CAP:2 * CAP], psQ[:, 1, 0:CAP],
                                      cols[:, bass.ds(4 * e + (C_MB1 + j), 1)], 0.0, ALU.add,
                                      ALU.max).then_inc(s["e_h_dve"], 1)
                dve.wait_ge(s["e_y_psum"], e + 1)
                held(dve, s["e_sent"], 16 * TILES * (e - 1))
                dve.tensor_tensor(yb[i][:, 0:4, :], psS[:, 0, :].rearrange("p (t d) -> p t d", d=P),
                                  mb2[:, bass.ds(e, 1), :].broadcast_to([P, 4, P]), ALU.add).then_inc(s["e_y_add"], 1)
                dve.tensor_tensor(yb[i][:, 4:5, :], psS[:, 1:2, 0:P], mb2[:, bass.ds(e, 1), :],
                                  ALU.add).then_inc(s["e_y_add"], 1)

            over(dve, EXPERTS, expert)
            for q in range(4):
                dve.wait_ge(s["back_ready"], q + 1)
                for c in range(TOPK):
                    v = X[:, 4 * q:4 * q + 4, :]
                    dve.tensor_tensor(v, v, back[:, c, 4 * q:4 * q + 4, :], ALU.add).then_inc(s["z_step"], 1)
                    dve.wait_ge(s["z_step"], 2 * q + c + 1)


INPUTS = ["x", "cond_64", "fside_16xSxS_0", "mask_BxS_bf1", "mask_BxS_bk0", "L0_cond_g_norm", "L0_cond_Wq",
          "L0_cond_Wkv", "L0_cond_q_scale", "L0_cond_k_scale", "L0_cond_null_attn_bias", "L0_cond_w0",
          "L0_cond_b0", "L0_cond_g0", "L0_cond_w1", "L0_cond_b1", "L0_cond_g1", "L0_cond_w2", "L0_cond_b2",
          "L0_cond_Wout", "L0_cond_g_out", "L0_ffn_ln1_g", "L0_ffn_ln1_b", "L0_ffn_w1", "L0_ffn_b1",
          "L0_ffn_ln2_g", "L0_ffn_ln2_b", "L0_ffn_w2", "L0_ffn_b2", "L1_cond_g_in", "L1_cond_null_attn_bias",
          "L1_cond_Wq", "L1_cond_Wkv", "L1_cond_Wo", "L1_cond_g_out", "L1_ffn_gate_w", "L1_ffn_gate_b",
          "L1_ffn_W1", "L1_ffn_b1", "L1_ffn_W2", "L1_ffn_b2"]


def kernel(**inputs):
    import numpy as np
    import concourse.bacc as bacc
    from concourse.bass_utils import run_bass_kernel_spmd

    nc = bacc.Bacc("TRN2", target_bir_lowering=False, num_devices=1)
    arrays, aps = {}, {}
    for name in INPUTS:
        v = np.ascontiguousarray(inputs[name])
        if v.dtype == np.bool_:
            v = v.view(np.uint32)
        arrays["in_" + name] = v
        aps[name] = nc.dram_tensor("in_" + name, v.shape, mybir.dt.from_np(v.dtype), kind="ExternalInput").ap()
    out = nc.dram_tensor("out_x", (NB, P, P), F32, kind="ExternalOutput").ap()
    build(nc, aps, out)
    return run_bass_kernel_spmd(nc, [arrays], core_ids=[0]).results[0]["out_x"]
```

```python
from contextlib import ExitStack

import concourse.bass as bass
from concourse import mybir

F32 = mybir.dt.float32
BF16 = mybir.dt.bfloat16
U32 = mybir.dt.uint32
I32 = mybir.dt.int32
U8 = mybir.dt.uint8
ALU = mybir.AluOpType
ACT = mybir.ActivationFunctionType
X_AXIS = mybir.AxisListType.X

P = 128
NB = 16
HEADS = 16
DH = 64
HIDDEN = 512
FB = HIDDEN // P
EXPERTS = 8
CAP = 320
TOPK = 2
SLOTS = EXPERTS * CAP
TILE_ROWS = [P, P, CAP - 2 * P]
TILES = len(TILE_ROWS)
ROW = 132
QB = 32
UNITS = P // QB
KEYS = P + 2
WIDTH = [QB * (u + 1) + 1 for u in range(UNITS)]
BIAS_AT = [4 * sum(WIDTH[:u]) for u in range(UNITS + 1)]
CONSTS = 18
ROWS_DMAS = 15
BCAST_DMAS = 29
SCRATCH_ALL = 1 + 16 * (TOPK * TILES + TOPK * NB // 4)
FAR = -1e30
MASKED = -1e20
LN_EPS = 1e-5


def build(nc, a, out):
    ctx = ExitStack()
    with ctx:
        def sb(name, shape, dt=F32):
            return ctx.enter_context(nc.sbuf_tensor(name, shape, dt))

        def pb(name, shape, dt=F32):
            return ctx.enter_context(nc.psum_tensor(name, shape, dt))

        def sem(name):
            return ctx.enter_context(nc.semaphore(name))

        def dram(name, shape, dt=F32):
            return nc.dram_tensor(name, shape, dt).ap()

        def at(ap, offset, dims):
            return bass.AP(ap.tensor, offset, dims)

        rel_d = dram("rel_scratch", (HEADS, QB, 2 * P))
        slot_d = [dram(f"slot_rows{c}", (SLOTS + P, ROW)) for c in range(TOPK)]
        back_d = [dram(f"choice_rows{c}", (NB * P + P, P)) for c in range(TOPK)]

        X = sb("X", [P, NB, P])
        Y = sb("Y", [P, NB, P])
        ident = sb("ident", [P, P])
        ones = sb("ones", [P, P])
        ones_bf = sb("ones_bf", [P, P], BF16)
        before_bf = sb("before_bf", [P, P], BF16)
        rows = sb("rows", [P, P])
        cols = sb("cols", [P, P])
        Wq = [sb("Wq0", [P, HEADS * DH]), sb("Wq1", [P, HEADS * DH])]
        Wkv = [sb("Wkv0", [P, P]), sb("Wkv1", [P, P])]
        Wo = [sb("Wo0", [P, 8, P]), sb("Wo1", [P, 8, P])]
        bias = [sb("bias0", [P, BIAS_AT[-1]]), sb("bias1", [P, BIAS_AT[-1]])]
        nullb = [sb("nullb0", [P, 4]), sb("nullb1", [P, 4])]
        mask_u8 = [sb("mask0_u8", [P, NB * P], U8), sb("mask1_u8", [P, NB * P], U8)]
        mask = [sb("mask0", [P, NB, KEYS], BF16), sb("mask1", [P, NB, KEYS], BF16)]
        g_out = [sb("g_out0", [P, P]), sb("g_out1", [P, P])]
        kqs = sb("kqs", [P, DH])
        qs_row = sb("qs_row", [P, DH])
        nk_row = sb("nk_row", [P, DH])
        vnull = sb("vnull", [P, DH])
        nk0 = sb("nk0", [P, 1])
        w1_raw = sb("w1_raw", [P, FB, P])
        w2_raw = sb("w2_raw", [P, FB, P])
        w1T = sb("w1T", [P, HIDDEN])
        w2T = sb("w2T", [P, FB, P])
        tern = sb("tern", [P, 2, HIDDEN])
        wabs = sb("wabs", [P, 2])
        wmean = sb("wmean", [P, 2])
        wscale = sb("wscale", [P, 2])
        fb1 = sb("fb1", [P, HIDDEN])
        fb2 = sb("fb2", [P, P])
        rel_rows = sb("rel_rows", [P, 5, P])
        rel_w1 = sb("rel_w1", [P, P])
        rel_w2 = sb("rel_w2", [P, HEADS])
        rel_b2 = sb("rel_b2", [HEADS, 1])
        rel_h = sb("rel_h", [P, P])
        rel_n = sb("rel_n", [P, P])
        rel_s = sb("rel_s", [P, P])
        rel_T = sb("rel_T", [P, P])
        rel_tab = sb("rel_tab", [HEADS, 2 * P])
        pos_i = sb("pos_i", [P, 1], I32)
        pos_f = sb("pos_f", [P, 1])
        half = sb("half", [P, 20])
        small = sb("small", [P, 16])
        gate_rows = sb("gate_rows", [EXPERTS, P])
        gateT = sb("gateT", [P, EXPERTS])
        gate_b = sb("gate_b", [P, EXPERTS])
        mb2 = sb("mb2", [P, EXPERTS, P])

        stats = sb("stats", [P, NB, 6])
        mv = sb("mv", [P, NB, 2])
        ve = sb("ve", [P, NB])
        rstd = sb("rstd", [P, NB])

        xn = sb("xn", [P, 2, P])
        xnT = [sb("xnT0", [P, P]), sb("xnT1", [P, P])]
        qsq = sb("qsq", [P, HEADS + 1, DH])
        qss = sb("qss", [P, HEADS + 1])
        qssc = sb("qssc", [P, HEADS + 1])
        qrn = sb("qrn", [P, HEADS + 1])
        qn = sb("qn", [P, HEADS * DH])
        qT = [sb("qT0", [P, 2, UNITS, 4, QB]), sb("qT1", [P, 2, UNITS, 4, QB])]
        kd = [sb("kd0", [P, 2, DH]), sb("kd1", [P, 2, DH])]
        vs = sb("vs", [P, DH])
        vp = [sb("vp0", [P, DH]), sb("vp1", [P, DH])]
        kk = [sb("kk0", [P, 2, KEYS]), sb("kk1", [P, 2, KEYS])]
        sc = [sb(f"sc{u}", [P, 2, 2, WIDTH[u]]) for u in range(UNITS)]
        negmax = sb("negmax", [P, UNITS, 4])
        psum_row = sb("psum_row", [P, UNITS, 4])
        rsum = sb("rsum", [P, UNITS, 4])
        pn = [sb(f"pn{i}", [P, 4, P]) for i in range(2)]
        PT = [sb(f"PT{i}", [P, 2, 2, P]) for i in range(2)]
        OT = [sb(f"OT{i}", [P, 8, UNITS, QB]) for i in range(2)]

        z = sb("z", [P, 2, HIDDEN])
        hT = [sb("hT0", [P, P]), sb("hT1", [P, P])]
        gn = sb("gn", [P, 2, HIDDEN])
        gnT = [sb("gnT0", [P, FB, P]), sb("gnT1", [P, FB, P])]
        zst = sb("zst", [P, 2, 6])
        zmv = sb("zmv", [P, 2, 2])
        zve = sb("zve", [P, 2])
        zrstd = sb("zrstd", [P, 2])
        ffo = sb("ffo", [P, P])

        lg = sb("lg", [P, NB, EXPERTS])
        lgm = sb("lgm", [P, NB])
        le = sb("le", [P, NB, EXPERTS])
        lsum = sb("lsum", [P, NB])
        prob = sb("prob", [P, NB, EXPERTS])
        top = sb("top", [P, NB, 8])
        topi = sb("topi", [P, NB, 8], U32)
        topf = sb("topf", [P, NB, TOPK])
        io_i = sb("io_i", [P, EXPERTS], I32)
        io_f = sb("io_f", [P, EXPERTS])
        oh = sb("oh", [P, NB, TOPK, EXPERTS])
        oh_bf = sb("oh_bf", [P, NB, TOPK, EXPERTS], BF16)
        cnt = sb("cnt", [P, NB, TOPK, EXPERTS])
        base = sb("base", [P, NB, TOPK, EXPERTS])
        posn = sb("posn", [P, NB, TOPK, EXPERTS])
        own = sb("own", [P, NB, TOPK])
        keep = sb("keep", [P, NB, TOPK])
        dest = sb("dest", [P, NB, TOPK])
        dest_u = sb("dest_u", [P, NB, TOPK], U32)
        trash_i = sb("trash_i", [P, 1], I32)
        trash = sb("trash", [P, 1])
        tok_i = sb("tok_i", [P, NB], I32)
        pay = sb("pay", [P, NB, ROW])
        wide_buf = sb("wide_buf", [P, TOPK * NB * P])
        empty = sb("empty", [P, ROW])
        zero_row = sb("zero_row", [P, 4, P])
        ept = sb("ept_id", [P, 1], I32)

        eW1 = [sb("eW10", [P, HIDDEN]), sb("eW11", [P, HIDDEN])]
        eW2 = [sb("eW20", [P, FB, P]), sb("eW21", [P, FB, P])]
        xb = [sb(f"xb{i}", [P, TOPK, TILES, ROW]) for i in range(2)]
        xbT = sb("xbT", [P, TOPK * CAP])
        hm = sb("hm", [P, FB, TOPK * CAP])
        tags = [sb(f"tags{i}", [P, TOPK, TILES, 4]) for i in range(2)]
        yb = [v[:, 0:TOPK * TILES * P].rearrange("p (c t d) -> p c t d", c=TOPK, t=TILES)
              for v in (gn[:].rearrange("p i d -> p (i d)"), qn[:])]
        masked_bias = [wide_buf[:, i * BIAS_AT[-1]:(i + 1) * BIAS_AT[-1]] for i in range(2)]
        back = wide_buf[:].rearrange("p (c t d) -> p c t d", c=TOPK, t=NB)

        psS = pb("psS", [P, 2, 512])
        psT = pb("psT", [P, 2, 512])
        psQ = pb("psQ", [P, 2, 512])
        psO = pb("psO", [P, 512])
        psA = pb("psA", [P, 512])

        psH = [[psQ[:, 0, :], psQ[:, 1, :]], [psO[:], psA[:]]]

        C_GN0, C_GIN1, C_LN1G, C_LN1B, C_LN2G, C_LN2B, C_MB1 = 0, 1, 2, 3, 4, 8, 12
        C_VN, C_NK, C_QS, C_KS = 44, 45, 46, 47
        N_ROWS = 48

        rows_in = sem("rows_in")
        x_in = sem("x_in")
        bcast_in = sem("bcast_in")
        ffnw_in = sem("ffnw_in")
        attw_in = sem("attw_in")
        table_in = sem("table_in")
        rel_out = sem("rel_out")
        rel_in = sem("rel_in")
        scratch_out = sem("scratch_out")
        const_done = sem("const_done")
        pool_step = sem("pool_step")
        dve_step = sem("dve_step")

        names = ["xn_ready", "xnT_psum", "xnT_ready", "kv_psum", "q_psum", "k_ready", "v_read", "v_ready", "kT_psum",
                 "kk_ready", "q_ready", "sq_ready", "ss_step", "rn_ready", "qn_ready", "qT_psum",
                 "scores_psum", "scores_ready", "negmax_ready", "exp_done", "rsum_ready",
                 "probs_ready", "probsT_psum", "probsT_ready", "out_psum", "out_ready", "y_psum",
                 "y_done", "kk_null", "bias_ready"]
        s = {n: sem(n) for n in names}
        for n in ["cols_psum", "wabs_ready", "rel_s_ready", "rel_n_ready", "rel_psum", "rel_T_ready",
                  "tern_ready", "ternT_psum", "setup_read", "ffnw_ready", "normed", "cols_ready", "r_x",
                  "mul_ready"]:
            s[n] = sem(n)
        for n in ["f_h", "f_h_psum", "f_hT", "f_z_psum", "f_z_ready", "f_gelu", "f_stat", "f_var", "f_rstd",
                  "f_gn", "f_gnT_psum", "f_gnT", "f_o_psum", "f_o_step"]:
            s[n] = sem(n)
        for n in ["ln_step", "ln_var", "ln_rstd", "r_T_psum", "r_T", "r_lg_psum", "r_step", "r_exp",
                  "r_oh", "r_pos_read", "r_pos_psum", "r_pay", "r_pool", "slots_out0", "slots_out1", "e_w0", "e_w1", "e_x0", "e_x1",
                  "e_T_psum", "e_T", "e_h_psum", "e_h_act", "e_h_dve", "e_y_psum", "e_y_add", "e_y0", "e_y1",
                  "e_out", "back_in", "z_step", "final_out", "back_ready", "e_sent0", "e_sent1", "e_tags"]:
            s[n] = sem(n)

        def unit_bias(layer, u):
            return bias[layer][:, BIAS_AT[u]:BIAS_AT[u + 1]].rearrange(
                "p (h e k) -> p h e k", h=2, e=2)

        def unit_masked(i, u):
            return masked_bias[i][:, BIAS_AT[u]:BIAS_AT[u + 1]].rearrange("p (h e k) -> p h e k", h=2, e=2)

        def unit_psum(u):
            return psS[:, :, 0:2 * WIDTH[u]].rearrange("p h (e k) -> p h e k", e=2)

        block = ctx.enter_context(nc.Block())

        def over(eng, count, body):
            body(0, 0)
            body(1, 1)
            with eng.Fori(1, count // 2 - 1) as k:
                body(2 * k, 0)
                body(2 * k + 1, 1)
            body(count - 2, 0)
            body(count - 1, 1)

        def held(eng, semaphore, value):
            if not (isinstance(value, int) and value <= 0):
                eng.wait_ge(semaphore, value)

        def apart(eng, *waits):
            values = [v if isinstance(v, int) else eng.to_reg(v) for _, v in waits]
            eng.wait_ge(const_done, CONSTS)
            for (semaphore, _), v in zip(waits, values):
                if not isinstance(v, int) or v > 0:
                    eng.wait_ge(semaphore, v)

        def arrived(e, i, count):
            return count * (e // 2 + 1) if isinstance(e, int) else (e - i) * (count // 2) + count

        def no(t, value):
            return isinstance(t, int) and t == value

        @block.sync
        def _(sp):
            n_rows = 0

            def row(name, r0, n=1, k=P, at_col=0):
                nonlocal n_rows
                src = a[name]
                src = at(src, src.offset, [[k, n], [1, k]])
                sp.dma_start(rows[r0:r0 + n, at_col:at_col + k], src).then_inc(rows_in, 16)
                n_rows += 1

            row("L0_cond_g_norm", C_GN0)
            row("L1_cond_g_in", C_GIN1)
            row("L0_ffn_ln1_g", C_LN1G)
            row("L0_ffn_ln1_b", C_LN1B)
            row("L0_ffn_ln2_g", C_LN2G, 4)
            row("L0_ffn_ln2_b", C_LN2B, 4)
            row("L1_ffn_b1", C_MB1, 32)
            for d in range(2):
                c = a["cond_64"]
                sp.dma_start(rows[C_VN:C_VN + 1, d * DH:(d + 1) * DH], c[1:2, :]).then_inc(rows_in, 16)
                sp.dma_start(rows[C_NK:C_NK + 1, d * DH:(d + 1) * DH], c[0:1, :]).then_inc(rows_in, 16)
                row("L0_cond_q_scale", C_QS, 1, DH, d * DH)
                row("L0_cond_k_scale", C_KS, 1, DH, d * DH)
            assert n_rows + 4 == ROWS_DMAS

            sp.dma_start(X[:], a["x"].rearrange("b n d -> n b d")).then_inc(x_in, 16)

            def spread(dst, name, k, offset=0):
                src = a[name]
                sp.dma_start(dst, at(src, src.offset + offset, [[0, P], [1, k]])).then_inc(bcast_in, 16)

            for i, name in enumerate(("L0_cond_w0", "L0_cond_b0", "L0_cond_g0", "L0_cond_b1",
                                      "L0_cond_g1")):
                spread(rel_rows[:, i, :], name, P)
            spread(kqs[:], "L0_cond_k_scale", DH)
            spread(qs_row[:], "L0_cond_q_scale", DH)
            spread(nk_row[:], "cond_64", DH)
            spread(vnull[:], "cond_64", DH, DH)
            spread(fb1[:], "L0_ffn_b1", HIDDEN)
            spread(fb2[:], "L0_ffn_b2", P)
            spread(g_out[0][:], "L0_cond_g_out", P)
            spread(g_out[1][:], "L1_cond_g_out", P)
            spread(gate_b[:], "L1_ffn_gate_b", EXPERTS)
            spread(mb2[:].rearrange("p e d -> p (e d)"), "L1_ffn_b2", EXPERTS * P)
            sp.dma_start(rel_w1[:], a["L0_cond_w1"]).then_inc(bcast_in, 16)
            sp.dma_start(rel_w2[:], a["L0_cond_w2"]).then_inc(bcast_in, 16)
            sp.dma_start(rel_b2[:], at(a["L0_cond_b2"], 0, [[1, HEADS], [1, 1]])).then_inc(bcast_in, 16)
            sp.dma_start(gate_rows[:], a["L1_ffn_gate_w"]).then_inc(bcast_in, 16)
            for layer, name in enumerate(("mask_BxS_bf1", "mask_BxS_bk0")):
                sp.dma_start(mask_u8[layer][:].bitcast(U32),
                             at(a[name], 0, [[0, P], [1, NB * P // 4]])).then_inc(bcast_in, 16)
            for layer in range(2):
                src = a[f"L{layer}_cond_null_attn_bias"]
                for m in range(4):
                    sp.dma_start(nullb[layer][QB * m:QB * (m + 1), :].rearrange("p (h e) -> p h e", e=2),
                                 at(src, 2 * m, [[0, QB], [8, 2], [1, 2]])).then_inc(bcast_in, 16)
            assert BCAST_DMAS == 5 + 10 + 4 + 2 + 8

            sp.dma_start(w1_raw[:], a["L0_ffn_w1"].rearrange("(j p) d -> p j d", p=P)).then_inc(ffnw_in, 16)
            sp.dma_start(w2_raw[:], a["L0_ffn_w2"].rearrange("p (j h) -> p j h", j=FB)).then_inc(ffnw_in, 16)
            for layer in range(2):
                wo = a["L0_cond_Wout" if layer == 0 else "L1_cond_Wo"]
                sp.dma_start(Wq[layer][:], a[f"L{layer}_cond_Wq"]).then_inc(attw_in, 16)
                sp.dma_start(Wkv[layer][:], a[f"L{layer}_cond_Wkv"]).then_inc(attw_in, 16)
                sp.dma_start(Wo[layer][:], wo.rearrange("(j p) d -> p j d", p=P)).then_inc(attw_in, 16)
            fs = a["fside_16xSxS_0"]
            for u in range(UNITS):
                for m in range(4):
                    for hh in range(2):
                        sp.dma_start(unit_bias(1, u)[QB * m:QB * (m + 1), hh, :, 1:WIDTH[u]],
                                     at(fs, ((8 * hh + 2 * m) * P + QB * u) * P,
                                        [[P, QB], [P * P, 2], [1, WIDTH[u] - 1]])).then_inc(table_in, 16)

            sp.wait_ge(rel_out, 1)
            sp.dma_start(rel_d, rel_tab[:].unsqueeze(1).broadcast_to([HEADS, QB, 2 * P])).then_inc(rel_out, 16)
            sp.wait_ge(rel_out, 17)
            for u in range(UNITS):
                for m in range(4):
                    for hh in range(2):
                        sp.dma_start(unit_bias(0, u)[QB * m:QB * (m + 1), hh, :, 1:WIDTH[u]],
                                     at(rel_d, (8 * hh + 2 * m) * QB * 2 * P + P - 1 - QB * u,
                                        [[2 * P - 1, QB], [QB * 2 * P, 2], [1, WIDTH[u] - 1]])).then_inc(
                                            rel_in, 16)

            sp.wait_ge(scratch_out, 1)
            for c in range(TOPK):
                for t, k in enumerate(TILE_ROWS):
                    sp.dma_start(at(slot_d[c], t * P * ROW, [[ROW, k], [CAP * ROW, EXPERTS], [1, ROW]]),
                                 empty[0:k, :].unsqueeze(1).broadcast_to([k, EXPERTS, ROW])).then_inc(
                                     scratch_out, 16)
                for r in range(0, NB, 4):
                    sp.dma_start(at(back_d[c], r * P * P, [[P, P], [P * P, 4], [1, P]]),
                                 zero_row[:]).then_inc(scratch_out, 16)

            def load_expert(e, i):
                sp.dma_start(eW1[i][:], a["L1_ffn_W1"][e]).then_inc(s[f"e_w{i}"], 16)
                sp.dma_start(eW2[i][:], a["L1_ffn_W2"][e].rearrange("(j p) d -> p j d", p=P)).then_inc(
                    s[f"e_w{i}"], 16)

            def load_slots(e, i):
                for c in range(TOPK):
                    src = slot_d[c][bass.ds(e * CAP, 2 * P), :].rearrange("(t p) r -> p t r", p=P)
                    sp.dma_start(xb[i][:, c, 0:2, :], src).then_inc(s[f"e_x{i}"], 16)
                    sp.dma_start(xb[i][0:TILE_ROWS[2], c, 2, :],
                                 slot_d[c][bass.ds(e * CAP + 2 * P, TILE_ROWS[2]), :]).then_inc(s[f"e_x{i}"], 16)

            load_expert(0, 0)
            load_expert(1, 1)
            for c in range(TOPK):
                sp.wait_ge(s[f"slots_out{c}"], 16 * NB)
            load_slots(0, 0)
            load_slots(1, 1)
            with sp.Fori(0, EXPERTS // 2 - 1) as k:
                for i in range(2):
                    e = 2 * k + i
                    sp.wait_ge(s["e_T_psum"], e + 1)
                    sp.wait_ge(s["e_tags"], 2 * e + 2)
                    load_slots(e + 2, i)
                    sp.wait_ge(s["e_y_psum"], 2 * e + 2)
                    load_expert(e + 2, i)
            for c in range(TOPK):
                sp.wait_ge(s[f"e_sent{c}"], 16 * TILES * EXPERTS)
            for q in range(4):
                for c in range(TOPK):
                    src = at(back_d[c], 4 * q * P * P, [[P, P], [P * P, 4], [1, P]])
                    sp.dma_start(back[:, c, 4 * q:4 * q + 4, :], src).then_inc(s["back_in"], 16)
                sp.wait_ge(s["back_in"], 32 * (q + 1))
                sp.sem_inc(s["back_ready"], 1)
            out_v = out.rearrange("b n d -> n b d")
            for q in range(4):
                sp.wait_ge(s["z_step"], 2 * (q + 1))
                sp.dma_start(out_v[:, 4 * q:4 * q + 4, :], X[:, 4 * q:4 * q + 4, :]).then_inc(
                    s["final_out"], 16)
            sp.wait_ge(s["final_out"], 64)

        @block.gpsimd
        def _(pool):
            pool.memset(ident[:], 0.0).then_inc(const_done, 1)
            pool.memset(ones[:], 1.0).then_inc(const_done, 1)
            pool.memset(ones_bf[:], 1.0).then_inc(const_done, 1)
            pool.memset(half[:], -0.5).then_inc(const_done, 1)
            pool.memset(rel_tab[:], FAR).then_inc(const_done, 1)
            pool.memset(kk[0][:], 0.0).then_inc(const_done, 1)
            pool.memset(kk[1][:], 0.0).then_inc(const_done, 1)
            pool.memset(mask[0][:], 0.0).then_inc(const_done, 1)
            pool.memset(mask[1][:], 0.0).then_inc(const_done, 1)
            pool.memset(empty[:], 0.0).then_inc(const_done, 1)
            pool.memset(zero_row[:], 0.0).then_inc(const_done, 1)
            pool.wait_ge(const_done, 11)
            pool.affine_select(ident[:], ident[:], pattern=[[-1, P]], compare_op=ALU.not_equal, fill=1.0,
                               base=0, channel_multiplier=1).then_inc(const_done, 1)
            pool.affine_select(before_bf[:], ones_bf[:], pattern=[[1, P]], compare_op=ALU.is_gt, fill=0.0,
                               base=0, channel_multiplier=-1).then_inc(const_done, 1)
            pool.iota(pos_i[:], pattern=[[0, 1]], base=P - 1, channel_multiplier=-1).then_inc(const_done, 1)
            pool.iota(io_i[:], pattern=[[1, EXPERTS]], base=0, channel_multiplier=0).then_inc(const_done, 1)
            pool.iota(trash_i[:], pattern=[[0, 1]], base=SLOTS, channel_multiplier=1).then_inc(const_done, 1)
            pool.iota(tok_i[:], pattern=[[P, NB]], base=0, channel_multiplier=1).then_inc(const_done, 1)
            pool.iota(ept[:], pattern=[[0, 1]], base=NB * P, channel_multiplier=1).then_inc(const_done, 1)
            pool.wait_ge(const_done, CONSTS)
            pool.tensor_copy(empty[:, P:P + 1].bitcast(I32), ept[:]).then_inc(scratch_out, 1)

            def rsqrt(dst, src, k, done, count=1):
                pool.tensor_tensor(dst, src, half[:, 0:k], ALU.pow).then_inc(done, count)

            for n, (dst, src) in enumerate(((small[:, 1:2], small[:, 0:1]), (small[:, 3:4], small[:, 2:3]),
                                            (small[:, 5:6], small[:, 4:5]))):
                pool.wait_ge(s["ln_var"], n + 1)
                rsqrt(dst, src, 1, s["ln_rstd"])
            pool.wait_ge(table_in, 16 * 32)
            pool.wait_ge(s["ln_rstd"], 3)
            for u in range(UNITS):
                for m in range(4):
                    if 4 * u + m:
                        pool.wait_ge(pool_step, 4 * u + m)
                    v = unit_bias(1, u)[QB * m:QB * (m + 1)].rearrange("p h e k -> p (h e) k")[:, :, 1:WIDTH[u]]
                    pool.affine_select(v, v, pattern=[[0, 4], [-1, WIDTH[u] - 1]], compare_op=ALU.is_ge,
                                       fill=FAR, base=QB * u, channel_multiplier=1).then_inc(pool_step, 1)

            lns = 3

            pool.wait_ge(pool_step, 16)

            def bulk_rstd(n):
                pool.wait_ge(s["ln_var"], n + 1)
                rsqrt(rstd[:], ve[:], NB, s["ln_rstd"])

            def q_norm(b):
                for h, (lo, hi) in enumerate(((0, 9), (9, HEADS + 1))):
                    pool.wait_ge(s["ss_step"], 4 * b + 2 * h + 2)
                    rsqrt(qrn[:, lo:hi], qssc[:, lo:hi], hi - lo, s["rn_ready"])

            def values_set(layer, b, i):
                B = b + NB * layer
                pool.wait_ge(s["v_read"], B + 1)
                held(pool, s["out_psum"], 4 * B - 4)
                pool.tensor_tensor(vp[i][:], vs[:], vnull[:], ALU.subtract).then_inc(s["v_ready"], 1)

            def mask_bias(layer, b, u, i):
                n = 4 * (b + NB * layer) + u
                apart(pool, (s["scores_ready"], n - 7))
                k = WIDTH[u]
                pool.tensor_tensor(unit_masked(i, u).rearrange("p h e k -> p (h e) k"),
                                   unit_bias(layer, u).rearrange("p h e k -> p (h e) k"),
                                   mask[layer][:, bass.ds(b, 1), 0:k].broadcast_to([P, 4, k]),
                                   ALU.add).then_inc(s["bias_ready"], 1)

            def attention(layer):
                def batch(b, i):
                    if not no(b, NB - 1):
                        mask_bias(layer, b + 1, 0, 1 - i)
                        if layer == 0:
                            q_norm(b + 1)
                        for u in range(1, UNITS):
                            mask_bias(layer, b + 1, u, 1 - i)
                        values_set(layer, b + 1, 1 - i)

                if layer == 0:
                    pool.wait_ge(rel_in, 16 * 32)
                    pool.wait_ge(s["setup_read"], 1)
                for u in range(UNITS):
                    mask_bias(layer, 0, u, 0)
                if layer == 0:
                    q_norm(0)
                values_set(layer, 0, 0)
                over(pool, NB, batch)

            bulk_rstd(lns)
            attention(0)
            bulk_rstd(lns + 1)
            bulk_rstd(lns + 2)

            def f_norm(t, i):
                pool.wait_ge(s["f_var"], t + 1)
                rsqrt(zrstd[:, i:i + 1], zve[:, i:i + 1], 1, s["f_rstd"])

            over(pool, NB, f_norm)
            bulk_rstd(lns + 3)
            attention(1)
            bulk_rstd(lns + 4)

            pool.wait_ge(s["normed"], 2)
            pool.tensor_copy(pay[:, :, 0:P], Y[:]).then_inc(s["r_pool"], 1)
            pool.tensor_copy(pay[:, :, P:P + 1].bitcast(I32), tok_i[:].unsqueeze(2)).then_inc(s["r_pool"], 1)
            pool.memset(pay[:, :, P + 3:ROW], 0.0).then_inc(s["r_pool"], 1)
            pool.wait_ge(s["r_pool"], 3)
            pool.wait_ge(s["r_pay"], 2)
            pool.wait_ge(scratch_out, SCRATCH_ALL)
            for t in range(NB):
                for c in range(TOPK):
                    if t:
                        pool.wait_ge(s[f"slots_out{c}"], 16 * t)
                    pool.indirect_dma_start(slot_d[c], bass.IndirectOffsetOnAxis(dest_u[:, t, c:c + 1], 0),
                                            pay[:, t, :], None).then_inc(s[f"slots_out{c}"], 16)

            def send(e, i):
                for t, k in enumerate(TILE_ROWS):
                    for c in range(TOPK):
                        apart(pool, (s[f"e_y{c}"], TILES * e + t + 1),
                              (s[f"e_sent{c}"], 16 * (TILES * e + t)))
                        pool.indirect_dma_start(back_d[c], bass.IndirectOffsetOnAxis(
                            tags[i][0:k, c, t, 0:1].bitcast(U32), 0), yb[i][0:k, c, t, :],
                            None).then_inc(s[f"e_sent{c}"], 16)

            over(pool, EXPERTS, send)

        @block.tensor
        def _(pe):
            pe.wait_ge(const_done, CONSTS)
            pe.wait_ge(rows_in, 16 * ROWS_DMAS)
            pe.transpose(psA[:, 0:N_ROWS], rows[0:N_ROWS, :], ident[0:N_ROWS, 0:N_ROWS]).then_inc(s["cols_psum"], 1)
            pe.wait_ge(bcast_in, 16 * BCAST_DMAS)
            pe.transpose(psA[:, 64:64 + EXPERTS], gate_rows[:], ident[0:EXPERTS, 0:EXPERTS]).then_inc(s["cols_psum"], 1)
            pe.wait_ge(s["wabs_ready"], 2)
            pe.matmul(psO[:, 0:2], ones[:], wabs[:], start=True, stop=True).then_inc(s["cols_psum"], 1)
            pe.wait_ge(s["rel_s_ready"], 1)
            pe.transpose(psQ[:, 0, 0:P], rel_s[:], ident[:]).then_inc(s["rel_psum"], 1)
            pe.wait_ge(s["rel_T_ready"], 1)
            pe.matmul(psQ[:, 0, P:2 * P], rel_T[:], rel_w1[:], start=True, stop=True).then_inc(s["rel_psum"], 1)
            pe.wait_ge(s["rel_s_ready"], 2)
            pe.transpose(psQ[:, 0, 2 * P:3 * P], rel_s[:], ident[:]).then_inc(s["rel_psum"], 1)
            pe.wait_ge(s["rel_T_ready"], 2)
            pe.matmul(psQ[0:HEADS, 0, 3 * P:4 * P], rel_w2[:], rel_T[:], start=True, stop=True).then_inc(
                s["rel_psum"], 1)
            pe.wait_ge(s["tern_ready"], 2)
            for i in range(2):
                for j in range(FB):
                    m = pe.transpose(psT[:, i, j * P:(j + 1) * P], tern[:, i, j * P:(j + 1) * P], ident[:])
            m.then_inc(s["ternT_psum"], 1)
            pe.wait_ge(s["setup_read"], 1)
            pe.wait_ge(s["ffnw_ready"], 2)

            def turn_input(layer, b, i):
                B = b + NB * layer
                pe.wait_ge(s["xn_ready"], B + 1)
                held(pe, s["y_done"], B - 3)
                held(pe, s["kk_ready"], B)
                held(pe, s["v_read"], B)
                pe.transpose(psA[:, 0:P], xn[:, i, :], ident[:]).then_inc(s["xnT_psum"], 1)

            def project_in(layer, b, i):
                B = b + NB * layer
                pe.wait_ge(s["xnT_ready"], B + 1)
                held(pe, s["q_ready"], B)
                pe.matmul(psA[:, P:2 * P], xnT[i][:], Wkv[layer][:], start=True, stop=True).then_inc(s["kv_psum"], 1)
                if layer == 0:
                    for h in range(2):
                        pe.matmul(psQ[:, h, :], xnT[i][:], Wq[0][:, 512 * h:512 * (h + 1)],
                                  start=True, stop=True).then_inc(s["q_psum"], 1)
                else:
                    for h in range(2):
                        for j in range(4):
                            m = pe.matmul(psQ[:, h, j * P:(j + 1) * P], Wq[1][:, (4 * h + j) * P:(4 * h + j + 1) * P],
                                          xnT[i][:], start=True, stop=True)
                        m.then_inc(s["q_psum"], 1)

            def turn_keys(layer, b, i):
                B = b + NB * layer
                pe.wait_ge(s["k_ready"], B + 1)
                pe.transpose(psA[:, 2 * P:3 * P], kd[i][:].rearrange("p a d -> p (a d)"), ident[:]).then_inc(
                    s["kT_psum"], 1)

            def turn_queries(b):
                for h in range(2):
                    pe.wait_ge(s["qn_ready"], 2 * b + h + 1)
                    for j in range(4):
                        m = pe.transpose(psQ[:, h, j * P:(j + 1) * P], qn[:, (4 * h + j) * P:(4 * h + j + 1) * P],
                                         ident[:])
                    m.then_inc(s["qT_psum"], 1)

            def scores(layer, b, u, i):
                B = b + NB * layer
                n = 4 * B + u
                w = WIDTH[u]
                if no(b, 0) and u == 0:
                    pe.wait_ge(s["kk_null"], 4 * (layer + 1))
                apart(pe, *([(s["kk_ready"], B + 1), (s["q_ready"], B + 1)] if u == 0 else []),
                      (s["scores_ready"], n))
                for h in range(2):
                    m = pe.matmul(psS[:, h, 0:2 * w], qT[i][:, h, u].rearrange("p m q -> p (m q)"),
                                  kk[i][:, :, 0:w], start=True, stop=True)
                m.then_inc(s["scores_psum"], 1)

            def turn_probs(n, u):
                apart(pe, (s["probs_ready"], n + 1), (s["probsT_ready"], n - 1))
                k = WIDTH[u] - 1
                for g in range(4):
                    m = pe.transpose(psT[0:k, u % 2, g * P:(g + 1) * P], pn[u % 2][:, g, 0:k], ident[:])
                m.then_inc(s["probsT_psum"], 1)

            def values(n, u, i, B=None):
                apart(pe, (s["probsT_ready"], n + 1), (s["out_ready"], n),
                      *([(s["v_ready"], B + 1)] if u == 0 else []))
                k = WIDTH[u] - 1
                for e in range(2):
                    m = pe.matmul(psO[DH * e:DH * (e + 1), 0:256], vp[i][0:k, :], PT[u % 2][0:k, :, e, :],
                                  start=True, stop=True)
                m.then_inc(s["out_psum"], 1)

            def project(layer, b, i, loading):
                B = b + NB * layer
                pe.wait_ge(s["out_ready"], 4 * B + 4)
                entry = B + 3 if loading else NB * (layer + 1) - 1
                pe.wait_ge(s["v_read"], entry + 1)
                if layer == 0 and loading:
                    pe.wait_ge(s["sq_ready"], 2 * entry + 1)
                else:
                    pe.wait_ge(s["kk_ready"], entry + 1)
                held(pe, s["y_done"], B)
                for j in range(8):
                    m = pe.matmul(psA[:, 3 * P:4 * P], OT[i][:, j].rearrange("p u q -> p (u q)"), Wo[layer][:, j, :],
                                  start=(j == 0), stop=(j == 7))
                m.then_inc(s["y_psum"], 1)

            def attention(layer):
                def batch(b, i):
                    n = 4 * (b + NB * layer)
                    first, last = no(b, 0), no(b, NB - 1)

                    def earlier(u, lag):
                        return not (first and u < lag)

                    for u in range(UNITS):
                        scores(layer, b, u, i)
                        if u == 0 and not last:
                            turn_input(layer, b + 1, 1 - i)
                        if earlier(u, 2):
                            turn_probs(n + u - 2, (u - 2) % UNITS)
                        if u == 0 and not last:
                            project_in(layer, b + 1, 1 - i)
                        if layer == 0 and u == 3 and not last:
                            turn_keys(layer, b + 1, 1 - i)
                            turn_queries(b + 1)
                        if earlier(u, 3):
                            values(n + u - 3, (u - 3) % UNITS, i if u == 3 else 1 - i, b + NB * layer)
                        if layer == 1 and u == 1 and not last:
                            turn_keys(layer, b + 1, 1 - i)
                        if u == 1 + layer and not first and not no(b, 1):
                            project(layer, b - 2, i, not last)

                if layer == 0:
                    pe.wait_ge(attw_in, 16 * 6)
                turn_input(layer, 0, 0)
                project_in(layer, 0, 0)
                turn_keys(layer, 0, 0)
                if layer == 0:
                    turn_queries(0)
                over(pe, NB, batch)
                N = 4 * (NB + NB * layer)
                project(layer, NB - 2, 0, False)
                turn_probs(N - 2, 2)
                values(N - 3, 1, 1)
                turn_probs(N - 1, 3)
                values(N - 2, 2, 1)
                values(N - 1, 3, 1)
                project(layer, NB - 1, 1, False)

            attention(0)

            def f_up(t, i):
                pe.wait_ge(s["f_h"], t + 1)
                held(pe, s["f_hT"], t)
                pe.transpose(psA[:, 0:P], xn[:, i, :], ident[:]).then_inc(s["f_h_psum"], 1)
                pe.wait_ge(s["f_hT"], t + 1)
                held(pe, s["f_z_ready"], t - 1)
                pe.matmul(psQ[:, i, :], hT[i][:], w1T[:], start=True, stop=True).then_inc(s["f_z_psum"], 1)

            def f_down(t, i):
                pe.wait_ge(s["f_gn"], t + 1)
                held(pe, s["f_gnT"], t - 1)
                for j in range(FB):
                    m = pe.transpose(psT[:, i, j * P:(j + 1) * P], gn[:, i, j * P:(j + 1) * P], ident[:])
                m.then_inc(s["f_gnT_psum"], 1)
                pe.wait_ge(s["f_gnT"], t + 1)
                held(pe, s["f_o_step"], 2 * t - 1)
                for j in range(FB):
                    m = pe.matmul(psO[:, 0:P], gnT[i][:, j, :], w2T[:, j, :], start=(j == 0),
                                  stop=(j == FB - 1))
                m.then_inc(s["f_o_psum"], 1)

            def ffn(t, i):
                if not no(t, NB - 1):
                    f_up(t + 1, 1 - i)
                f_down(t, i)

            f_up(0, 0)
            over(pe, NB, ffn)

            attention(1)

            def gate(t, i):
                pe.wait_ge(s["r_x"], t + 1)
                held(pe, s["r_T"], t)
                pe.transpose(psA[:, 0:P], xn[:, i, :], ident[:]).then_inc(s["r_T_psum"], 1)
                pe.wait_ge(s["r_T"], t + 1)
                pe.matmul(psQ[:, 0, bass.ts(t, EXPERTS)], hT[i][:], gateT[:], start=True, stop=True).then_inc(
                    s["r_lg_psum"], 1)

            over(pe, NB, gate)
            pe.wait_ge(s["r_oh"], 1)
            flat = oh_bf[:].rearrange("p t c e -> p (t c e)")
            pe.matmul(psQ[:, 1, 0:256], before_bf[:], flat, start=True, stop=True)
            pe.matmul(psQ[:, 1, 256:512], ones_bf[:], flat, start=True, stop=True).then_inc(s["r_pos_psum"], 1)
            pe.wait_ge(s["r_pos_read"], 1)

            def turn_rows(e, i):
                pe.wait_ge(s[f"e_x{i}"], arrived(e, i, 64))
                held(pe, s["e_T"], 2 * e)
                for c in range(TOPK):
                    for t, k in enumerate(TILE_ROWS):
                        m = pe.transpose(psT[:, c, t * P:t * P + k], xb[i][0:k, c, t, 0:P], ident[0:k, 0:k])
                m.then_inc(s["e_T_psum"], 1)

            def expert(e, i):
                pe.wait_ge(s[f"e_w{i}"], arrived(e, i, 32))
                pe.wait_ge(s["e_T"], 2 * e + 2)
                for j in range(FB):
                    for h in range(2):
                        held(pe, s["e_h_act" if h == 0 else "e_h_dve"], 4 * e + j - 1)
                        pe.matmul(psH[j % 2][h][:, 0:CAP], eW1[i][:, j * P:(j + 1) * P], xbT[:, h * CAP:(h + 1) * CAP],
                                  start=True, stop=True).then_inc(s["e_h_psum"], 1)
                if not no(e, EXPERTS - 1):
                    turn_rows(e + 1, 1 - i)
                pe.wait_ge(s["e_h_act"], 4 * e + 4)
                pe.wait_ge(s["e_h_dve"], 4 * e + 4)
                for c in range(TOPK):
                    held(pe, s["e_y_add"], 4 * e - 2 + 2 * c)
                    for t, k in enumerate(TILE_ROWS):
                        at_row = c * CAP + t * P
                        for j in range(FB):
                            m = pe.matmul(psS[0:k, c, t * P:(t + 1) * P], hm[:, j, at_row:at_row + k],
                                          eW2[i][:, j, :], start=(j == 0), stop=(j == FB - 1))
                    m.then_inc(s["e_y_psum"], 1)

            turn_rows(0, 0)
            over(pe, EXPERTS, expert)

        @block.scalar
        def _(act):
            act.wait_ge(ffnw_in, 32)
            for i, w in enumerate((w1_raw, w2_raw)):
                act.activation(tern[:, i, :], w[:].rearrange("p j d -> p (j d)"), ACT.Abs,
                               accum_out=wabs[:, i:i + 1]).then_inc(s["wabs_ready"], 1)
            for n in range(2):
                act.wait_ge(s["rel_n_ready"], n + 1)
                act.activation(rel_s[:], rel_n[:], ACT.Silu).then_inc(s["rel_s_ready"], 1)
            act.wait_ge(s["ternT_psum"], 1)
            act.copy(w1T[:], psT[:, 0, :]).then_inc(s["ffnw_ready"], 1)
            act.copy(w2T[:].rearrange("p j d -> p (j d)"), psT[:, 1, :]).then_inc(s["ffnw_ready"], 1)

            def input_T(layer, b, i):
                B = b + NB * layer
                act.wait_ge(s["xnT_psum"], B + 1)
                held(act, s["q_psum"], 2 * B - 2)
                c = C_GN0 if layer == 0 else C_GIN1
                act.activation(xnT[i][:], psA[:, 0:P], ACT.Copy, scale=cols[:, c:c + 1]).then_inc(
                    s["xnT_ready"], 1)

            def squares(b):
                act.wait_ge(s["kv_psum"], b + 1)
                held(act, s["ss_step"], 4 * b)
                act.activation(qsq[:, 0, :], psA[:, P:P + DH], ACT.Square)
                for h in range(2):
                    act.wait_ge(s["q_psum"], 2 * b + h + 1)
                    act.activation(qsq[:, 1 + 8 * h:9 + 8 * h, :], psQ[:, h, :].rearrange("p (h d) -> p h d", d=DH),
                                   ACT.Square).then_inc(s["sq_ready"], 1)

            def queries(layer, b, i):
                B = b + NB * layer
                held(act, s["scores_psum"], 4 * B - 4)
                for h in range(2):
                    if layer == 0:
                        act.wait_ge(s["qT_psum"], 2 * b + h + 1)
                    else:
                        act.wait_ge(s["q_psum"], 2 * B + h + 1)
                    m = act.activation(qT[i][:, h].rearrange("p u m q -> p m u q"),
                                       psQ[:, h, :].rearrange("p (m u q) -> p m u q", u=UNITS, q=QB), ACT.Copy,
                                       scale=1.0 if layer == 0 else DH ** -0.5)
                m.then_inc(s["q_ready"], 1)

            def keys_T(layer, b, i):
                B = b + NB * layer
                act.wait_ge(s["kT_psum"], B + 1)
                held(act, s["scores_psum"], 4 * B - 4)
                act.copy(kk[i][0:DH, 0, 1:P + 1], psA[0:DH, 2 * P:3 * P])
                act.copy(kk[i][DH:P, 1, 1:P + 1], psA[DH:P, 2 * P:3 * P]).then_inc(s["kk_ready"], 1)

            def weights(n, u):
                act.wait_ge(s["negmax_ready"], n + 1)
                for g in range(4):
                    v = sc[u][:, g // 2, g % 2, :]
                    m = act.activation(v, v, ACT.Exp, bias=negmax[:, u, g:g + 1], accum_out=psum_row[:, u, g:g + 1])
                m.then_inc(s["exp_done"], 1)

            def weights_T(n, u):
                act.wait_ge(s["probsT_psum"], n + 1)
                held(act, s["out_psum"], n - 1)
                k = WIDTH[u] - 1
                act.copy(PT[u % 2][0:k].rearrange("p h e q -> p (h e q)"), psT[0:k, u % 2, :]).then_inc(
                    s["probsT_ready"], 1)

            def attention(layer):
                def batch(b, i):
                    n = 4 * (b + NB * layer)
                    first, last = no(b, 0), no(b, NB - 1)
                    for u in range(UNITS):
                        if u == 0 and not last:
                            input_T(layer, b + 1, 1 - i)
                        if not (first and u < 2):
                            weights_T(n + u - 2, (u - 2) % UNITS)
                        if layer == 0 and u == 3 and not last:
                            keys_T(layer, b + 1, 1 - i)
                            queries(layer, b + 1, 1 - i)
                        weights(n + u, u)
                        if layer == 0 and u == 0 and not last:
                            squares(b + 1)
                        if layer == 1 and u == 1 and not last:
                            queries(layer, b + 1, 1 - i)
                        if layer == 1 and u == 1 and not last:
                            keys_T(layer, b + 1, 1 - i)

                if layer == 0:
                    act.wait_ge(s["cols_ready"], 1)
                input_T(layer, 0, 0)
                if layer == 0:
                    squares(0)
                keys_T(layer, 0, 0)
                queries(layer, 0, 0)
                over(act, NB, batch)
                N = 4 * (NB + NB * layer)
                weights_T(N - 2, 2)
                weights_T(N - 1, 3)

            attention(0)

            def f_in(t, i):
                act.wait_ge(s["f_h_psum"], t + 1)
                held(act, s["f_z_psum"], t - 1)
                act.activation(hT[i][:], psA[:, 0:P], ACT.Identity, scale=cols[:, C_LN1G:C_LN1G + 1],
                               bias=cols[:, C_LN1B:C_LN1B + 1]).then_inc(s["f_hT"], 1)

            def f_mid(t, i):
                act.wait_ge(s["f_gnT_psum"], t + 1)
                held(act, s["f_o_psum"], t - 1)
                for j in range(FB):
                    m = act.activation(gnT[i][:, j, :], psT[:, i, j * P:(j + 1) * P], ACT.Identity,
                                       scale=cols[:, C_LN2G + j:C_LN2G + j + 1],
                                       bias=cols[:, C_LN2B + j:C_LN2B + j + 1])
                m.then_inc(s["f_gnT"], 1)

            def f_gelu(t, i):
                act.wait_ge(s["f_z_ready"], t + 1)
                act.activation(z[:, i, :], z[:, i, :], ACT.Gelu).then_inc(s["f_gelu"], 1)

            def ffn(t, i):
                if not no(t, NB - 1):
                    f_in(t + 1, 1 - i)
                f_mid(t, i)
                if not no(t, NB - 1):
                    f_gelu(t + 1, 1 - i)

            f_in(0, 0)
            f_gelu(0, 0)
            over(act, NB, ffn)

            attention(1)

            def gate(t, i):
                act.wait_ge(s["r_T_psum"], t + 1)
                held(act, s["r_lg_psum"], t - 1)
                act.copy(hT[i][:], psA[:, 0:P]).then_inc(s["r_T"], 1)

            over(act, NB, gate)
            act.wait_ge(s["r_step"], 3)
            act.activation(le[:], le[:], ACT.Exp).then_inc(s["r_exp"], 1)

            def rows_T(e):
                act.wait_ge(s["e_T_psum"], e + 1)
                held(act, s["e_h_psum"], 8 * e)
                for c in range(TOPK):
                    act.copy(xbT[:, c * CAP:(c + 1) * CAP], psT[:, c, 0:CAP]).then_inc(s["e_T"], 1)

            def expert(e, i):
                held(act, s["e_y_psum"], TOPK * e)
                for j in range(FB):
                    act.wait_ge(s["e_h_psum"], 8 * e + 2 * j + 1)
                    act.activation(hm[:, j, 0:CAP], psH[j % 2][0][:, 0:CAP], ACT.Relu,
                                   bias=cols[:, bass.ds(4 * e + (C_MB1 + j), 1)]).then_inc(s["e_h_act"], 1)
                if not no(e, EXPERTS - 1):
                    rows_T(e + 1)
                for c in range(TOPK):
                    act.wait_ge(s["e_y_add"], 4 * e + 2 * c + 2)
                    for t, k in enumerate(TILE_ROWS):
                        act.activation(yb[i][0:k, c, t, :], yb[i][0:k, c, t, :], ACT.Copy,
                                       scale=tags[i][0:k, c, t, 1 + c:2 + c]).then_inc(s[f"e_y{c}"], 1)

            rows_T(0)
            over(act, EXPERTS, expert)

        @block.vector
        def _(dve):
            steps = 0

            def step(ins):
                nonlocal steps
                ins.then_inc(dve_step, 1)
                steps += 1
                dve.wait_ge(dve_step, steps)

            def norm_scale(dst, src, k, n, eps=LN_EPS):
                dve.tensor_scalar(dst, src, eps, None, ALU.add).then_inc(s["ln_var"], 1)
                dve.wait_ge(s["ln_rstd"], n)

            dve.wait_ge(const_done, CONSTS)
            step(dve.tensor_copy(pos_f[:], pos_i[:]))
            step(dve.tensor_copy(trash[:], trash_i[:]))
            step(dve.tensor_copy(io_f[:], io_i[:]))
            dve.wait_ge(bcast_in, 16 * BCAST_DMAS)

            def rel_norm(n, g):
                step(dve.bn_stats(stats[:, 0, :], rel_h[:]))
                step(dve.bn_aggr(mv[:, 0, :], stats[:, 0, :]))
                norm_scale(small[:, 2 * n:2 * n + 1], mv[:, 0, 1:2], 1, n + 1)
                step(dve.tensor_scalar(rel_n[:], rel_h[:], mv[:, 0, 0:1], small[:, 2 * n + 1:2 * n + 2],
                                       ALU.subtract, ALU.mult))
                dve.tensor_tensor(rel_n[:], rel_n[:], g, ALU.mult).then_inc(s["rel_n_ready"], 1)

            step(dve.scalar_tensor_tensor(rel_h[:], rel_rows[:, 0, :], pos_f[:], rel_rows[:, 1, :],
                                          ALU.mult, ALU.add))
            rel_norm(0, rel_rows[:, 2, :])
            dve.wait_ge(s["rel_psum"], 1)
            dve.tensor_copy(rel_T[:], psQ[:, 0, 0:P]).then_inc(s["rel_T_ready"], 1)
            dve.wait_ge(s["rel_psum"], 2)
            step(dve.tensor_tensor(rel_h[:], psQ[:, 0, P:2 * P], rel_rows[:, 3, :], ALU.add))
            rel_norm(1, rel_rows[:, 4, :])
            dve.wait_ge(s["rel_psum"], 3)
            dve.tensor_copy(rel_T[:], psQ[:, 0, 2 * P:3 * P]).then_inc(s["rel_T_ready"], 1)
            dve.wait_ge(s["rel_psum"], 4)
            step(dve.tensor_scalar(rel_tab[:, 0:P], psQ[0:HEADS, 0, 3 * P:4 * P], rel_b2[:], None, ALU.add))
            dve.tensor_copy(half[:, 18:19], half[:, 19:20]).then_inc(rel_out, 1)
            dve.wait_ge(s["cols_psum"], 2)
            step(dve.tensor_copy(gateT[:], psA[:, 64:64 + EXPERTS]))
            dve.tensor_copy(cols[:, 0:N_ROWS], psA[:, 0:N_ROWS]).then_inc(s["cols_ready"], 1)
            dve.wait_ge(s["cols_ready"], 1)
            step(dve.tensor_tensor(rel_h[:, 0:DH], nk_row[:], nk_row[:], ALU.mult))
            step(dve.tensor_reduce(small[:, 6:7], rel_h[:, 0:DH], X_AXIS, ALU.add))
            step(dve.tensor_scalar(small[:, 7:8], small[:, 6:7], 1e-24, None, ALU.max))
            norm_scale(small[:, 4:5], small[:, 7:8], 1, 3, 0.0)
            step(dve.tensor_tensor(nk0[:], cols[:, C_NK:C_NK + 1], small[:, 5:6], ALU.mult))
            step(dve.tensor_tensor(nk0[:], nk0[:], cols[:, C_QS:C_QS + 1], ALU.mult))
            step(dve.scalar_tensor_tensor(nk0[:], nk0[:], 8.0, cols[:, C_KS:C_KS + 1], ALU.mult, ALU.mult))

            def null_keys(column):
                for i in range(2):
                    for e in range(2):
                        half_of = slice(DH * e, DH * (e + 1))
                        dve.tensor_copy(kk[i][half_of, e, 0:1], column[half_of]).then_inc(s["kk_null"], 1)

            null_keys(nk0[:])
            step(dve.tensor_tensor(kqs[:], kqs[:], qs_row[:], ALU.mult))
            step(dve.tensor_scalar(kqs[:], kqs[:], 8.0, None, ALU.mult))
            for layer in range(2):
                step(dve.tensor_scalar(mask[layer][:, :, 1:P + 1],
                                       mask_u8[layer][:].rearrange("p (b k) -> p b k", k=P), -MASKED, MASKED,
                                       ALU.mult, ALU.add))
            dve.wait_ge(s["cols_psum"], 3)
            step(dve.tensor_scalar(wmean[:], psO[:, 0:2], 1.0 / (HIDDEN * P), 1e-5, ALU.mult, ALU.max))
            step(dve.reciprocal(wscale[:], wmean[:]))
            for i, w in enumerate((w1_raw, w2_raw)):
                flat_w = w[:].rearrange("p j d -> p (j d)")
                step(dve.tensor_scalar(tern[:, i, :], flat_w, wscale[:, i:i + 1], 0.5, ALU.mult, ALU.is_gt))
                step(dve.tensor_scalar(z[:, i, :], flat_w, wscale[:, i:i + 1], -0.5, ALU.mult, ALU.is_lt))
                dve.tensor_tensor(tern[:, i, :], tern[:, i, :], z[:, i, :], ALU.subtract).then_inc(
                    s["tern_ready"], 1)
            for layer in range(2):
                for u in range(UNITS):
                    ins = dve.tensor_copy(unit_bias(layer, u)[:, :, :, 0],
                                          nullb[layer][:].rearrange("p (h e) -> p h e", e=2))
            ins.then_inc(s["setup_read"], 1)

            def norm_stats(src, n):
                nonlocal steps
                with dve.Fori(0, NB) as t:
                    dve.bn_stats(stats[:, t, :], src[:, t, :]).then_inc(dve_step, 1)
                steps += NB
                dve.wait_ge(dve_step, steps)
                for t in range(NB):
                    ins = dve.bn_aggr(mv[:, t, :], stats[:, t, :])
                step(ins)
                norm_scale(ve[:], mv[:, :, 1], NB, n)

            def normed(t):
                return mv[:, t, 0:1], rstd[:, bass.ds(t, 1)]

            def norm_output(layer, n):
                nonlocal steps
                norm_stats(Y, n)
                with dve.Fori(0, NB) as t:
                    mean, r = normed(t)
                    dve.tensor_scalar(Y[:, t, :], Y[:, t, :], mean, r, ALU.subtract, ALU.mult).then_inc(
                        dve_step, 1)
                steps += NB
                dve.wait_ge(dve_step, steps)
                dve.tensor_tensor(Y[:], Y[:], g_out[layer][:].unsqueeze(1).broadcast_to([P, NB, P]),
                                  ALU.mult).then_inc(s["normed"], 1)
                dve.wait_ge(s["normed"], layer + 1)

            def input_norm(layer, b, i):
                B = b + NB * layer
                held(dve, s["xnT_psum"], B - 1)
                mean, r = normed(b)
                dve.tensor_scalar(xn[:, i, :], X[:, b, :], mean, r, ALU.subtract, ALU.mult).then_inc(
                    s["xn_ready"], 1)

            def values_in(layer, b, i):
                B = b + NB * layer
                dve.wait_ge(s["kv_psum"], B + 1)
                if layer == 0:
                    dve.wait_ge(s["sq_ready"], 2 * b + 1)
                held(dve, s["v_ready"], B)
                dve.tensor_copy(vs[:], psA[:, P + DH:2 * P]).then_inc(s["v_read"], 1)

            def keys_in(layer, b, i):
                B = b + NB * layer
                dve.wait_ge(s["kv_psum"], B + 1)
                if layer == 0:
                    dve.wait_ge(s["rn_ready"], 2 * b + 1)
                held(dve, s["kT_psum"], B - 1)
                k_raw = psA[:, P:P + DH].unsqueeze(1).broadcast_to([P, 2, DH])
                if layer == 0:
                    ins = dve.scalar_tensor_tensor(kd[i][:], k_raw, qrn[:, 0:1],
                                                   kqs[:].unsqueeze(1).broadcast_to([P, 2, DH]),
                                                   ALU.mult, ALU.mult)
                else:
                    ins = dve.tensor_copy(kd[i][:], k_raw)
                ins.then_inc(s["k_ready"], 1)

            def sum_squares(b, h):
                lo, hi = (0, 9) if h == 0 else (9, HEADS + 1)
                dve.wait_ge(s["sq_ready"], 2 * b + h + 1)
                dve.tensor_reduce(qss[:, lo:hi], qsq[:, lo:hi, :], X_AXIS, ALU.add).then_inc(s["ss_step"], 1)
                dve.wait_ge(s["ss_step"], 4 * b + 2 * h + 1)
                dve.tensor_scalar(qssc[:, lo:hi], qss[:, lo:hi], 1e-24, None, ALU.max).then_inc(s["ss_step"], 1)

            def queries_norm(b, h):
                dve.wait_ge(s["rn_ready"], 2 * b + h + 1)
                held(dve, s["qT_psum"], 2 * b + h - 1)
                dve.tensor_tensor(qn[:, 512 * h:512 * (h + 1)].rearrange("p (h d) -> p h d", d=DH),
                                  psQ[:, h, :].rearrange("p (h d) -> p h d", d=DH),
                                  qrn[:, 1 + 8 * h:9 + 8 * h].unsqueeze(2).broadcast_to([P, 8, DH]),
                                  ALU.mult).then_inc(s["qn_ready"], 1)

            def biased(n, u, i):
                held(dve, s["probs_ready"], n - 3)
                dve.wait_ge(s["bias_ready"], n + 1)
                dve.wait_ge(s["scores_psum"], n + 1)
                dve.tensor_tensor(sc[u][:], unit_psum(u), unit_masked(i, u), ALU.add).then_inc(s["scores_ready"], 1)
                dve.wait_ge(s["scores_ready"], n + 1)
                dve.tensor_reduce(negmax[:, u, :], sc[u][:].rearrange("p h e k -> p (h e) k"), X_AXIS,
                                  ALU.max, negate=True).then_inc(s["negmax_ready"], 1)

            def divide(n, u):
                dve.wait_ge(s["exp_done"], n + 1)
                dve.reciprocal(rsum[:, u, :], psum_row[:, u, :]).then_inc(s["rsum_ready"], 1)
                dve.wait_ge(s["rsum_ready"], n + 1)
                held(dve, s["probsT_psum"], n - 1)
                k = WIDTH[u] - 1
                dve.tensor_tensor(pn[u % 2][:, :, 0:k],
                                  sc[u][:].rearrange("p h e k -> p (h e) k")[:, :, 1:k + 1],
                                  rsum[:, u, :].unsqueeze(2).broadcast_to([P, 4, k]),
                                  ALU.mult).then_inc(s["probs_ready"], 1)

            def outputs(layer, n, b, u, i):
                B = b + NB * layer
                dve.wait_ge(s["out_psum"], n + 1)
                if u == 0:
                    held(dve, s["y_psum"], B - 1)
                dve.tensor_scalar(OT[i][:, :, u, :], psO[:, 0:256].rearrange("p (j q) -> p j q", q=QB),
                                  cols[:, C_VN:C_VN + 1], None, ALU.add).then_inc(s["out_ready"], 1)

            def project_out(layer, b):
                B = b + NB * layer
                dve.wait_ge(s["y_psum"], B + 1)
                dve.tensor_copy(Y[:, b, :], psA[:, 3 * P:4 * P]).then_inc(s["y_done"], 1)

            def attention(layer):
                def batch(b, i):
                    B = b + NB * layer
                    n = 4 * B
                    first, last = no(b, 0), no(b, NB - 1)
                    for u in range(UNITS):
                        if layer == 1 and u == 3 and not first and not no(b, 1):
                            project_out(layer, b - 2)
                        biased(n + u, u, i)
                        if layer == 0 and u == 1 and not last:
                            sum_squares(b + 1, 0)
                        if u == 1 and not last:
                            values_in(layer, b + 1, 1 - i)
                        if layer == 1 and u == 1 and not last:
                            keys_in(layer, b + 1, 1 - i)
                        if not (first and u < 1):
                            divide(n + u - 1, (u - 1) % UNITS)
                        if layer == 0 and u == 1 and not last:
                            sum_squares(b + 1, 1)
                        if layer == 0 and u == 2 and not first and not no(b, 1):
                            project_out(layer, b - 2)
                        if layer == 0 and u == 2 and not last:
                            keys_in(layer, b + 1, 1 - i)
                            queries_norm(b + 1, 0)
                            queries_norm(b + 1, 1)
                        if not (first and u < 3):
                            outputs(layer, n + u - 3, b if u == 3 else b - 1, (u - 3) % UNITS, i if u == 3 else 1 - i)
                        if u == 0 and not last and not no(b, NB - 2):
                            input_norm(layer, b + 2, i)

                input_norm(layer, 0, 0)
                input_norm(layer, 1, 1)
                values_in(layer, 0, 0)
                if layer == 0:
                    sum_squares(0, 0)
                    sum_squares(0, 1)
                    keys_in(layer, 0, 0)
                    queries_norm(0, 0)
                    queries_norm(0, 1)
                else:
                    keys_in(layer, 0, 0)
                over(dve, NB, batch)
                n = 4 * (NB + NB * layer)
                project_out(layer, NB - 2)
                divide(n - 1, 3)
                outputs(layer, n - 3, NB - 1, 1, 1)
                outputs(layer, n - 2, NB - 1, 2, 1)
                outputs(layer, n - 1, NB - 1, 3, 1)
                project_out(layer, NB - 1)
                dve.wait_ge(s["y_done"], NB * (layer + 1))

            dve.wait_ge(x_in, 16)
            norm_stats(X, 4)
            attention(0)

            norm_output(0, 5)
            norm_stats(Y, 6)

            def f_norm_in(t, i):
                held(dve, s["f_h_psum"], t - 1)
                mean, r = normed(t)
                dve.tensor_scalar(xn[:, i, :], Y[:, t, :], mean, r, ALU.subtract, ALU.mult).then_inc(s["f_h"], 1)

            def f_hidden(t, i):
                dve.wait_ge(s["f_z_psum"], t + 1)
                dve.scalar_tensor_tensor(z[:, i, :], psQ[:, i, :], wmean[:, 0:1], fb1[:], ALU.mult,
                                         ALU.add).then_inc(s["f_z_ready"], 1)

            def f_stats(t, i):
                dve.wait_ge(s["f_gelu"], t + 1)
                dve.bn_stats(zst[:, i, :], z[:, i, :]).then_inc(s["f_stat"], 1)
                apart(dve, (s["f_stat"], 2 * t + 1))
                dve.bn_aggr(zmv[:, i, :], zst[:, i, :]).then_inc(s["f_stat"], 1)
                dve.wait_ge(s["f_stat"], 2 * t + 2)
                dve.tensor_scalar(zve[:, i:i + 1], zmv[:, i, 1:2], LN_EPS, None, ALU.add).then_inc(s["f_var"], 1)

            def f_norm_mid(t, i):
                dve.wait_ge(s["f_rstd"], t + 1)
                held(dve, s["f_gnT_psum"], t - 1)
                dve.tensor_scalar(gn[:, i, :], z[:, i, :], zmv[:, i, 0:1], zrstd[:, i:i + 1], ALU.subtract,
                                  ALU.mult).then_inc(s["f_gn"], 1)

            def f_out(t):
                dve.wait_ge(s["f_o_psum"], t + 1)
                dve.scalar_tensor_tensor(ffo[:], psO[:, 0:P], wmean[:, 1:2], fb2[:], ALU.mult,
                                         ALU.add).then_inc(s["f_o_step"], 1)
                dve.wait_ge(s["f_o_step"], 2 * t + 1)
                dve.tensor_tensor(X[:, t, :], X[:, t, :], ffo[:], ALU.add).then_inc(s["f_o_step"], 1)

            def ffn(t, i):
                f_norm_mid(t, i)
                if not no(t, NB - 1) and not no(t, NB - 2):
                    f_norm_in(t + 2, i)
                if not no(t, NB - 1):
                    f_hidden(t + 1, 1 - i)
                f_out(t)
                if not no(t, NB - 1):
                    f_stats(t + 1, 1 - i)

            f_norm_in(0, 0)
            f_norm_in(1, 1)
            f_hidden(0, 0)
            f_stats(0, 0)
            over(dve, NB, ffn)
            dve.wait_ge(s["f_o_step"], 2 * NB)

            null_keys(cols[:, C_NK:C_NK + 1])
            norm_stats(X, 7)
            attention(1)

            norm_output(1, 8)

            def gate(t, i):
                held(dve, s["r_T_psum"], t - 1)
                dve.tensor_copy(xn[:, i, :], Y[:, t, :]).then_inc(s["r_x"], 1)

            over(dve, NB, gate)

            def wide(v, shape, axis):
                return v.unsqueeze(axis).broadcast_to(shape)

            TE = [P, NB, EXPERTS]
            TCE = [P, NB, TOPK, EXPERTS]
            dve.wait_ge(s["r_lg_psum"], NB)
            dve.tensor_tensor(lg[:], psQ[:, 0, 0:P].rearrange("p (t e) -> p t e", e=EXPERTS),
                              wide(gate_b[:], TE, 1), ALU.add).then_inc(s["r_step"], 1)
            dve.wait_ge(s["r_step"], 1)
            dve.tensor_reduce(lgm[:], lg[:], X_AXIS, ALU.max, negate=True).then_inc(s["r_step"], 1)
            dve.wait_ge(s["r_step"], 2)
            dve.tensor_tensor(le[:], lg[:], wide(lgm[:], TE, 2), ALU.add).then_inc(s["r_step"], 1)
            dve.wait_ge(s["r_exp"], 1)
            step(dve.tensor_reduce(lsum[:], le[:], X_AXIS, ALU.add))
            step(dve.reciprocal(lsum[:], lsum[:]))
            step(dve.tensor_tensor(prob[:], le[:], wide(lsum[:], TE, 2), ALU.mult))
            for t in range(NB):
                ins = dve.max(top[:, t, :], prob[:, t, :])
            step(ins)
            for t in range(NB):
                ins = dve.max_index(topi[:, t, :], top[:, t, :], prob[:, t, :])
            step(ins)
            step(dve.tensor_copy(topf[:], topi[:, :, 0:TOPK]))
            step(dve.tensor_tensor(oh[:].rearrange("p t c e -> p (t c) e"),
                                   wide(io_f[:], [P, NB * TOPK, EXPERTS], 1),
                                   wide(topf[:].rearrange("p t c -> p (t c)"), [P, NB * TOPK, EXPERTS], 2),
                                   ALU.is_equal))
            dve.tensor_copy(oh_bf[:], oh[:]).then_inc(s["r_oh"], 1)
            dve.wait_ge(s["r_pos_psum"], 1)
            counted = psQ[:, 1, :].rearrange("p (w t ce) -> p w t ce", w=2, ce=TOPK * EXPERTS)
            baset = base[:].rearrange("p t c e -> p t (c e)")
            step(dve.memset(baset[:, 0, :], 0.0))
            for t in range(1, NB):
                step(dve.tensor_tensor(baset[:, t, :], baset[:, t - 1, :], counted[:, 1, t - 1, :], ALU.add))
            step(dve.tensor_tensor(posn[:].rearrange("p t c e -> p t (c e)"), counted[:, 0], baset, ALU.add))
            dve.tensor_tensor(posn[:], posn[:], oh[:], ALU.mult).then_inc(s["r_pos_read"], 1)
            dve.wait_ge(s["r_pos_read"], 1)
            step(dve.tensor_reduce(own[:], posn[:], X_AXIS, ALU.add))
            step(dve.tensor_scalar(keep[:], own[:], float(CAP), None, ALU.is_lt))
            step(dve.scalar_tensor_tensor(dest[:], topf[:], float(CAP), own[:], ALU.mult, ALU.add))
            step(dve.scalar_tensor_tensor(dest[:], dest[:], trash[:], keep[:], ALU.subtract, ALU.mult))
            step(dve.tensor_scalar(dest[:], dest[:], trash[:], None, ALU.add))
            dve.tensor_copy(dest_u[:], dest[:]).then_inc(s["r_pay"], 1)
            dve.tensor_tensor(pay[:, :, P + 1:P + 1 + TOPK], top[:, :, 0:TOPK], keep[:], ALU.mult).then_inc(s["r_pay"], 1)

            def expert(e, i):
                for c in range(TOPK):
                    held(dve, s[f"e_sent{c}"], 16 * TILES * (e - 1))
                dve.wait_ge(s[f"e_x{i}"], arrived(e, i, 64))
                dve.tensor_copy(tags[i][:, :, 0:2, :], xb[i][:, :, 0:2, P:ROW]).then_inc(s["e_tags"], 1)
                k = TILE_ROWS[2]
                dve.tensor_copy(tags[i][0:k, :, 2, :], xb[i][0:k, :, 2, P:ROW]).then_inc(s["e_tags"], 1)
                held(dve, s["e_y_psum"], TOPK * e)
                for j in range(FB):
                    dve.wait_ge(s["e_h_psum"], 8 * e + 2 * j + 2)
                    dve.tensor_scalar(hm[:, j, CAP:2 * CAP], psH[j % 2][1][:, 0:CAP],
                                      cols[:, bass.ds(4 * e + (C_MB1 + j), 1)], 0.0, ALU.add,
                                      ALU.max).then_inc(s["e_h_dve"], 1)
                for c in range(TOPK):
                    dve.wait_ge(s["e_y_psum"], TOPK * e + c + 1)
                    dve.tensor_tensor(yb[i][:, c, 0:2, :], psS[:, c, 0:2 * P].rearrange("p (t d) -> p t d", d=P),
                                      mb2[:, bass.ds(e, 1), :].broadcast_to([P, 2, P]), ALU.add).then_inc(
                                          s["e_y_add"], 1)
                    k = TILE_ROWS[2]
                    dve.tensor_tensor(yb[i][0:k, c, 2:3, :], psS[0:k, c:c + 1, 2 * P:3 * P],
                                      mb2[0:k, bass.ds(e, 1), :], ALU.add).then_inc(s["e_y_add"], 1)

            over(dve, EXPERTS, expert)
            for q in range(4):
                dve.wait_ge(s["back_ready"], q + 1)
                for c in range(TOPK):
                    v = X[:, 4 * q:4 * q + 4, :]
                    dve.tensor_tensor(v, v, back[:, c, 4 * q:4 * q + 4, :], ALU.add).then_inc(s["z_step"], 1)
                    dve.wait_ge(s["z_step"], 2 * q + c + 1)


INPUTS = ["x", "cond_64", "fside_16xSxS_0", "mask_BxS_bf1", "mask_BxS_bk0", "L0_cond_g_norm", "L0_cond_Wq",
          "L0_cond_Wkv", "L0_cond_q_scale", "L0_cond_k_scale", "L0_cond_null_attn_bias", "L0_cond_w0",
          "L0_cond_b0", "L0_cond_g0", "L0_cond_w1", "L0_cond_b1", "L0_cond_g1", "L0_cond_w2", "L0_cond_b2",
          "L0_cond_Wout", "L0_cond_g_out", "L0_ffn_ln1_g", "L0_ffn_ln1_b", "L0_ffn_w1", "L0_ffn_b1",
          "L0_ffn_ln2_g", "L0_ffn_ln2_b", "L0_ffn_w2", "L0_ffn_b2", "L1_cond_g_in", "L1_cond_null_attn_bias",
          "L1_cond_Wq", "L1_cond_Wkv", "L1_cond_Wo", "L1_cond_g_out", "L1_ffn_gate_w", "L1_ffn_gate_b",
          "L1_ffn_W1", "L1_ffn_b1", "L1_ffn_W2", "L1_ffn_b2"]


def kernel(**inputs):
    import numpy as np
    import concourse.bacc as bacc
    from concourse.bass_utils import run_bass_kernel_spmd

    nc = bacc.Bacc("TRN2", target_bir_lowering=False, num_devices=1)
    arrays, aps = {}, {}
    for name in INPUTS:
        v = np.ascontiguousarray(inputs[name])
        if v.dtype == np.bool_:
            v = v.view(np.uint32)
        arrays["in_" + name] = v
        aps[name] = nc.dram_tensor("in_" + name, v.shape, mybir.dt.from_np(v.dtype), kind="ExternalInput").ap()
    out = nc.dram_tensor("out_x", (NB, P, P), F32, kind="ExternalOutput").ap()
    build(nc, aps, out)
    return run_bass_kernel_spmd(nc, [arrays], core_ids=[0]).results[0]["out_x"]
```

```python
from contextlib import ExitStack

import concourse.bass as bass
from concourse import mybir

F32 = mybir.dt.float32
BF16 = mybir.dt.bfloat16
U32 = mybir.dt.uint32
I32 = mybir.dt.int32
U8 = mybir.dt.uint8
ALU = mybir.AluOpType
ACT = mybir.ActivationFunctionType
X_AXIS = mybir.AxisListType.X

P = 128
NB = 16
HEADS = 16
DH = 64
HIDDEN = 512
FB = HIDDEN // P
EXPERTS = 8
CAP = 320
TOPK = 2
SLOTS = EXPERTS * CAP
TILE_ROWS = [P, P, CAP - 2 * P]
TILES = len(TILE_ROWS)
ROW = 132
QB = 32
UNITS = P // QB
KEYS = P + 2
WIDTH = [QB * (u + 1) + 1 for u in range(UNITS)]
BIAS_AT = [4 * sum(WIDTH[:u]) for u in range(UNITS + 1)]
CONSTS = 18
ROWS_DMAS = 15
BCAST_DMAS = 14
LATE_DMAS = 7
REL_DMAS = 8
SCRATCH_ALL = 1 + 16 * (TOPK * TILES + TOPK * NB // 4)
FAR = -1e30
MASKED = -1e20
LN_EPS = 1e-5


def build(nc, a, out):
    ctx = ExitStack()
    with ctx:
        def sb(name, shape, dt=F32):
            return ctx.enter_context(nc.sbuf_tensor(name, shape, dt))

        def pb(name, shape, dt=F32):
            return ctx.enter_context(nc.psum_tensor(name, shape, dt))

        def sem(name):
            return ctx.enter_context(nc.semaphore(name))

        def dram(name, shape, dt=F32):
            return nc.dram_tensor(name, shape, dt).ap()

        def at(ap, offset, dims):
            return bass.AP(ap.tensor, offset, dims)

        rel_d = dram("rel_scratch", (HEADS, QB, 2 * P))
        slot_d = [dram(f"slot_rows{c}", (SLOTS + P, ROW)) for c in range(TOPK)]
        back_d = [dram(f"choice_rows{c}", (NB * P + P, P)) for c in range(TOPK)]

        X = sb("X", [P, NB, P])
        Y = sb("Y", [P, NB, P])
        ident = sb("ident", [P, P])
        ones = sb("ones", [P, P])
        ones_bf = sb("ones_bf", [P, P], BF16)
        before_bf = sb("before_bf", [P, P], BF16)
        rows = sb("rows", [P, P])
        cols = sb("cols", [P, P])
        Wq = [sb("Wq0", [P, HEADS * DH]), sb("Wq1", [P, HEADS * DH])]
        Wkv = [sb("Wkv0", [P, P]), sb("Wkv1", [P, P])]
        Wo = [sb("Wo0", [P, 8, P]), sb("Wo1", [P, 8, P])]
        bias = [sb("bias0", [P, BIAS_AT[-1]]), sb("bias1", [P, BIAS_AT[-1]])]
        nullb = [sb("nullb0", [P, 4]), sb("nullb1", [P, 4])]
        mask_u8 = [sb("mask0_u8", [P, NB * P], U8), sb("mask1_u8", [P, NB * P], U8)]
        mask = [sb("mask0", [P, NB, KEYS], BF16), sb("mask1", [P, NB, KEYS], BF16)]
        g_out = [sb("g_out0", [P, P]), sb("g_out1", [P, P])]
        kqs = sb("kqs", [P, DH])
        qs_row = sb("qs_row", [P, DH])
        nk_row = sb("nk_row", [P, DH])
        vnull = sb("vnull", [P, DH])
        nk0 = sb("nk0", [P, 1])
        w1_raw = sb("w1_raw", [P, FB, P])
        w2_raw = sb("w2_raw", [P, FB, P])
        w1T = sb("w1T", [P, HIDDEN])
        w2T = sb("w2T", [P, FB, P])
        tern = sb("tern", [P, 2, HIDDEN])
        wabs = sb("wabs", [P, 2])
        wmean = sb("wmean", [P, 2])
        wscale = sb("wscale", [P, 2])
        fb1 = sb("fb1", [P, HIDDEN])
        fb2 = sb("fb2", [P, P])
        rel_rows = sb("rel_rows", [P, 5, P])
        rel_w1 = sb("rel_w1", [P, P])
        rel_w2 = sb("rel_w2", [P, HEADS])
        rel_b2 = sb("rel_b2", [HEADS, 1])
        rel_h = sb("rel_h", [P, P])
        rel_n = sb("rel_n", [P, P])
        rel_s = sb("rel_s", [P, P])
        rel_T = sb("rel_T", [P, P])
        rel_tab = sb("rel_tab", [HEADS, 2 * P])
        pos_i = sb("pos_i", [P, 1], I32)
        pos_f = sb("pos_f", [P, 1])
        half = sb("half", [P, 20])
        small = sb("small", [P, 16])
        gate_rows = sb("gate_rows", [EXPERTS, P])
        gateT = sb("gateT", [P, EXPERTS])
        gate_b = sb("gate_b", [P, EXPERTS])
        mb2 = sb("mb2", [P, EXPERTS, P])

        stats = sb("stats", [P, NB, 6])
        mv = sb("mv", [P, NB, 2])
        ve = sb("ve", [P, NB])
        rstd = sb("rstd", [P, NB])

        run = {w: (sb(f"{w}_st", [P, 2, 6]), sb(f"{w}_mv", [P, 2, 2]), sb(f"{w}_ve", [P, 2]),
                   sb(f"{w}_rs", [P, 2])) for w in ("o", "h", "x")}
        centred = sb("centred", [P, P])
        xn = sb("xn", [P, 2, P])
        xnT = [sb("xnT0", [P, P]), sb("xnT1", [P, P])]
        qsq = sb("qsq", [P, HEADS + 1, DH])
        qss = sb("qss", [P, HEADS + 1])
        qssc = sb("qssc", [P, HEADS + 1])
        qrn = sb("qrn", [P, HEADS + 1])
        qn = sb("qn", [P, HEADS * DH])
        qT = [sb("qT0", [P, 2, UNITS, 4, QB]), sb("qT1", [P, 2, UNITS, 4, QB])]
        kd = [sb("kd0", [P, 2, DH]), sb("kd1", [P, 2, DH])]
        vs = sb("vs", [P, DH])
        vp = [sb("vp0", [P, DH]), sb("vp1", [P, DH])]
        kk = [sb("kk0", [P, 2, KEYS]), sb("kk1", [P, 2, KEYS])]
        sc = [sb(f"sc{u}", [P, 2, 2, WIDTH[u]]) for u in range(UNITS)]
        negmax = sb("negmax", [P, UNITS, 4])
        psum_row = sb("psum_row", [P, UNITS, 4])
        rsum = sb("rsum", [P, UNITS, 4])
        pn = [sb(f"pn{i}", [P, 4, P]) for i in range(2)]
        PT = [sb(f"PT{i}", [P, 2, 2, P]) for i in range(2)]
        OT = [sb(f"OT{i}", [P, 8, UNITS, QB]) for i in range(2)]

        z = sb("z", [P, 2, HIDDEN])
        hT = [sb("hT0", [P, P]), sb("hT1", [P, P])]
        gn = sb("gn", [P, 2, HIDDEN])
        gnT = [sb("gnT0", [P, FB, P]), sb("gnT1", [P, FB, P])]
        zst = sb("zst", [P, 2, 6])
        zmv = sb("zmv", [P, 2, 2])
        zve = sb("zve", [P, 2])
        zrstd = sb("zrstd", [P, 2])
        ffo = sb("ffo", [P, P])

        lg = sb("lg", [P, NB, EXPERTS])
        lgm = sb("lgm", [P, NB])
        le = sb("le", [P, NB, EXPERTS])
        lsum = sb("lsum", [P, NB])
        prob = sb("prob", [P, NB, EXPERTS])
        top = sb("top", [P, NB, 8])
        topi = sb("topi", [P, NB, 8], U32)
        topf = sb("topf", [P, NB, TOPK])
        io_i = sb("io_i", [P, EXPERTS], I32)
        io_f = sb("io_f", [P, EXPERTS])
        oh = sb("oh", [P, NB, TOPK, EXPERTS])
        oh_bf = sb("oh_bf", [P, NB, TOPK, EXPERTS], BF16)
        posn = sb("posn", [P, NB, TOPK, EXPERTS])
        own = sb("own", [P, NB, TOPK])
        keep = sb("keep", [P, NB, TOPK])
        dest = sb("dest", [P, NB, TOPK])
        dest_u = sb("dest_u", [P, NB, TOPK], U32)
        trash_i = sb("trash_i", [P, 1], I32)
        trash = sb("trash", [P, 1])
        tok_i = sb("tok_i", [P, NB], I32)
        pay = sb("pay", [P, NB, ROW])
        wide_buf = sb("wide_buf", [P, TOPK * NB * P])
        empty = sb("empty", [P, ROW])
        zero_row = sb("zero_row", [P, 4, P])
        ept = sb("ept_id", [P, 1], I32)

        eW1 = [sb("eW10", [P, HIDDEN]), sb("eW11", [P, HIDDEN])]
        eW2 = [sb("eW20", [P, FB, P]), sb("eW21", [P, FB, P])]
        xb = [sb(f"xb{i}", [P, TOPK, TILES, ROW]) for i in range(2)]
        xbT = sb("xbT", [P, TOPK * CAP])
        hm = sb("hm", [P, FB, TOPK * CAP])
        tags = [sb(f"tags{i}", [P, TOPK, TILES, 4]) for i in range(2)]
        yb = [v[:, 0:TOPK * TILES * P].rearrange("p (c t d) -> p c t d", c=TOPK, t=TILES)
              for v in (gn[:].rearrange("p i d -> p (i d)"), qn[:])]
        masked_bias = [wide_buf[:, i * BIAS_AT[-1]:(i + 1) * BIAS_AT[-1]] for i in range(2)]
        back = wide_buf[:].rearrange("p (c t d) -> p c t d", c=TOPK, t=NB)

        yT = hm[:].rearrange("p j r -> p (j r)")[:, 0:NB * P].rearrange("p (g d) -> p g d", g=4)

        psS = pb("psS", [P, 2, 512])
        psT = pb("psT", [P, 2, 512])
        psQ = pb("psQ", [P, 2, 512])
        psO = pb("psO", [P, 512])
        psA = pb("psA", [P, 512])

        psG = [psT[:, 0, :], psT[:, 1, :], psO[:], psA[:]]
        psH = [[psQ[:, 0, :], psQ[:, 1, :]], [psO[:], psA[:]]]

        C_GN0, C_GIN1, C_LN1G, C_LN1B, C_LN2G, C_LN2B, C_MB1 = 0, 1, 2, 3, 4, 8, 12
        C_VN, C_NK, C_QS, C_KS = 44, 45, 46, 47
        N_ROWS = 48

        rows_in = sem("rows_in")
        x_in = sem("x_in")
        bcast_in = sem("bcast_in")
        late_in = sem("late_in")
        net_in = sem("net_in")
        ffnw_in = sem("ffnw_in")
        attw_in = sem("attw_in")
        table_in = sem("table_in")
        rel_out = sem("rel_out")
        rel_in = sem("rel_in")
        scratch_out = sem("scratch_out")
        const_done = sem("const_done")
        pool_step = sem("pool_step")
        dve_step = sem("dve_step")

        names = ["xn_ready", "xnT_psum", "xnT_ready", "kv_psum", "q_psum", "k_ready", "v_read", "v_ready", "kT_psum",
                 "kk_ready", "q_ready", "sq_ready", "ss_step", "rn_ready", "qn_ready", "qT_psum",
                 "scores_psum", "scores_ready", "negmax_ready", "exp_done", "rsum_ready",
                 "probs_ready", "probsT_psum", "probsT_ready", "out_psum", "out_ready", "y_psum",
                 "y_done", "kk_null", "bias_ready"]
        s = {n: sem(n) for n in names}
        for n in ["cols_psum", "wabs_ready", "rel_s_ready", "rel_n_ready", "rel_psum", "rel_T_ready",
                  "tern_ready", "ternT_psum", "masks_ready", "setup_read", "ffnw_ready", "cols_ready"]:
            s[n] = sem(n)
        for n in ["f_h", "f_h_psum", "f_hT", "f_z_psum", "f_z_ready", "f_gelu", "f_stat", "f_var", "f_rstd",
                  "f_gn", "f_gnT_psum", "f_gnT", "f_o_psum", "f_o_step"]:
            s[n] = sem(n)
        for n in ["ln_var", "ln_rstd", "r_T_psum", "r_T", "r_T_dve", "r_lg_psum", "r_step", "r_exp",
                  "r_oh", "r_pos_read", "r_pos_psum", "r_pay", "r_pool", "slots_out0", "slots_out1",
                  "e_w0", "e_w1", "e_x0", "e_x1",
                  "e_T_psum", "e_T", "e_h_psum", "e_h_act", "e_h_dve", "e_y_psum", "e_y_add", "e_y0", "e_y1",
                  "back_in0", "back_in1", "back_in2", "back_in3", "z_step", "final_out",
                  "e_sent0", "e_sent1", "e_tags"]:
            s[n] = sem(n)
        for n in ["o_stat", "o_var", "o_rstd", "h_stat", "h_var", "h_rstd", "x_stat", "x_var", "x_rstd",
                  "n_step"]:
            s[n] = sem(n)

        def unit_bias(layer, u):
            return bias[layer][:, BIAS_AT[u]:BIAS_AT[u + 1]].rearrange(
                "p (h e k) -> p h e k", h=2, e=2)

        def unit_masked(i, u):
            return masked_bias[i][:, BIAS_AT[u]:BIAS_AT[u + 1]].rearrange("p (h e k) -> p h e k", h=2, e=2)

        def unit_psum(u):
            return psS[:, :, 0:2 * WIDTH[u]].rearrange("p h (e k) -> p h e k", e=2)

        block = ctx.enter_context(nc.Block())

        def over(eng, count, body, first=2):
            for t in range(first):
                body(t, t % 2)
            with eng.Fori(first // 2, count // 2 - 1) as k:
                body(2 * k, 0)
                body(2 * k + 1, 1)
            body(count - 2, 0)
            body(count - 1, 1)

        def held(eng, semaphore, value):
            if not (isinstance(value, int) and value <= 0):
                eng.wait_ge(semaphore, value)

        def apart(eng, *waits):
            values = [v if isinstance(v, int) else eng.to_reg(v) for _, v in waits]
            eng.wait_ge(const_done, CONSTS)
            for (semaphore, _), v in zip(waits, values):
                if not isinstance(v, int) or v > 0:
                    eng.wait_ge(semaphore, v)

        def arrived(e, i, count):
            return count * (e // 2 + 1) if isinstance(e, int) else (e - i) * (count // 2) + count

        def no(t, value):
            return isinstance(t, int) and t == value

        @block.sync
        def _(sp):
            n_rows = 0

            def row(name, r0, n=1, k=P, at_col=0):
                nonlocal n_rows
                src = a[name]
                src = at(src, src.offset, [[k, n], [1, k]])
                sp.dma_start(rows[r0:r0 + n, at_col:at_col + k], src).then_inc(rows_in, 16)
                n_rows += 1

            def spread(dst, name, k, done, offset=0):
                src = a[name]
                sp.dma_start(dst, at(src, src.offset + offset, [[0, P], [1, k]])).then_inc(done, 16)

            for i, name in enumerate(("L0_cond_w0", "L0_cond_b0", "L0_cond_g0", "L0_cond_b1",
                                      "L0_cond_g1")):
                spread(rel_rows[:, i, :], name, P, net_in)
            sp.dma_start(rel_w1[:], a["L0_cond_w1"]).then_inc(net_in, 16)
            sp.dma_start(rel_w2[:], a["L0_cond_w2"]).then_inc(net_in, 16)
            sp.dma_start(rel_b2[:], at(a["L0_cond_b2"], 0, [[1, HEADS], [1, 1]])).then_inc(net_in, 16)

            sp.dma_start(X[:], a["x"].rearrange("b n d -> n b d")).then_inc(x_in, 16)

            row("L0_cond_g_norm", C_GN0)
            row("L1_cond_g_in", C_GIN1)
            row("L0_ffn_ln1_g", C_LN1G)
            row("L0_ffn_ln1_b", C_LN1B)
            row("L0_ffn_ln2_g", C_LN2G, 4)
            row("L0_ffn_ln2_b", C_LN2B, 4)
            row("L1_ffn_b1", C_MB1, 32)
            for d in range(2):
                c = a["cond_64"]
                sp.dma_start(rows[C_VN:C_VN + 1, d * DH:(d + 1) * DH], c[1:2, :]).then_inc(rows_in, 16)
                sp.dma_start(rows[C_NK:C_NK + 1, d * DH:(d + 1) * DH], c[0:1, :]).then_inc(rows_in, 16)
                row("L0_cond_q_scale", C_QS, 1, DH, d * DH)
                row("L0_cond_k_scale", C_KS, 1, DH, d * DH)
            assert n_rows + 4 == ROWS_DMAS

            spread(kqs[:], "L0_cond_k_scale", DH, bcast_in)
            spread(qs_row[:], "L0_cond_q_scale", DH, bcast_in)
            spread(nk_row[:], "cond_64", DH, bcast_in)
            spread(vnull[:], "cond_64", DH, bcast_in, DH)
            for layer, name in enumerate(("mask_BxS_bf1", "mask_BxS_bk0")):
                sp.dma_start(mask_u8[layer][:].bitcast(U32),
                             at(a[name], 0, [[0, P], [1, NB * P // 4]])).then_inc(bcast_in, 16)
            for layer in range(2):
                src = a[f"L{layer}_cond_null_attn_bias"]
                for m in range(4):
                    sp.dma_start(nullb[layer][QB * m:QB * (m + 1), :].rearrange("p (h e) -> p h e", e=2),
                                 at(src, 2 * m, [[0, QB], [8, 2], [1, 2]])).then_inc(bcast_in, 16)
            assert BCAST_DMAS == 4 + 2 + 8

            sp.wait_ge(rel_out, 1)
            sp.dma_start(rel_d, rel_tab[:].unsqueeze(1).broadcast_to([HEADS, QB, 2 * P])).then_inc(rel_out, 16)

            for layer in range(2):
                wo = a["L0_cond_Wout" if layer == 0 else "L1_cond_Wo"]
                sp.dma_start(Wq[layer][:], a[f"L{layer}_cond_Wq"]).then_inc(attw_in, 16)
                sp.dma_start(Wkv[layer][:], a[f"L{layer}_cond_Wkv"]).then_inc(attw_in, 16)
                sp.dma_start(Wo[layer][:], wo.rearrange("(j p) d -> p j d", p=P)).then_inc(attw_in, 16)
            sp.dma_start(w1_raw[:], a["L0_ffn_w1"].rearrange("(j p) d -> p j d", p=P)).then_inc(ffnw_in, 16)
            sp.dma_start(w2_raw[:], a["L0_ffn_w2"].rearrange("p (j h) -> p j h", j=FB)).then_inc(ffnw_in, 16)

            sp.wait_ge(rel_out, 17)
            for u in range(UNITS):
                for m in range(4):
                    for hh in range(2):
                        sp.dma_start(unit_bias(0, u)[QB * m:QB * (m + 1), hh, :, 1:WIDTH[u]],
                                     at(rel_d, (8 * hh + 2 * m) * QB * 2 * P + P - 1 - QB * u,
                                        [[2 * P - 1, QB], [QB * 2 * P, 2], [1, WIDTH[u] - 1]])).then_inc(
                                            rel_in, 16)

            spread(fb1[:], "L0_ffn_b1", HIDDEN, late_in)
            spread(fb2[:], "L0_ffn_b2", P, late_in)
            spread(g_out[0][:], "L0_cond_g_out", P, late_in)
            spread(g_out[1][:], "L1_cond_g_out", P, late_in)
            spread(gate_b[:], "L1_ffn_gate_b", EXPERTS, late_in)
            spread(mb2[:].rearrange("p e d -> p (e d)"), "L1_ffn_b2", EXPERTS * P, late_in)
            sp.dma_start(gate_rows[:], a["L1_ffn_gate_w"]).then_inc(late_in, 16)
            fs = a["fside_16xSxS_0"]
            for u in range(UNITS):
                for m in range(4):
                    for hh in range(2):
                        sp.dma_start(unit_bias(1, u)[QB * m:QB * (m + 1), hh, :, 1:WIDTH[u]],
                                     at(fs, ((8 * hh + 2 * m) * P + QB * u) * P,
                                        [[P, QB], [P * P, 2], [1, WIDTH[u] - 1]])).then_inc(table_in, 16)

            sp.wait_ge(scratch_out, 1)
            for c in range(TOPK):
                for t, k in enumerate(TILE_ROWS):
                    sp.dma_start(at(slot_d[c], t * P * ROW, [[ROW, k], [CAP * ROW, EXPERTS], [1, ROW]]),
                                 empty[0:k, :].unsqueeze(1).broadcast_to([k, EXPERTS, ROW])).then_inc(
                                     scratch_out, 16)
                for r in range(0, NB, 4):
                    sp.dma_start(at(back_d[c], r * P * P, [[P, P], [P * P, 4], [1, P]]),
                                 zero_row[:]).then_inc(scratch_out, 16)

            def load_expert(e, i):
                sp.dma_start(eW1[i][:], a["L1_ffn_W1"][e]).then_inc(s[f"e_w{i}"], 16)
                sp.dma_start(eW2[i][:], a["L1_ffn_W2"][e].rearrange("(j p) d -> p j d", p=P)).then_inc(
                    s[f"e_w{i}"], 16)

            def load_slots(e, i):
                for c in range(TOPK):
                    src = slot_d[c][bass.ds(e * CAP, 2 * P), :].rearrange("(t p) r -> p t r", p=P)
                    sp.dma_start(xb[i][:, c, 0:2, :], src).then_inc(s[f"e_x{i}"], 16)
                    sp.dma_start(xb[i][0:TILE_ROWS[2], c, 2, :],
                                 slot_d[c][bass.ds(e * CAP + 2 * P, TILE_ROWS[2]), :]).then_inc(s[f"e_x{i}"], 16)

            load_expert(0, 0)
            load_expert(1, 1)
            for c in range(TOPK):
                sp.wait_ge(s[f"slots_out{c}"], 16 * NB)
            load_slots(0, 0)
            load_slots(1, 1)
            with sp.Fori(0, EXPERTS // 2 - 1) as k:
                for i in range(2):
                    e = 2 * k + i
                    sp.wait_ge(s["e_T_psum"], e + 1)
                    sp.wait_ge(s["e_tags"], 2 * e + 2)
                    load_slots(e + 2, i)
                    sp.wait_ge(s["e_y_psum"], 2 * e + 2)
                    load_expert(e + 2, i)
            for c in range(TOPK):
                sp.wait_ge(s[f"e_sent{c}"], 16 * TILES * EXPERTS)
            for q in range(4):
                for c in range(TOPK):
                    src = at(back_d[c], 4 * q * P * P, [[P, P], [P * P, 4], [1, P]])
                    sp.dma_start(back[:, c, 4 * q:4 * q + 4, :], src).then_inc(s[f"back_in{q}"], 16)
            out_v = out.rearrange("b n d -> n b d")
            for q in range(4):
                sp.wait_ge(s["z_step"], 2 * (q + 1))
                sp.dma_start(out_v[:, 4 * q:4 * q + 4, :], X[:, 4 * q:4 * q + 4, :]).then_inc(
                    s["final_out"], 16)
            sp.wait_ge(s["final_out"], 64)

        @block.gpsimd
        def _(pool):
            pool.memset(ident[:], 0.0).then_inc(const_done, 1)
            pool.memset(ones[:], 1.0).then_inc(const_done, 1)
            pool.memset(ones_bf[:], 1.0).then_inc(const_done, 1)
            pool.memset(half[:], -0.5).then_inc(const_done, 1)
            pool.memset(rel_tab[:], FAR).then_inc(const_done, 1)
            pool.memset(kk[0][:], 0.0).then_inc(const_done, 1)
            pool.memset(kk[1][:], 0.0).then_inc(const_done, 1)
            pool.memset(mask[0][:], 0.0).then_inc(const_done, 1)
            pool.memset(mask[1][:], 0.0).then_inc(const_done, 1)
            pool.memset(empty[:], 0.0).then_inc(const_done, 1)
            pool.memset(zero_row[:], 0.0).then_inc(const_done, 1)
            pool.wait_ge(const_done, 11)
            pool.affine_select(ident[:], ident[:], pattern=[[-1, P]], compare_op=ALU.not_equal, fill=1.0,
                               base=0, channel_multiplier=1).then_inc(const_done, 1)
            pool.affine_select(before_bf[:], ones_bf[:], pattern=[[1, P]], compare_op=ALU.is_gt, fill=0.0,
                               base=0, channel_multiplier=-1).then_inc(const_done, 1)
            pool.iota(pos_i[:], pattern=[[0, 1]], base=P - 1, channel_multiplier=-1).then_inc(const_done, 1)
            pool.iota(io_i[:], pattern=[[1, EXPERTS]], base=0, channel_multiplier=0).then_inc(const_done, 1)
            pool.iota(trash_i[:], pattern=[[0, 1]], base=SLOTS, channel_multiplier=1).then_inc(const_done, 1)
            pool.iota(tok_i[:], pattern=[[P, NB]], base=0, channel_multiplier=1).then_inc(const_done, 1)
            pool.iota(ept[:], pattern=[[0, 1]], base=NB * P, channel_multiplier=1).then_inc(const_done, 1)
            pool.wait_ge(const_done, CONSTS)
            pool.tensor_copy(empty[:, P:P + 1].bitcast(I32), ept[:]).then_inc(scratch_out, 1)

            def rsqrt(dst, src, k, done, count=1):
                pool.tensor_tensor(dst, src, half[:, 0:k], ALU.pow).then_inc(done, count)

            for n, (dst, src, k) in enumerate(((small[:, 1:2], small[:, 0:1], 1), (small[:, 3:4], small[:, 2:3], 1),
                                               (rstd[:], ve[:], NB), (small[:, 5:6], small[:, 4:5], 1))):
                pool.wait_ge(s["ln_var"], n + 1)
                rsqrt(dst, src, k, s["ln_rstd"])

            def hide(b):
                pool.wait_ge(table_in, 16 * 32)
                if b == 3:
                    pool.wait_ge(s["o_rstd"], 1)
                else:
                    pool.wait_ge(s["h_rstd"], b - 3)
                for k in {3: range(0, 4), NB - 2: range(4, 10), NB - 1: range(10, 16)}[b]:
                    u, m = k // 4, k % 4
                    if k:
                        pool.wait_ge(pool_step, k)
                    v = unit_bias(1, u)[QB * m:QB * (m + 1)].rearrange("p h e k -> p (h e) k")[:, :, 1:WIDTH[u]]
                    pool.affine_select(v, v, pattern=[[0, 4], [-1, WIDTH[u] - 1]], compare_op=ALU.is_ge,
                                       fill=FAR, base=QB * u, channel_multiplier=1).then_inc(pool_step, 1)
                pool.wait_ge(pool_step, k + 1)

            def q_norm(b):
                for h, (lo, hi) in enumerate(((0, 9), (9, HEADS + 1))):
                    pool.wait_ge(s["ss_step"], 4 * b + 2 * h + 2)
                    rsqrt(qrn[:, lo:hi], qssc[:, lo:hi], hi - lo, s["rn_ready"])

            def values_set(layer, b, i):
                B = b + NB * layer
                pool.wait_ge(s["v_read"], B + 1)
                held(pool, s["out_psum"], 4 * B - 4)
                pool.tensor_tensor(vp[i][:], vs[:], vnull[:], ALU.subtract).then_inc(s["v_ready"], 1)

            def output_rstd(n, i):
                pool.wait_ge(s["o_var"], n + 1)
                rsqrt(run["o"][3][:, i:i + 1], run["o"][2][:, i:i + 1], 1, s["o_rstd"])

            def input_rstd(w, n, t, i):
                apart(pool, (s[f"{w}_var"], n + 1))
                rsqrt(rstd[:, bass.ds(t, 1)], run[w][2][:, i:i + 1], 1, s[f"{w}_rstd"])

            def mask_bias(layer, b, u, i):
                n = 4 * (b + NB * layer) + u
                apart(pool, (s["scores_ready"], n - 7))
                k = WIDTH[u]
                pool.tensor_tensor(unit_masked(i, u).rearrange("p h e k -> p (h e) k"),
                                   unit_bias(layer, u).rearrange("p h e k -> p (h e) k"),
                                   mask[layer][:, bass.ds(b, 1), 0:k].broadcast_to([P, 4, k]),
                                   ALU.add).then_inc(s["bias_ready"], 1)

            def attention(layer):
                def batch(b, i):
                    if layer == 0 and isinstance(b, int) and b in (3, NB - 2, NB - 1):
                        hide(b)
                    if not no(b, NB - 1):
                        mask_bias(layer, b + 1, 0, 1 - i)
                        if layer == 0:
                            q_norm(b + 1)
                        for u in range(1, UNITS):
                            mask_bias(layer, b + 1, u, 1 - i)
                        values_set(layer, b + 1, 1 - i)
                    if not (no(b, 0) or no(b, 1)):
                        output_rstd(b - 2 + NB * layer, i)
                    if layer == 0 and not (no(b, 0) or no(b, 1) or no(b, 2)):
                        input_rstd("h", b - 3, b - 3, 1 - i)

                if layer == 0:
                    q_norm(0)
                    pool.wait_ge(rel_in, 16 * 32)
                    pool.wait_ge(s["masks_ready"], 1)
                for u in range(UNITS):
                    mask_bias(layer, 0, u, 0)
                values_set(layer, 0, 0)
                over(pool, NB, batch, 4)
                for b in (NB - 2, NB - 1):
                    if layer == 0:
                        input_rstd("h", b - 1, b - 1, (b - 1) % 2)
                    output_rstd(b + NB * layer, b % 2)
                if layer == 0:
                    input_rstd("h", NB - 1, NB - 1, 1)

            attention(0)

            def f_norm(t, i):
                pool.wait_ge(s["f_var"], t + 1)
                rsqrt(zrstd[:, i:i + 1], zve[:, i:i + 1], 1, s["f_rstd"])
                if not (no(t, 0) or no(t, 1) or no(t, 2)):
                    input_rstd("x", t - 3, t - 3, 1 - i)

            over(pool, NB, f_norm, 4)
            for t in range(NB - 3, NB):
                input_rstd("x", t, t, t % 2)
            attention(1)

            pool.wait_ge(s["n_step"], 2 * NB * 2)
            pool.tensor_copy(pay[:, :, 0:P], Y[:]).then_inc(s["r_pool"], 1)
            pool.tensor_copy(pay[:, :, P:P + 1].bitcast(I32), tok_i[:].unsqueeze(2)).then_inc(s["r_pool"], 1)
            pool.memset(pay[:, :, P + 3:ROW], 0.0).then_inc(s["r_pool"], 1)
            pool.wait_ge(s["r_pool"], 3)
            pool.wait_ge(s["r_pay"], 2)
            pool.wait_ge(scratch_out, SCRATCH_ALL)
            for t in range(NB):
                for c in range(TOPK):
                    if t:
                        pool.wait_ge(s[f"slots_out{c}"], 16 * t)
                    pool.indirect_dma_start(slot_d[c], bass.IndirectOffsetOnAxis(dest_u[:, t, c:c + 1], 0),
                                            pay[:, t, :], None).then_inc(s[f"slots_out{c}"], 16)

            def send(e, i):
                for t, k in enumerate(TILE_ROWS):
                    for c in range(TOPK):
                        apart(pool, (s[f"e_y{c}"], TILES * e + t + 1),
                              (s[f"e_sent{c}"], 16 * (TILES * e + t)))
                        pool.indirect_dma_start(back_d[c], bass.IndirectOffsetOnAxis(
                            tags[i][0:k, c, t, 0:1].bitcast(U32), 0), yb[i][0:k, c, t, :],
                            None).then_inc(s[f"e_sent{c}"], 16)

            over(pool, EXPERTS, send)

        @block.tensor
        def _(pe):
            pe.wait_ge(const_done, CONSTS)
            pe.wait_ge(net_in, 16 * REL_DMAS)
            pe.wait_ge(s["rel_s_ready"], 1)
            pe.transpose(psQ[:, 0, 0:P], rel_s[:], ident[:]).then_inc(s["rel_psum"], 1)
            pe.wait_ge(s["rel_T_ready"], 1)
            pe.matmul(psQ[:, 0, P:2 * P], rel_T[:], rel_w1[:], start=True, stop=True).then_inc(s["rel_psum"], 1)
            pe.wait_ge(s["rel_s_ready"], 2)
            pe.transpose(psQ[:, 0, 2 * P:3 * P], rel_s[:], ident[:]).then_inc(s["rel_psum"], 1)
            pe.wait_ge(s["rel_T_ready"], 2)
            pe.matmul(psQ[0:HEADS, 0, 3 * P:4 * P], rel_w2[:], rel_T[:], start=True, stop=True).then_inc(
                s["rel_psum"], 1)
            pe.wait_ge(rows_in, 16 * ROWS_DMAS)
            pe.transpose(psA[:, 0:N_ROWS], rows[0:N_ROWS, :], ident[0:N_ROWS, 0:N_ROWS]).then_inc(s["cols_psum"], 1)
            pe.wait_ge(s["wabs_ready"], 2)
            pe.matmul(psO[:, 0:2], ones[:], wabs[:], start=True, stop=True).then_inc(s["cols_psum"], 1)
            pe.wait_ge(s["cols_ready"], 1)

            def turn_ternary():
                pe.wait_ge(s["tern_ready"], 2)
                for i in range(2):
                    for j in range(FB):
                        m = pe.transpose(psT[:, i, j * P:(j + 1) * P], tern[:, i, j * P:(j + 1) * P], ident[:])
                m.then_inc(s["ternT_psum"], 1)
                pe.wait_ge(s["ffnw_ready"], 2)

            def turn_input(layer, b, i):
                B = b + NB * layer
                pe.wait_ge(s["xn_ready"], B + 1)
                held(pe, s["y_done"], B - 3)
                held(pe, s["kk_ready"], B)
                held(pe, s["v_read"], B)
                pe.transpose(psA[:, 0:P], xn[:, i, :], ident[:]).then_inc(s["xnT_psum"], 1)

            def project_in(layer, b, i):
                B = b + NB * layer
                pe.wait_ge(s["xnT_ready"], B + 1)
                held(pe, s["q_ready"], B)
                pe.matmul(psA[:, P:2 * P], xnT[i][:], Wkv[layer][:], start=True, stop=True).then_inc(s["kv_psum"], 1)
                if layer == 0:
                    for h in range(2):
                        pe.matmul(psQ[:, h, :], xnT[i][:], Wq[0][:, 512 * h:512 * (h + 1)],
                                  start=True, stop=True).then_inc(s["q_psum"], 1)
                else:
                    for h in range(2):
                        for j in range(4):
                            m = pe.matmul(psQ[:, h, j * P:(j + 1) * P], Wq[1][:, (4 * h + j) * P:(4 * h + j + 1) * P],
                                          xnT[i][:], start=True, stop=True)
                        m.then_inc(s["q_psum"], 1)

            def turn_keys(layer, b, i):
                B = b + NB * layer
                pe.wait_ge(s["k_ready"], B + 1)
                pe.transpose(psA[:, 2 * P:3 * P], kd[i][:].rearrange("p a d -> p (a d)"), ident[:]).then_inc(
                    s["kT_psum"], 1)

            def turn_queries(b):
                for h in range(2):
                    pe.wait_ge(s["qn_ready"], 2 * b + h + 1)
                    for j in range(4):
                        m = pe.transpose(psQ[:, h, j * P:(j + 1) * P], qn[:, (4 * h + j) * P:(4 * h + j + 1) * P],
                                         ident[:])
                    m.then_inc(s["qT_psum"], 1)

            def scores(layer, b, u, i):
                B = b + NB * layer
                n = 4 * B + u
                w = WIDTH[u]
                if no(b, 0) and u == 0:
                    pe.wait_ge(s["kk_null"], 4 * (layer + 1))
                apart(pe, *([(s["kk_ready"], B + 1), (s["q_ready"], B + 1)] if u == 0 else []),
                      (s["scores_ready"], n))
                for h in range(2):
                    m = pe.matmul(psS[:, h, 0:2 * w], qT[i][:, h, u].rearrange("p m q -> p (m q)"),
                                  kk[i][:, :, 0:w], start=True, stop=True)
                m.then_inc(s["scores_psum"], 1)

            def turn_probs(n, u):
                apart(pe, (s["probs_ready"], n + 1), (s["probsT_ready"], n - 1))
                k = WIDTH[u] - 1
                for g in range(4):
                    m = pe.transpose(psT[0:k, u % 2, g * P:(g + 1) * P], pn[u % 2][:, g, 0:k], ident[:])
                m.then_inc(s["probsT_psum"], 1)

            def values(n, u, i, B=None):
                apart(pe, (s["probsT_ready"], n + 1), (s["out_ready"], n),
                      *([(s["v_ready"], B + 1)] if u == 0 else []))
                k = WIDTH[u] - 1
                for e in range(2):
                    m = pe.matmul(psO[DH * e:DH * (e + 1), 0:256], vp[i][0:k, :], PT[u % 2][0:k, :, e, :],
                                  start=True, stop=True)
                m.then_inc(s["out_psum"], 1)

            def project(layer, b, i, loading):
                B = b + NB * layer
                pe.wait_ge(s["out_ready"], 4 * B + 4)
                entry = B + 3 if loading else NB * (layer + 1) - 1
                pe.wait_ge(s["v_read"], entry + 1)
                if layer == 0 and loading:
                    pe.wait_ge(s["sq_ready"], 2 * entry + 1)
                else:
                    pe.wait_ge(s["kk_ready"], entry + 1)
                if isinstance(B, int):
                    held(pe, s["y_done"], B)
                for j in range(8):
                    m = pe.matmul(psA[:, 3 * P:4 * P], OT[i][:, j].rearrange("p u q -> p (u q)"), Wo[layer][:, j, :],
                                  start=(j == 0), stop=(j == 7))
                m.then_inc(s["y_psum"], 1)

            def attention(layer):
                def batch(b, i):
                    n = 4 * (b + NB * layer)
                    first, last = no(b, 0), no(b, NB - 1)

                    def earlier(u, lag):
                        return not (first and u < lag)

                    for u in range(UNITS):
                        scores(layer, b, u, i)
                        if earlier(u, 2):
                            turn_probs(n + u - 2, (u - 2) % UNITS)
                        if u == 0 and not last:
                            project_in(layer, b + 1, 1 - i)
                        if u == 3 and not last and not no(b, NB - 2):
                            turn_input(layer, b + 2, i)
                        if earlier(u, 3):
                            values(n + u - 3, (u - 3) % UNITS, i if u == 3 else 1 - i, b + NB * layer)
                        if u == 2 - layer and not last:
                            turn_keys(layer, b + 1, 1 - i)
                        if layer == 0 and u == 2 and not last:
                            turn_queries(b + 1)
                        if u == 1 + layer and not first and not no(b, 1):
                            project(layer, b - 2, i, not last)

                if layer == 0:
                    pe.wait_ge(attw_in, 16 * 6)
                turn_input(layer, 0, 0)
                project_in(layer, 0, 0)
                turn_keys(layer, 0, 0)
                if layer == 0:
                    turn_queries(0)
                turn_input(layer, 1, 1)
                if layer == 0:
                    turn_ternary()
                over(pe, NB, batch)
                N = 4 * (NB + NB * layer)
                project(layer, NB - 2, 0, False)
                turn_probs(N - 2, 2)
                values(N - 3, 1, 1)
                turn_probs(N - 1, 3)
                values(N - 2, 2, 1)
                values(N - 1, 3, 1)
                project(layer, NB - 1, 1, False)

            attention(0)

            def f_turn(t, i):
                pe.wait_ge(s["f_h"], t + 1)
                held(pe, s["f_hT"], t)
                pe.transpose(psA[:, 0:P], xn[:, i, :], ident[:]).then_inc(s["f_h_psum"], 1)

            def f_up(t, i):
                pe.wait_ge(s["f_hT"], t + 1)
                held(pe, s["f_z_ready"], t - 1)
                pe.matmul(psQ[:, i, :], hT[i][:], w1T[:], start=True, stop=True).then_inc(s["f_z_psum"], 1)

            def f_turn_mid(t, i):
                pe.wait_ge(s["f_gn"], t + 1)
                held(pe, s["f_gnT"], t - 1)
                for j in range(FB):
                    m = pe.transpose(psT[:, i, j * P:(j + 1) * P], gn[:, i, j * P:(j + 1) * P], ident[:])
                m.then_inc(s["f_gnT_psum"], 1)

            def f_down(t, i):
                pe.wait_ge(s["f_gnT"], t + 1)
                held(pe, s["f_o_step"], 2 * t - 1)
                for j in range(FB):
                    m = pe.matmul(psO[:, 0:P], gnT[i][:, j, :], w2T[:, j, :], start=(j == 0),
                                  stop=(j == FB - 1))
                m.then_inc(s["f_o_psum"], 1)

            def ffn(t, i):
                early = no(t, 0) or no(t, 1)
                f_turn(t, i)
                if not early:
                    f_turn_mid(t - 2, i)
                f_up(t, i)
                if not early:
                    f_down(t - 2, i)

            over(pe, NB, ffn, 4)
            for t in (NB - 2, NB - 1):
                f_turn_mid(t, t % 2)
                f_down(t, t % 2)

            attention(1)

            pe.wait_ge(late_in, 16 * LATE_DMAS)
            pe.wait_ge(s["y_done"], 2 * NB)
            pe.transpose(psA[:, 2 * P:2 * P + EXPERTS], gate_rows[:], ident[0:EXPERTS, 0:EXPERTS]).then_inc(
                s["cols_psum"], 1)
            pe.wait_ge(s["setup_read"], 1)

            for g in range(4):
                for t in range(4):
                    m = pe.transpose(psG[g][:, t * P:(t + 1) * P], Y[:, 4 * g + t, :], ident[:])
                m.then_inc(s["r_T_psum"], 1)
            for t in range(NB):
                if t % 8 == 0:
                    pe.wait_ge(s["r_T"], t // 8 + 1)
                if t % 8 == 4:
                    pe.wait_ge(s["r_T_dve"], t // 8 + 1)
                m = pe.matmul(psQ[:, 0, t * EXPERTS:(t + 1) * EXPERTS], yT[:, t // 4, (t % 4) * P:(t % 4 + 1) * P],
                              gateT[:], start=True, stop=True)
            m.then_inc(s["r_lg_psum"], 1)
            pe.wait_ge(s["r_oh"], 1)
            ce = TOPK * EXPERTS
            pe.matmul(psQ[:, 1, 0:NB * ce], before_bf[:], oh_bf[:].rearrange("p t c e -> p (t c e)"),
                      start=True, stop=False)
            for t in range(NB - 1):
                m = pe.matmul(psQ[:, 1, (t + 1) * ce:NB * ce].rearrange("p (r x) -> p r x", x=ce), ones_bf[:],
                              oh_bf[:, t:t + 1].rearrange("p t c e -> p t (c e)").broadcast_to([P, NB - 1 - t, ce]),
                              start=False, stop=t == NB - 2)
            m.then_inc(s["r_pos_psum"], 1)
            pe.wait_ge(s["r_pos_read"], 1)

            def turn_rows(e, i):
                pe.wait_ge(s[f"e_x{i}"], arrived(e, i, 64))
                held(pe, s["e_T"], 2 * e)
                for c in range(TOPK):
                    for t, k in enumerate(TILE_ROWS):
                        m = pe.transpose(psT[:, c, t * P:t * P + k], xb[i][0:k, c, t, 0:P], ident[0:k, 0:k])
                m.then_inc(s["e_T_psum"], 1)

            def expert(e, i):
                pe.wait_ge(s[f"e_w{i}"], arrived(e, i, 32))
                pe.wait_ge(s["e_T"], 2 * e + 2)
                for j in range(FB):
                    for h in range(2):
                        held(pe, s["e_h_act" if h == 0 else "e_h_dve"], 4 * e + j - 1)
                        pe.matmul(psH[j % 2][h][:, 0:CAP], eW1[i][:, j * P:(j + 1) * P], xbT[:, h * CAP:(h + 1) * CAP],
                                  start=True, stop=True).then_inc(s["e_h_psum"], 1)
                if not no(e, EXPERTS - 1):
                    turn_rows(e + 1, 1 - i)
                pe.wait_ge(s["e_h_act"], 4 * e + 4)
                pe.wait_ge(s["e_h_dve"], 4 * e + 4)
                for c in range(TOPK):
                    held(pe, s["e_y_add"], 4 * e - 2 + 2 * c)
                    for t, k in enumerate(TILE_ROWS):
                        at_row = c * CAP + t * P
                        for j in range(FB):
                            m = pe.matmul(psS[0:k, c, t * P:(t + 1) * P], hm[:, j, at_row:at_row + k],
                                          eW2[i][:, j, :], start=(j == 0), stop=(j == FB - 1))
                    m.then_inc(s["e_y_psum"], 1)

            turn_rows(0, 0)
            over(pe, EXPERTS, expert)

        @block.scalar
        def _(act):
            for n in range(2):
                act.wait_ge(s["rel_n_ready"], n + 1)
                act.activation(rel_s[:], rel_n[:], ACT.Silu).then_inc(s["rel_s_ready"], 1)
            act.wait_ge(ffnw_in, 32)
            for i, w in enumerate((w1_raw, w2_raw)):
                act.activation(tern[:, i, :], w[:].rearrange("p j d -> p (j d)"), ACT.Abs,
                               accum_out=wabs[:, i:i + 1]).then_inc(s["wabs_ready"], 1)

            def ternary_T():
                act.wait_ge(s["ternT_psum"], 1)
                act.copy(w1T[:], psT[:, 0, :]).then_inc(s["ffnw_ready"], 1)
                act.copy(w2T[:].rearrange("p j d -> p (j d)"), psT[:, 1, :]).then_inc(s["ffnw_ready"], 1)

            def input_T(layer, b, i):
                B = b + NB * layer
                act.wait_ge(s["xnT_psum"], B + 1)
                held(act, s["q_psum"], 2 * B - 2)
                c = C_GN0 if layer == 0 else C_GIN1
                act.activation(xnT[i][:], psA[:, 0:P], ACT.Copy, scale=cols[:, c:c + 1]).then_inc(
                    s["xnT_ready"], 1)

            def squares(b):
                act.wait_ge(s["kv_psum"], b + 1)
                held(act, s["ss_step"], 4 * b)
                act.activation(qsq[:, 0, :], psA[:, P:P + DH], ACT.Square)
                for h in range(2):
                    act.wait_ge(s["q_psum"], 2 * b + h + 1)
                    act.activation(qsq[:, 1 + 8 * h:9 + 8 * h, :], psQ[:, h, :].rearrange("p (h d) -> p h d", d=DH),
                                   ACT.Square).then_inc(s["sq_ready"], 1)

            def queries(layer, b, i):
                B = b + NB * layer
                held(act, s["scores_psum"], 4 * B - 4)
                for h in range(2):
                    if layer == 0:
                        act.wait_ge(s["qT_psum"], 2 * b + h + 1)
                    else:
                        act.wait_ge(s["q_psum"], 2 * B + h + 1)
                    m = act.activation(qT[i][:, h].rearrange("p u m q -> p m u q"),
                                       psQ[:, h, :].rearrange("p (m u q) -> p m u q", u=UNITS, q=QB), ACT.Copy,
                                       scale=1.0 if layer == 0 else DH ** -0.5)
                m.then_inc(s["q_ready"], 1)

            def keys_T(layer, b, i):
                B = b + NB * layer
                act.wait_ge(s["kT_psum"], B + 1)
                held(act, s["scores_psum"], 4 * B - 4)
                act.copy(kk[i][0:DH, 0, 1:P + 1], psA[0:DH, 2 * P:3 * P])
                act.copy(kk[i][DH:P, 1, 1:P + 1], psA[DH:P, 2 * P:3 * P]).then_inc(s["kk_ready"], 1)

            def weights(n, u):
                act.wait_ge(s["negmax_ready"], n + 1)
                for g in range(4):
                    v = sc[u][:, g // 2, g % 2, :]
                    m = act.activation(v, v, ACT.Exp, bias=negmax[:, u, g:g + 1], accum_out=psum_row[:, u, g:g + 1])
                m.then_inc(s["exp_done"], 1)

            def weights_T(n, u):
                act.wait_ge(s["probsT_psum"], n + 1)
                held(act, s["out_psum"], n - 1)
                k = WIDTH[u] - 1
                act.copy(PT[u % 2][0:k].rearrange("p h e q -> p (h e q)"), psT[0:k, u % 2, :]).then_inc(
                    s["probsT_ready"], 1)

            def attention(layer):
                def batch(b, i):
                    n = 4 * (b + NB * layer)
                    first, last = no(b, 0), no(b, NB - 1)
                    for u in range(UNITS):
                        if not (first and u < 2):
                            weights_T(n + u - 2, (u - 2) % UNITS)
                        if layer == 0 and u == 2 and not last:
                            keys_T(layer, b + 1, 1 - i)
                            queries(layer, b + 1, 1 - i)
                        if u == 3 and not last and not no(b, NB - 2):
                            input_T(layer, b + 2, i)
                        weights(n + u, u)
                        if layer == 0 and u == 0 and not last:
                            squares(b + 1)
                        if layer == 1 and u == 1 and not last:
                            queries(layer, b + 1, 1 - i)
                        if layer == 1 and u == 1 and not last:
                            keys_T(layer, b + 1, 1 - i)

                if layer == 0:
                    act.wait_ge(s["cols_ready"], 1)
                input_T(layer, 0, 0)
                if layer == 0:
                    squares(0)
                keys_T(layer, 0, 0)
                queries(layer, 0, 0)
                input_T(layer, 1, 1)
                if layer == 0:
                    ternary_T()
                over(act, NB, batch)
                N = 4 * (NB + NB * layer)
                weights_T(N - 2, 2)
                weights_T(N - 1, 3)

            attention(0)

            def f_in(t, i):
                act.wait_ge(s["f_h_psum"], t + 1)
                held(act, s["f_z_psum"], t - 1)
                act.activation(hT[i][:], psA[:, 0:P], ACT.Identity, scale=cols[:, C_LN1G:C_LN1G + 1],
                               bias=cols[:, C_LN1B:C_LN1B + 1]).then_inc(s["f_hT"], 1)

            def f_mid(t, i):
                act.wait_ge(s["f_gnT_psum"], t + 1)
                held(act, s["f_o_psum"], t - 1)
                for j in range(FB):
                    m = act.activation(gnT[i][:, j, :], psT[:, i, j * P:(j + 1) * P], ACT.Identity,
                                       scale=cols[:, C_LN2G + j:C_LN2G + j + 1],
                                       bias=cols[:, C_LN2B + j:C_LN2B + j + 1])
                m.then_inc(s["f_gnT"], 1)

            def f_gelu(t, i):
                act.wait_ge(s["f_z_ready"], t + 1)
                act.activation(z[:, i, :], z[:, i, :], ACT.Gelu).then_inc(s["f_gelu"], 1)

            def ffn(t, i):
                f_in(t, i)
                if not (no(t, 0) or no(t, 1)):
                    f_mid(t - 2, i)
                f_gelu(t, i)

            over(act, NB, ffn, 4)
            f_mid(NB - 2, 0)
            f_mid(NB - 1, 1)

            attention(1)

            for g in (0, 2):
                act.wait_ge(s["r_T_psum"], g + 1)
                act.copy(yT[:, g, :], psG[g]).then_inc(s["r_T"], 1)
            act.wait_ge(s["r_step"], 3)
            act.activation(le[:], le[:], ACT.Exp).then_inc(s["r_exp"], 1)

            def rows_T(e):
                act.wait_ge(s["e_T_psum"], e + 1)
                held(act, s["e_h_psum"], 8 * e)
                for c in range(TOPK):
                    act.copy(xbT[:, c * CAP:(c + 1) * CAP], psT[:, c, 0:CAP]).then_inc(s["e_T"], 1)

            def hidden(e, blocks):
                for j in blocks:
                    act.wait_ge(s["e_h_psum"], 8 * e + 2 * j + 1)
                    act.activation(hm[:, j, 0:CAP], psH[j % 2][0][:, 0:CAP], ACT.Relu,
                                   bias=cols[:, bass.ds(4 * e + (C_MB1 + j), 1)]).then_inc(s["e_h_act"], 1)

            def scaled(e, i, c):
                act.wait_ge(s["e_y_add"], 4 * e + 2 * c + 2)
                for t, k in enumerate(TILE_ROWS):
                    act.activation(yb[i][0:k, c, t, :], yb[i][0:k, c, t, :], ACT.Copy,
                                   scale=tags[i][0:k, c, t, 1 + c:2 + c]).then_inc(s[f"e_y{c}"], 1)

            def expert(e, i):
                held(act, s["e_y_psum"], TOPK * e)
                hidden(e, (0, 1))
                if not no(e, 0):
                    scaled(e - 1, 1 - i, 1)
                hidden(e, (2, 3))
                if not no(e, EXPERTS - 1):
                    rows_T(e + 1)
                scaled(e, i, 0)

            rows_T(0)
            over(act, EXPERTS, expert)
            scaled(EXPERTS - 1, 1, 1)

        @block.vector
        def _(dve):
            steps = 0

            def step(ins):
                nonlocal steps
                ins.then_inc(dve_step, 1)
                steps += 1
                dve.wait_ge(dve_step, steps)

            def norm_scale(dst, src, n, eps=LN_EPS):
                dve.tensor_scalar(dst, src, eps, None, ALU.add).then_inc(s["ln_var"], 1)
                dve.wait_ge(s["ln_rstd"], n)

            dve.wait_ge(const_done, CONSTS)
            step(dve.tensor_copy(pos_f[:], pos_i[:]))
            step(dve.tensor_copy(trash[:], trash_i[:]))
            step(dve.tensor_copy(io_f[:], io_i[:]))
            dve.wait_ge(net_in, 16 * REL_DMAS)

            def rel_norm(n, g):
                step(dve.bn_stats(stats[:, 0, :], rel_h[:]))
                step(dve.bn_aggr(mv[:, 0, :], stats[:, 0, :]))
                norm_scale(small[:, 2 * n:2 * n + 1], mv[:, 0, 1:2], n + 1)
                step(dve.tensor_scalar(rel_n[:], rel_h[:], mv[:, 0, 0:1], small[:, 2 * n + 1:2 * n + 2],
                                       ALU.subtract, ALU.mult))
                dve.tensor_tensor(rel_n[:], rel_n[:], g, ALU.mult).then_inc(s["rel_n_ready"], 1)

            step(dve.scalar_tensor_tensor(rel_h[:], rel_rows[:, 0, :], pos_f[:], rel_rows[:, 1, :],
                                          ALU.mult, ALU.add))
            rel_norm(0, rel_rows[:, 2, :])
            dve.wait_ge(s["rel_psum"], 1)
            dve.tensor_copy(rel_T[:], psQ[:, 0, 0:P]).then_inc(s["rel_T_ready"], 1)
            dve.wait_ge(s["rel_psum"], 2)
            step(dve.tensor_tensor(rel_h[:], psQ[:, 0, P:2 * P], rel_rows[:, 3, :], ALU.add))
            rel_norm(1, rel_rows[:, 4, :])
            dve.wait_ge(s["rel_psum"], 3)
            dve.tensor_copy(rel_T[:], psQ[:, 0, 2 * P:3 * P]).then_inc(s["rel_T_ready"], 1)
            dve.wait_ge(s["rel_psum"], 4)
            step(dve.tensor_scalar(rel_tab[:, 0:P], psQ[0:HEADS, 0, 3 * P:4 * P], rel_b2[:], None, ALU.add))
            dve.tensor_copy(half[:, 18:19], half[:, 19:20]).then_inc(rel_out, 1)
            dve.wait_ge(x_in, 16)
            for t in range(NB):
                ins = dve.bn_stats(stats[:, t, :], X[:, t, :])
            step(ins)
            for t in range(NB):
                ins = dve.bn_aggr(mv[:, t, :], stats[:, t, :])
            step(ins)
            dve.tensor_scalar(ve[:], mv[:, :, 1], LN_EPS, None, ALU.add).then_inc(s["ln_var"], 1)
            dve.wait_ge(bcast_in, 16 * BCAST_DMAS)
            dve.wait_ge(s["cols_psum"], 1)
            dve.tensor_copy(cols[:, 0:N_ROWS], psA[:, 0:N_ROWS]).then_inc(s["cols_ready"], 1)
            dve.wait_ge(s["cols_ready"], 1)
            step(dve.tensor_tensor(rel_h[:, 0:DH], nk_row[:], nk_row[:], ALU.mult))
            step(dve.tensor_reduce(small[:, 6:7], rel_h[:, 0:DH], X_AXIS, ALU.add))
            step(dve.tensor_scalar(small[:, 7:8], small[:, 6:7], 1e-24, None, ALU.max))
            norm_scale(small[:, 4:5], small[:, 7:8], 4, 0.0)
            step(dve.tensor_tensor(nk0[:], cols[:, C_NK:C_NK + 1], small[:, 5:6], ALU.mult))
            step(dve.tensor_tensor(nk0[:], nk0[:], cols[:, C_QS:C_QS + 1], ALU.mult))
            step(dve.scalar_tensor_tensor(nk0[:], nk0[:], 8.0, cols[:, C_KS:C_KS + 1], ALU.mult, ALU.mult))

            def null_keys(column):
                for i in range(2):
                    for e in range(2):
                        half_of = slice(DH * e, DH * (e + 1))
                        dve.tensor_copy(kk[i][half_of, e, 0:1], column[half_of]).then_inc(s["kk_null"], 1)

            null_keys(nk0[:])
            step(dve.tensor_tensor(kqs[:], kqs[:], qs_row[:], ALU.mult))
            step(dve.tensor_scalar(kqs[:], kqs[:], 8.0, None, ALU.mult))
            for layer in range(2):
                step(dve.tensor_scalar(mask[layer][:, :, 1:P + 1],
                                       mask_u8[layer][:].rearrange("p (b k) -> p b k", k=P), -MASKED, MASKED,
                                       ALU.mult, ALU.add))
            for layer in range(2):
                for u in range(UNITS):
                    ins = dve.tensor_copy(unit_bias(layer, u)[:, :, :, 0],
                                          nullb[layer][:].rearrange("p (h e) -> p h e", e=2))
            ins.then_inc(s["masks_ready"], 1)
            def normed(t):
                return mv[:, t, 0:1], rstd[:, bass.ds(t, 1)]

            def ternary():
                dve.wait_ge(s["cols_psum"], 2)
                step(dve.tensor_scalar(wmean[:], psO[:, 0:2], 1.0 / (HIDDEN * P), 1e-5, ALU.mult, ALU.max))
                step(dve.reciprocal(wscale[:], wmean[:]))
                for i, w in enumerate((w1_raw, w2_raw)):
                    flat_w = w[:].rearrange("p j d -> p (j d)")
                    step(dve.tensor_scalar(tern[:, i, :], flat_w, wscale[:, i:i + 1], 0.5, ALU.mult, ALU.is_gt))
                    step(dve.tensor_scalar(z[:, i, :], flat_w, wscale[:, i:i + 1], -0.5, ALU.mult, ALU.is_lt))
                    dve.tensor_tensor(tern[:, i, :], tern[:, i, :], z[:, i, :], ALU.subtract).then_inc(
                        s["tern_ready"], 1)

            def input_norm(layer, b, i):
                B = b + NB * layer
                held(dve, s["xnT_psum"], B - 1)
                mean, r = normed(b)
                dve.tensor_scalar(xn[:, i, :], X[:, b, :], mean, r, ALU.subtract, ALU.mult).then_inc(
                    s["xn_ready"], 1)

            def values_in(layer, b, i):
                B = b + NB * layer
                dve.wait_ge(s["kv_psum"], B + 1)
                if layer == 0:
                    dve.wait_ge(s["sq_ready"], 2 * b + 1)
                held(dve, s["v_ready"], B)
                dve.tensor_copy(vs[:], psA[:, P + DH:2 * P]).then_inc(s["v_read"], 1)

            def keys_in(layer, b, i):
                B = b + NB * layer
                dve.wait_ge(s["kv_psum"], B + 1)
                if layer == 0:
                    dve.wait_ge(s["rn_ready"], 2 * b + 1)
                held(dve, s["kT_psum"], B - 1)
                k_raw = psA[:, P:P + DH].unsqueeze(1).broadcast_to([P, 2, DH])
                if layer == 0:
                    ins = dve.scalar_tensor_tensor(kd[i][:], k_raw, qrn[:, 0:1],
                                                   kqs[:].unsqueeze(1).broadcast_to([P, 2, DH]),
                                                   ALU.mult, ALU.mult)
                else:
                    ins = dve.tensor_copy(kd[i][:], k_raw)
                ins.then_inc(s["k_ready"], 1)

            def sum_squares(b, h):
                lo, hi = (0, 9) if h == 0 else (9, HEADS + 1)
                dve.wait_ge(s["sq_ready"], 2 * b + h + 1)
                dve.tensor_reduce(qss[:, lo:hi], qsq[:, lo:hi, :], X_AXIS, ALU.add).then_inc(s["ss_step"], 1)
                dve.wait_ge(s["ss_step"], 4 * b + 2 * h + 1)
                dve.tensor_scalar(qssc[:, lo:hi], qss[:, lo:hi], 1e-24, None, ALU.max).then_inc(s["ss_step"], 1)

            def queries_norm(b, h):
                dve.wait_ge(s["rn_ready"], 2 * b + h + 1)
                held(dve, s["qT_psum"], 2 * b + h - 1)
                dve.tensor_tensor(qn[:, 512 * h:512 * (h + 1)].rearrange("p (h d) -> p h d", d=DH),
                                  psQ[:, h, :].rearrange("p (h d) -> p h d", d=DH),
                                  qrn[:, 1 + 8 * h:9 + 8 * h].unsqueeze(2).broadcast_to([P, 8, DH]),
                                  ALU.mult).then_inc(s["qn_ready"], 1)

            def biased(n, u, i):
                held(dve, s["probs_ready"], n - 3)
                dve.wait_ge(s["bias_ready"], n + 1)
                dve.wait_ge(s["scores_psum"], n + 1)
                dve.tensor_tensor(sc[u][:], unit_psum(u), unit_masked(i, u), ALU.add).then_inc(s["scores_ready"], 1)
                dve.wait_ge(s["scores_ready"], n + 1)
                dve.tensor_reduce(negmax[:, u, :], sc[u][:].rearrange("p h e k -> p (h e) k"), X_AXIS,
                                  ALU.max, negate=True).then_inc(s["negmax_ready"], 1)

            def divide(n, u):
                dve.wait_ge(s["exp_done"], n + 1)
                dve.reciprocal(rsum[:, u, :], psum_row[:, u, :]).then_inc(s["rsum_ready"], 1)
                dve.wait_ge(s["rsum_ready"], n + 1)
                held(dve, s["probsT_psum"], n - 1)
                k = WIDTH[u] - 1
                dve.tensor_tensor(pn[u % 2][:, :, 0:k],
                                  sc[u][:].rearrange("p h e k -> p (h e) k")[:, :, 1:k + 1],
                                  rsum[:, u, :].unsqueeze(2).broadcast_to([P, 4, k]),
                                  ALU.mult).then_inc(s["probs_ready"], 1)

            def outputs(layer, n, b, u, i):
                B = b + NB * layer
                dve.wait_ge(s["out_psum"], n + 1)
                if u == 0:
                    held(dve, s["y_psum"], B - 1)
                dve.tensor_scalar(OT[i][:, :, u, :], psO[:, 0:256].rearrange("p (j q) -> p j q", q=QB),
                                  cols[:, C_VN:C_VN + 1], None, ALU.add).then_inc(s["out_ready"], 1)

            def project_out(layer, b, i):
                B = b + NB * layer
                dve.wait_ge(s["y_psum"], B + 1)
                dve.bn_stats(run["o"][0][:, i, :], psA[:, 3 * P:4 * P]).then_inc(s["o_stat"], 1)
                dve.tensor_copy(Y[:, b, :], psA[:, 3 * P:4 * P]).then_inc(s["y_done"], 1)

            def moments(w, n, i):
                apart(dve, (s[f"{w}_stat"], 2 * n + 1))
                dve.bn_aggr(run[w][1][:, i, :], run[w][0][:, i, :]).then_inc(s[f"{w}_stat"], 1)

            def variance(w, n, i):
                if isinstance(n, int):
                    held(dve, s[f"{w}_rstd"], n - 1)
                dve.wait_ge(s[f"{w}_stat"], 2 * n + 2)
                dve.tensor_scalar(run[w][2][:, i:i + 1], run[w][1][:, i, 1:2], LN_EPS, None, ALU.add).then_inc(
                    s[f"{w}_var"], 1)

            def input_stats(w, src, t, i, written):
                apart(dve, written)
                dve.bn_stats(run[w][0][:, i, :], src[:, t, :]).then_inc(s[f"{w}_stat"], 1)

            def input_variance(w, t, i):
                variance(w, t, i)
                dve.tensor_copy(mv[:, t, :], run[w][1][:, i, :])

            def centre(layer, b, i):
                if no(b, 0):
                    dve.wait_ge(late_in, 16 * LATE_DMAS)
                dve.wait_ge(s["o_rstd"], b + NB * layer + 1)
                dve.scalar_tensor_tensor(centred[:], Y[:, b, :], run["o"][1][:, i, 0:1], g_out[layer][:],
                                         ALU.subtract, ALU.mult).then_inc(s["n_step"], 1)

            def rescale(layer, b, i):
                B = b + NB * layer
                dve.wait_ge(s["n_step"], 2 * B + 1)
                dve.tensor_scalar(Y[:, b, :], centred[:], run["o"][3][:, i:i + 1], None, ALU.mult).then_inc(
                    s["n_step"], 1)

            def output_norm(layer, b, i):
                centre(layer, b, i)
                rescale(layer, b, i)
                if layer == 0:
                    input_stats("h", Y, b, i, (s["n_step"], 2 * b + 2))
                    moments("h", b, i)
                    input_variance("h", b, i)

            def attention(layer):
                def batch(b, i):
                    B = b + NB * layer
                    n = 4 * B
                    first, last = no(b, 0), no(b, NB - 1)
                    normed_now = not (first or no(b, 1) or no(b, 2))
                    for u in range(UNITS):
                        if layer == 1 and u == 3 and not first and not no(b, 1):
                            project_out(layer, b - 2, i)
                        if layer == 0 and u == 1 and not last:
                            sum_squares(b + 1, 0)
                        if layer == 0 and u == 1 and not last:
                            values_in(layer, b + 1, 1 - i)
                        if layer == 0 and u == 2 and not first and not no(b, 1):
                            project_out(layer, b - 2, i)
                        if layer == 0 and u == 2 and not last:
                            keys_in(layer, b + 1, 1 - i)
                            queries_norm(b + 1, 0)
                            queries_norm(b + 1, 1)
                        biased(n + u, u, i)
                        if layer == 0 and u == 1 and not last:
                            sum_squares(b + 1, 1)
                        if layer == 1 and u == 1 and not last:
                            values_in(layer, b + 1, 1 - i)
                        if layer == 1 and u == 1 and not last:
                            keys_in(layer, b + 1, 1 - i)
                        if not (first and u < 1):
                            divide(n + u - 1, (u - 1) % UNITS)
                        if u == 2 + layer and not first and not no(b, 1):
                            moments("o", B - 2, i)
                        if layer == 0 and u == 3 and normed_now:
                            moments("h", b - 3, 1 - i)
                        if not (first and u < 3):
                            outputs(layer, n + u - 3, b if u == 3 else b - 1, (u - 3) % UNITS, i if u == 3 else 1 - i)
                        if u == 3 and not first and not no(b, 1):
                            variance("o", B - 2, i)
                        if u == 0 and normed_now:
                            centre(layer, b - 3, 1 - i)
                        if u == 1 and normed_now:
                            rescale(layer, b - 3, 1 - i)
                        if layer == 0 and u == 2 and normed_now:
                            input_stats("h", Y, b - 3, 1 - i, (s["n_step"], 2 * b - 4))
                        if layer == 0 and u == 3 and normed_now:
                            input_variance("h", b - 3, 1 - i)
                        if u == 0 and not last and not no(b, NB - 2):
                            input_norm(layer, b + 2, i)

                input_norm(layer, 0, 0)
                input_norm(layer, 1, 1)
                if layer == 0:
                    ternary()
                values_in(layer, 0, 0)
                if layer == 0:
                    sum_squares(0, 0)
                    sum_squares(0, 1)
                    keys_in(layer, 0, 0)
                    queries_norm(0, 0)
                    queries_norm(0, 1)
                else:
                    keys_in(layer, 0, 0)
                over(dve, NB, batch, 4)
                n = 4 * (NB + NB * layer)
                output_norm(layer, NB - 3, 1)
                project_out(layer, NB - 2, 0)
                moments("o", NB - 2 + NB * layer, 0)
                divide(n - 1, 3)
                variance("o", NB - 2 + NB * layer, 0)
                outputs(layer, n - 3, NB - 1, 1, 1)
                outputs(layer, n - 2, NB - 1, 2, 1)
                outputs(layer, n - 1, NB - 1, 3, 1)
                output_norm(layer, NB - 2, 0)
                project_out(layer, NB - 1, 1)
                moments("o", NB - 1 + NB * layer, 1)
                variance("o", NB - 1 + NB * layer, 1)
                output_norm(layer, NB - 1, 1)
                dve.wait_ge(s["n_step"], 2 * NB * (layer + 1))

            attention(0)

            dve.wait_ge(s["h_rstd"], NB)

            def f_norm_in(t, i):
                held(dve, s["f_h_psum"], t - 1)
                mean, r = normed(t)
                dve.tensor_scalar(xn[:, i, :], Y[:, t, :], mean, r, ALU.subtract, ALU.mult).then_inc(s["f_h"], 1)

            def f_hidden(t, i):
                dve.wait_ge(s["f_z_psum"], t + 1)
                dve.scalar_tensor_tensor(z[:, i, :], psQ[:, i, :], wmean[:, 0:1], fb1[:], ALU.mult,
                                         ALU.add).then_inc(s["f_z_ready"], 1)

            def f_stats(t, i):
                dve.wait_ge(s["f_gelu"], t + 1)
                dve.bn_stats(zst[:, i, :], z[:, i, :]).then_inc(s["f_stat"], 1)

            def f_norm_mid(t, i):
                dve.wait_ge(s["f_rstd"], t + 1)
                held(dve, s["f_gnT_psum"], t - 1)
                dve.tensor_scalar(gn[:, i, :], z[:, i, :], zmv[:, i, 0:1], zrstd[:, i:i + 1], ALU.subtract,
                                  ALU.mult).then_inc(s["f_gn"], 1)

            def f_out(t, i):
                dve.wait_ge(s["f_o_psum"], t + 1)
                dve.scalar_tensor_tensor(ffo[:], psO[:, 0:P], wmean[:, 1:2], fb2[:], ALU.mult,
                                         ALU.add).then_inc(s["f_o_step"], 1)
                dve.wait_ge(s["f_o_step"], 2 * t + 1)
                dve.tensor_tensor(X[:, t, :], X[:, t, :], ffo[:], ALU.add).then_inc(s["f_o_step"], 1)

            def f_aggr(t, i):
                apart(dve, (s["f_stat"], 2 * t + 1))
                dve.bn_aggr(zmv[:, i, :], zst[:, i, :]).then_inc(s["f_stat"], 1)

            def f_variance(t, i):
                dve.wait_ge(s["f_stat"], 2 * t + 2)
                dve.tensor_scalar(zve[:, i:i + 1], zmv[:, i, 1:2], LN_EPS, None, ALU.add).then_inc(s["f_var"], 1)

            def ffn(t, i):
                out_now = not (no(t, 0) or no(t, 1) or no(t, 2))
                if not no(t, 0):
                    f_norm_mid(t - 1, 1 - i)
                f_hidden(t, i)
                if out_now:
                    f_out(t - 3, 1 - i)
                if not no(t, NB - 1):
                    f_norm_in(t + 1, 1 - i)
                f_stats(t, i)
                if out_now:
                    input_stats("x", X, t - 3, 1 - i, (s["f_o_step"], 2 * t - 4))
                f_aggr(t, i)
                if out_now:
                    moments("x", t - 3, 1 - i)
                f_variance(t, i)
                if out_now:
                    input_variance("x", t - 3, 1 - i)

            f_norm_in(0, 0)
            over(dve, NB, ffn, 4)
            f_norm_mid(NB - 1, 1)
            for t in range(NB - 3, NB):
                f_out(t, t % 2)
                input_stats("x", X, t, t % 2, (s["f_o_step"], 2 * t + 2))
                moments("x", t, t % 2)
                input_variance("x", t, t % 2)
            dve.wait_ge(s["x_rstd"], NB)

            null_keys(cols[:, C_NK:C_NK + 1])
            attention(1)

            dve.wait_ge(late_in, 16 * LATE_DMAS)
            dve.wait_ge(s["cols_psum"], 3)
            dve.tensor_copy(gateT[:], psA[:, 2 * P:2 * P + EXPERTS]).then_inc(s["setup_read"], 1)

            for g in (1, 3):
                dve.wait_ge(s["r_T_psum"], g + 1)
                dve.tensor_copy(yT[:, g, :], psG[g]).then_inc(s["r_T_dve"], 1)

            def wide(v, shape, axis):
                return v.unsqueeze(axis).broadcast_to(shape)

            TE = [P, NB, EXPERTS]
            TCE = [P, NB, TOPK, EXPERTS]
            dve.wait_ge(s["r_lg_psum"], 1)
            dve.tensor_tensor(lg[:], psQ[:, 0, 0:P].rearrange("p (t e) -> p t e", e=EXPERTS),
                              wide(gate_b[:], TE, 1), ALU.add).then_inc(s["r_step"], 1)
            dve.wait_ge(s["r_step"], 1)
            dve.tensor_reduce(lgm[:], lg[:], X_AXIS, ALU.max, negate=True).then_inc(s["r_step"], 1)
            dve.wait_ge(s["r_step"], 2)
            dve.tensor_tensor(le[:], lg[:], wide(lgm[:], TE, 2), ALU.add).then_inc(s["r_step"], 1)
            dve.wait_ge(s["r_exp"], 1)
            step(dve.tensor_reduce(lsum[:], le[:], X_AXIS, ALU.add))
            step(dve.reciprocal(lsum[:], lsum[:]))
            step(dve.tensor_tensor(prob[:], le[:], wide(lsum[:], TE, 2), ALU.mult))
            for t in range(NB):
                ins = dve.max(top[:, t, :], prob[:, t, :])
            step(ins)
            for t in range(NB):
                ins = dve.max_index(topi[:, t, :], top[:, t, :], prob[:, t, :])
            step(ins)
            step(dve.tensor_copy(topf[:], topi[:, :, 0:TOPK]))
            step(dve.tensor_tensor(oh[:].rearrange("p t c e -> p (t c) e"),
                                   wide(io_f[:], [P, NB * TOPK, EXPERTS], 1),
                                   wide(topf[:].rearrange("p t c -> p (t c)"), [P, NB * TOPK, EXPERTS], 2),
                                   ALU.is_equal))
            dve.tensor_copy(oh_bf[:], oh[:]).then_inc(s["r_oh"], 1)
            dve.wait_ge(s["r_pos_psum"], 1)
            step(dve.tensor_tensor(posn[:].rearrange("p t c e -> p (t c e)"), psQ[:, 1, 0:NB * TOPK * EXPERTS],
                                   oh[:].rearrange("p t c e -> p (t c e)"), ALU.mult))
            dve.tensor_reduce(own[:], posn[:], X_AXIS, ALU.add).then_inc(s["r_pos_read"], 1)
            dve.wait_ge(s["r_pos_read"], 1)
            step(dve.tensor_scalar(keep[:], own[:], float(CAP), None, ALU.is_lt))
            step(dve.scalar_tensor_tensor(dest[:], topf[:], float(CAP), own[:], ALU.mult, ALU.add))
            step(dve.scalar_tensor_tensor(dest[:], dest[:], trash[:], keep[:], ALU.subtract, ALU.mult))
            step(dve.tensor_scalar(dest[:], dest[:], trash[:], None, ALU.add))
            dve.tensor_copy(dest_u[:], dest[:]).then_inc(s["r_pay"], 1)
            dve.tensor_tensor(pay[:, :, P + 1:P + 1 + TOPK], top[:, :, 0:TOPK], keep[:], ALU.mult).then_inc(s["r_pay"], 1)

            def hidden(e, blocks):
                for j in blocks:
                    dve.wait_ge(s["e_h_psum"], 8 * e + 2 * j + 2)
                    dve.tensor_scalar(hm[:, j, CAP:2 * CAP], psH[j % 2][1][:, 0:CAP],
                                      cols[:, bass.ds(4 * e + (C_MB1 + j), 1)], 0.0, ALU.add,
                                      ALU.max).then_inc(s["e_h_dve"], 1)

            def result(e, i, c):
                dve.wait_ge(s["e_y_psum"], TOPK * e + c + 1)
                dve.tensor_tensor(yb[i][:, c, 0:2, :], psS[:, c, 0:2 * P].rearrange("p (t d) -> p t d", d=P),
                                  mb2[:, bass.ds(e, 1), :].broadcast_to([P, 2, P]), ALU.add).then_inc(
                                      s["e_y_add"], 1)
                k = TILE_ROWS[2]
                dve.tensor_tensor(yb[i][0:k, c, 2:3, :], psS[0:k, c:c + 1, 2 * P:3 * P],
                                  mb2[0:k, bass.ds(e, 1), :], ALU.add).then_inc(s["e_y_add"], 1)

            def expert(e, i):
                held(dve, s["e_y_psum"], TOPK * e)
                hidden(e, (0, 1))
                if not no(e, 0):
                    result(e - 1, 1 - i, 1)
                hidden(e, (2, 3))
                for c in range(TOPK):
                    held(dve, s[f"e_sent{c}"], 16 * TILES * (e - 1))
                dve.wait_ge(s[f"e_x{i}"], arrived(e, i, 64))
                dve.tensor_copy(tags[i][:, :, 0:2, :], xb[i][:, :, 0:2, P:ROW]).then_inc(s["e_tags"], 1)
                k = TILE_ROWS[2]
                dve.tensor_copy(tags[i][0:k, :, 2, :], xb[i][0:k, :, 2, P:ROW]).then_inc(s["e_tags"], 1)
                result(e, i, 0)

            over(dve, EXPERTS, expert)
            result(EXPERTS - 1, 1, 1)
            for q in range(4):
                dve.wait_ge(s[f"back_in{q}"], 16 * TOPK)
                for c in range(TOPK):
                    v = X[:, 4 * q:4 * q + 4, :]
                    dve.tensor_tensor(v, v, back[:, c, 4 * q:4 * q + 4, :], ALU.add).then_inc(s["z_step"], 1)
                    dve.wait_ge(s["z_step"], 2 * q + c + 1)


INPUTS = ["x", "cond_64", "fside_16xSxS_0", "mask_BxS_bf1", "mask_BxS_bk0", "L0_cond_g_norm", "L0_cond_Wq",
          "L0_cond_Wkv", "L0_cond_q_scale", "L0_cond_k_scale", "L0_cond_null_attn_bias", "L0_cond_w0",
          "L0_cond_b0", "L0_cond_g0", "L0_cond_w1", "L0_cond_b1", "L0_cond_g1", "L0_cond_w2", "L0_cond_b2",
          "L0_cond_Wout", "L0_cond_g_out", "L0_ffn_ln1_g", "L0_ffn_ln1_b", "L0_ffn_w1", "L0_ffn_b1",
          "L0_ffn_ln2_g", "L0_ffn_ln2_b", "L0_ffn_w2", "L0_ffn_b2", "L1_cond_g_in", "L1_cond_null_attn_bias",
          "L1_cond_Wq", "L1_cond_Wkv", "L1_cond_Wo", "L1_cond_g_out", "L1_ffn_gate_w", "L1_ffn_gate_b",
          "L1_ffn_W1", "L1_ffn_b1", "L1_ffn_W2", "L1_ffn_b2"]


def kernel(**inputs):
    import numpy as np
    import concourse.bacc as bacc
    from concourse.bass_utils import run_bass_kernel_spmd

    nc = bacc.Bacc("TRN2", target_bir_lowering=False, num_devices=1)
    arrays, aps = {}, {}
    for name in INPUTS:
        v = np.ascontiguousarray(inputs[name])
        if v.dtype == np.bool_:
            v = v.view(np.uint32)
        arrays["in_" + name] = v
        aps[name] = nc.dram_tensor("in_" + name, v.shape, mybir.dt.from_np(v.dtype), kind="ExternalInput").ap()
    out = nc.dram_tensor("out_x", (NB, P, P), F32, kind="ExternalOutput").ap()
    build(nc, aps, out)
    return run_bass_kernel_spmd(nc, [arrays], core_ids=[0]).results[0]["out_x"]
```
